# Optimizing a Trainium2 kernel written in Bass

```python
import numpy as np
import jax
import jax.numpy as jnp

def _softmax(x, axis=-1):
    return jax.nn.softmax(x, axis=axis)

def _gelu(x):
    return jax.nn.gelu(x, approximate=True)

def _silu(x):
    return jax.nn.silu(x)

def _sigmoid(x):
    return jax.nn.sigmoid(x)

def _layernorm(x, axis=-1, eps=1e-05):
    m = jnp.mean(x, axis=axis, keepdims=True)
    v = jnp.var(x, axis=axis, keepdims=True)
    return (x - m) / jnp.sqrt(v + eps)

def _scatter_add(tgt, idx, src, axis=0):
    return tgt.at[idx].add(src)

def _segment_sum(src, seg, n):
    return jax.ops.segment_sum(src, seg, n)
kernel_name = 'mk_decoder_preln_d2_seqx_r4_7b8302'

def setup_inputs(seed: int=0):
    np.random.seed(seed)
    _w = jnp.asarray

    def _rec_inputs():
        import jax
        import jax.numpy as jnp
        _rk = jax.random.key(seed)
        x = -0.0005207 + 1.001 * jax.random.normal(jax.random.fold_in(_rk, 1), (4, 1024, 256), jnp.float32)
        _lenS = 1024 - jax.random.randint(jax.random.fold_in(_rk, 7), (4,), 0, max(1, 1024 // 4) + 1, jnp.int32)
        _lenS2 = 77 - jax.random.randint(jax.random.fold_in(_rk, 8), (4,), 0, max(1, 77 // 4) + 1, jnp.int32)
        _ctx_1024P = jax.random.normal(jax.random.fold_in(_rk, 11), (4, 16, 256), jnp.float32)
        _ctx_1024c = jax.random.dirichlet(jax.random.fold_in(_rk, 511), 0.3 * jnp.ones((16,), jnp.float32), (4, 77))
        _ctx_1024t = jnp.einsum('bsk,bkd->bsd', _ctx_1024c, _ctx_1024P)
        _ctx_1024t = _ctx_1024t * jax.lax.rsqrt(jnp.mean(jnp.square(_ctx_1024t)) + 1e-12) * 0.953939
        ctx_1024 = 2.81802e-05 + 1.00001 * (_ctx_1024t + 0.3 * jax.random.normal(jax.random.fold_in(_rk, 611), (4, 77, 256), jnp.float32))
        return (x, ctx_1024)
    x, ctx_1024 = _rec_inputs()

    def _L0_attn_setup():
        import jax, jax.numpy as jnp
        import numpy as np
        D_MODEL = 256
        NUM_HEAD = 16
        CHUNK = 64
        NGROUPS = 2
        D_HEAD = D_MODEL // NUM_HEAD
        NEG = -1e+30

        def _scan_op(a, b):
            ga, xa = a
            gb, xb = b
            return (gb * ga, gb * xa + xb)
        key = jax.random.key(seed)
        ks = jax.random.split(key, 4)
        bs, seq = (2, 1024)
        proj_dim = 3 * D_MODEL + 2 * NGROUPS * D_HEAD
        hidden = jax.random.normal(ks[0], (bs, seq, D_MODEL), jnp.float32)
        W_in = jax.random.normal(ks[1], (D_MODEL, proj_dim), jnp.float32) * D_MODEL ** (-0.5)
        gate_bias = jnp.log(jax.random.uniform(ks[2], (D_MODEL,), jnp.float32, 1.0, CHUNK - 1.0))
        rms_weight = jnp.ones((D_MODEL,), jnp.float32)
        W_out = jax.random.normal(ks[3], (D_MODEL, D_MODEL), jnp.float32) * D_MODEL ** (-0.5)
        return {'hidden_states': hidden, 'rms_weight': rms_weight, 'W_in': W_in, 'gate_bias': gate_bias, 'W_out': W_out}
    _L0_attn_all = _L0_attn_setup()
    _L0_attn_in = {k: v for k, v in _L0_attn_all.items() if k in ('rms_weight', 'W_in', 'gate_bias', 'W_out')}
    del _L0_attn_all

    def _L0_xattn_setup():
        import jax, jax.numpy as jnp
        import numpy as np
        B, Q, K, D, H, DH = (4, 128, 1024, 256, 8, 128)
        key = jax.random.key(seed)
        ks = jax.random.split(key, 5)
        s = 1.0 / np.sqrt(D)
        return {'inputs_q': jax.random.normal(ks[0], (B, Q, D), jnp.float32), 'inputs_kv': jax.random.normal(ks[1], (B, K, D), jnp.float32), 'Wq': jax.random.normal(ks[2], (D, H, DH), jnp.float32) * s, 'Wkv': jax.random.normal(ks[3], (D, H, 2 * DH), jnp.float32) * s, 'Wproj': jax.random.normal(ks[4], (H, DH, D), jnp.float32) * (1.0 / np.sqrt(H * DH)), 'b_proj': jnp.zeros((D,), jnp.float32)}
    _L0_xattn_all = _L0_xattn_setup()
    _L0_xattn_in = {k: v for k, v in _L0_xattn_all.items() if k in ('Wq', 'Wkv', 'Wproj', 'b_proj')}
    del _L0_xattn_all

    def _L0_ffn_setup():
        import jax, jax.numpy as jnp
        import numpy as np
        B, S, D = (2, 128, 256)
        E, K, I = (16, 8, 256)
        I_SH = 256
        ROUTE_SCALE = 2.826
        key = jax.random.key(seed)
        ks = jax.random.split(key, 8)
        s = 0.02
        return {'x': jax.random.normal(ks[0], (B, S, D), dtype=jnp.float32), 'gate_w': jax.random.normal(ks[1], (E, D), dtype=jnp.float32) * s, 'expert_bias': jnp.zeros((E,), dtype=jnp.float32), 'w_gate': jax.random.normal(ks[2], (E, I, D), dtype=jnp.float32) * s, 'w_up': jax.random.normal(ks[3], (E, I, D), dtype=jnp.float32) * s, 'w_down': jax.random.normal(ks[4], (E, D, I), dtype=jnp.float32) * s, 'shared_gate_w': jax.random.normal(ks[5], (I_SH, D), dtype=jnp.float32) * s, 'shared_up_w': jax.random.normal(ks[6], (I_SH, D), dtype=jnp.float32) * s, 'shared_down_w': jax.random.normal(ks[7], (D, I_SH), dtype=jnp.float32) * s}
    _L0_ffn_all = _L0_ffn_setup()
    _L0_ffn_in = {k: v for k, v in _L0_ffn_all.items() if k in ('gate_w', 'expert_bias', 'w_gate', 'w_up', 'w_down', 'shared_gate_w', 'shared_up_w', 'shared_down_w')}
    del _L0_ffn_all

    def _L1_attn_setup():
        import jax, jax.numpy as jnp
        import numpy as np
        D_MODEL = 256
        D_QK = 256
        NUM_HEADS = 16
        HEAD_DIM = D_QK // NUM_HEADS
        V_DIM = D_MODEL // NUM_HEADS
        B, S = (2, 512)
        key = jax.random.key(seed)
        ks = jax.random.split(key, 9)
        sc = 0.02
        return {'x': jax.random.normal(ks[0], (B, S, D_MODEL), dtype=jnp.float32), 'Wqk': jax.random.normal(ks[1], (D_MODEL, 2 * D_QK), dtype=jnp.float32) * sc, 'bqk': jax.random.normal(ks[2], (2 * D_QK,), dtype=jnp.float32) * sc, 'Wv': jax.random.normal(ks[3], (D_MODEL, D_MODEL), dtype=jnp.float32) * sc, 'bv': jax.random.normal(ks[4], (D_MODEL,), dtype=jnp.float32) * sc, 'Wn': jax.random.normal(ks[5], (D_MODEL, NUM_HEADS), dtype=jnp.float32) * sc, 'bn': jax.random.normal(ks[6], (NUM_HEADS,), dtype=jnp.float32) * sc, 'Wo': jax.random.normal(ks[7], (D_MODEL, D_MODEL), dtype=jnp.float32) * sc, 'bo': jax.random.normal(ks[8], (D_MODEL,), dtype=jnp.float32) * sc}
    _L1_attn_all = _L1_attn_setup()
    _L1_attn_in = {k: v for k, v in _L1_attn_all.items() if k in ('Wqk', 'bqk', 'Wv', 'bv', 'Wn', 'bn', 'Wo', 'bo')}
    del _L1_attn_all

    def _L1_xattn_setup():
        import jax, jax.numpy as jnp
        import numpy as np
        N_EMBD = 256
        N_HEAD = 16
        R = 16
        SCALING = 1.0 / 16.0

        def lora_linear(x, W, b, A, B):
            return x @ W.T + b + x @ A.T @ B.T * SCALING
        key = jax.random.key(seed)
        ks = jax.random.split(key, 16)
        B, T, S, C = (8, 256, 64, N_EMBD)
        std = 0.02
        return {'x': jax.random.normal(ks[0], (B, T, C), jnp.float32), 'feature': jax.random.normal(ks[1], (B, S, C), jnp.float32), 'Wq': jax.random.normal(ks[2], (C, C), jnp.float32) * std, 'bq': jnp.zeros((C,), jnp.float32), 'Aq': jax.random.normal(ks[3], (R, C), jnp.float32) * std, 'Bq': jnp.zeros((C, R), jnp.float32), 'Wf': jax.random.normal(ks[4], (2 * C, C), jnp.float32) * std, 'bf': jnp.zeros((2 * C,), jnp.float32), 'Af': jax.random.normal(ks[5], (R, C), jnp.float32) * std, 'Bf': jnp.zeros((2 * C, R), jnp.float32), 'Wp': jax.random.normal(ks[6], (C, C), jnp.float32) * std, 'bp': jnp.zeros((C,), jnp.float32), 'Ap': jax.random.normal(ks[7], (R, C), jnp.float32) * std, 'Bp': jnp.zeros((C, R), jnp.float32)}
    _L1_xattn_all = _L1_xattn_setup()
    _L1_xattn_in = {k: v for k, v in _L1_xattn_all.items() if k in ('Wq', 'bq', 'Aq', 'Bq', 'Wf', 'bf', 'Af', 'Bf', 'Wp', 'bp', 'Ap', 'Bp')}
    del _L1_xattn_all

    def _L1_ffn_setup():
        import jax, jax.numpy as jnp
        import numpy as np
        E = 8
        D = 256
        DO = 256
        R = 64
        H = 64
        B, T = (8, 512)
        key = jax.random.key(seed)
        ks = jax.random.split(key, 12)
        s = lambda k, shape, fan: jax.random.normal(k, shape, jnp.float32) / np.sqrt(fan)
        return {'x': jax.random.normal(ks[0], (B, T, D), jnp.float32), 'W_base': s(ks[1], (D, DO), D), 'b_base': jnp.zeros((DO,), jnp.float32), 'Wd1': s(ks[2], (E, D, H), D), 'bd1': jnp.zeros((E, H), jnp.float32), 'Wd2': s(ks[3], (E, H, D), H), 'bd2': jnp.zeros((E, D), jnp.float32), 'Wa_down': s(ks[4], (E, D, R), D), 'ba_down': jnp.zeros((E, R), jnp.float32), 'Wa_up': s(ks[5], (E, R, DO), R), 'ba_up': jnp.zeros((E, DO), jnp.float32)}
    _L1_ffn_all = _L1_ffn_setup()
    _L1_ffn_in = {k: v for k, v in _L1_ffn_all.items() if k in ('W_base', 'b_base', 'Wd1', 'bd1', 'Wd2', 'bd2', 'Wa_down', 'ba_down', 'Wa_up', 'ba_up')}
    del _L1_ffn_all
    return {'x': x, 'ctx_1024': ctx_1024, 'L0_attn_rms_weight': _L0_attn_in['rms_weight'], 'L0_attn_W_in': _L0_attn_in['W_in'], 'L0_attn_gate_bias': _L0_attn_in['gate_bias'], 'L0_attn_W_out': _L0_attn_in['W_out'], 'L0_xattn_Wq': _L0_xattn_in['Wq'], 'L0_xattn_Wkv': _L0_xattn_in['Wkv'], 'L0_xattn_Wproj': _L0_xattn_in['Wproj'], 'L0_xattn_b_proj': _L0_xattn_in['b_proj'], 'L0_ffn_gate_w': _L0_ffn_in['gate_w'], 'L0_ffn_expert_bias': _L0_ffn_in['expert_bias'], 'L0_ffn_w_gate': _L0_ffn_in['w_gate'], 'L0_ffn_w_up': _L0_ffn_in['w_up'], 'L0_ffn_w_down': _L0_ffn_in['w_down'], 'L0_ffn_shared_gate_w': _L0_ffn_in['shared_gate_w'], 'L0_ffn_shared_up_w': _L0_ffn_in['shared_up_w'], 'L0_ffn_shared_down_w': _L0_ffn_in['shared_down_w'], 'L1_attn_Wqk': _L1_attn_in['Wqk'], 'L1_attn_bqk': _L1_attn_in['bqk'], 'L1_attn_Wv': _L1_attn_in['Wv'], 'L1_attn_bv': _L1_attn_in['bv'], 'L1_attn_Wn': _L1_attn_in['Wn'], 'L1_attn_bn': _L1_attn_in['bn'], 'L1_attn_Wo': _L1_attn_in['Wo'], 'L1_attn_bo': _L1_attn_in['bo'], 'L1_xattn_Wq': _L1_xattn_in['Wq'], 'L1_xattn_bq': _L1_xattn_in['bq'], 'L1_xattn_Aq': _L1_xattn_in['Aq'], 'L1_xattn_Bq': _L1_xattn_in['Bq'], 'L1_xattn_Wf': _L1_xattn_in['Wf'], 'L1_xattn_bf': _L1_xattn_in['bf'], 'L1_xattn_Af': _L1_xattn_in['Af'], 'L1_xattn_Bf': _L1_xattn_in['Bf'], 'L1_xattn_Wp': _L1_xattn_in['Wp'], 'L1_xattn_bp': _L1_xattn_in['bp'], 'L1_xattn_Ap': _L1_xattn_in['Ap'], 'L1_xattn_Bp': _L1_xattn_in['Bp'], 'L1_ffn_W_base': _L1_ffn_in['W_base'], 'L1_ffn_b_base': _L1_ffn_in['b_base'], 'L1_ffn_Wd1': _L1_ffn_in['Wd1'], 'L1_ffn_bd1': _L1_ffn_in['bd1'], 'L1_ffn_Wd2': _L1_ffn_in['Wd2'], 'L1_ffn_bd2': _L1_ffn_in['bd2'], 'L1_ffn_Wa_down': _L1_ffn_in['Wa_down'], 'L1_ffn_ba_down': _L1_ffn_in['ba_down'], 'L1_ffn_Wa_up': _L1_ffn_in['Wa_up'], 'L1_ffn_ba_up': _L1_ffn_in['ba_up']}

def reference(x, ctx_1024, L0_attn_rms_weight, L0_attn_W_in, L0_attn_gate_bias, L0_attn_W_out, L0_xattn_Wq, L0_xattn_Wkv, L0_xattn_Wproj, L0_xattn_b_proj, L0_ffn_gate_w, L0_ffn_expert_bias, L0_ffn_w_gate, L0_ffn_w_up, L0_ffn_w_down, L0_ffn_shared_gate_w, L0_ffn_shared_up_w, L0_ffn_shared_down_w, L1_attn_Wqk, L1_attn_bqk, L1_attn_Wv, L1_attn_bv, L1_attn_Wn, L1_attn_bn, L1_attn_Wo, L1_attn_bo, L1_xattn_Wq, L1_xattn_bq, L1_xattn_Aq, L1_xattn_Bq, L1_xattn_Wf, L1_xattn_bf, L1_xattn_Af, L1_xattn_Bf, L1_xattn_Wp, L1_xattn_bp, L1_xattn_Ap, L1_xattn_Bp, L1_ffn_W_base, L1_ffn_b_base, L1_ffn_Wd1, L1_ffn_bd1, L1_ffn_Wd2, L1_ffn_bd2, L1_ffn_Wa_down, L1_ffn_ba_down, L1_ffn_Wa_up, L1_ffn_ba_up):
    import jax
    import jax.numpy as jnp

    def _L0_attn_ref(hidden_states, rms_weight, W_in, gate_bias, W_out):
        import jax, jax.numpy as jnp
        import numpy as np
        D_MODEL = 256
        NUM_HEAD = 16
        CHUNK = 64
        NGROUPS = 2
        D_HEAD = D_MODEL // NUM_HEAD
        NEG = -1e+30

        def _scan_op(a, b):
            ga, xa = a
            gb, xb = b
            return (gb * ga, gb * xa + xb)
        bs, seq, d = hidden_states.shape
        dh = d // NUM_HEAD
        nc = seq // CHUNK
        scale = dh ** (-0.5)
        rep = NUM_HEAD // NGROUPS
        shortcut = hidden_states
        h = hidden_states * jax.lax.rsqrt(jnp.mean(hidden_states ** 2, axis=-1, keepdims=True) + 1e-06) * rms_weight
        proj = h @ W_in
        z, x, g, q, k = jnp.split(proj, [d, 2 * d, 3 * d, 3 * d + NGROUPS * dh], axis=-1)
        z = jax.nn.sigmoid(z)
        g = jax.nn.sigmoid(g + gate_bias)
        q = jnp.tile(q, (1, 1, rep))
        k = jnp.tile(k, (1, 1, rep))
        qh = q.reshape(bs, seq, NUM_HEAD, dh).transpose(0, 2, 1, 3)
        xc = x.reshape(bs, nc, CHUNK, d)
        gc = g.reshape(bs, nc, CHUNK, d)
        kc = k.reshape(bs, nc, CHUNK, d)
        g2 = jnp.concatenate([gc, gc], axis=-1)
        v = (1.0 - g2) * jnp.concatenate([xc, kc], axis=-1)
        _, xk = jax.lax.associative_scan(_scan_op, (g2, v), axis=2)
        intra_x = xk[..., :d].reshape(bs, seq, NUM_HEAD, dh).transpose(0, 2, 1, 3)
        intra_k = xk[..., d:].reshape(bs, seq, NUM_HEAD, dh).transpose(0, 2, 1, 3)
        chunk_k = intra_k[:, :, ::CHUNK, :]
        chunk_x = intra_x[:, :, ::CHUNK, :]
        scores = jnp.einsum('bhsd,bhcd->bhsc', qh, chunk_k) * scale
        allowed = jnp.arange(seq)[:, None] // CHUNK > jnp.arange(nc)[None, :]
        masked = jnp.where(allowed, scores, NEG)
        intra_lse = jnp.einsum('bhsd,bhsd->bhs', qh, intra_k) * scale
        m = jnp.maximum(jnp.max(masked, axis=-1), intra_lse)
        w = jnp.exp(masked - m[..., None])
        intra_w = jnp.exp(intra_lse - m)
        denom = jnp.sum(w, axis=-1) + intra_w
        out = (jnp.einsum('bhsc,bhcd->bhsd', w, chunk_x) + intra_w[..., None] * intra_x) / denom[..., None]
        out = out.transpose(0, 2, 1, 3).reshape(bs, seq, d)
        return z * out @ W_out + shortcut

    def _L0_xattn_ref(inputs_q, inputs_kv, Wq, Wkv, Wproj, b_proj):
        import jax, jax.numpy as jnp
        import numpy as np
        B, Q, K, D, H, DH = (4, 128, 1024, 256, 8, 128)
        q = jnp.einsum('bqd,dhe->bqhe', inputs_q, Wq)
        kv = jnp.einsum('bkd,dhe->bkhe', inputs_kv, Wkv)
        k, v = (kv[..., :DH], kv[..., DH:])
        attn = jnp.einsum('bqhd,bkhd->bhqk', q, k) / np.sqrt(DH)
        attn = jax.nn.softmax(attn.astype(jnp.float32), axis=-1).astype(v.dtype)
        o = jnp.einsum('bhqk,bkhd->bqhd', attn, v)
        return jnp.einsum('bqhd,hdo->bqo', o, Wproj) + b_proj

    def _L0_ffn_ref(x, gate_w, expert_bias, w_gate, w_up, w_down, shared_gate_w, shared_up_w, shared_down_w):
        import jax, jax.numpy as jnp
        import numpy as np
        B, S, D = (2, 128, 256)
        E, K, I = (16, 8, 256)
        I_SH = 256
        ROUTE_SCALE = 2.826
        gates = jnp.einsum('bsd,ed->bse', x, gate_w)
        scores = jax.nn.sigmoid(gates.astype(jnp.float32))
        sel_scores = scores + expert_bias
        _, inds = jax.lax.top_k(sel_scores, K)
        selected = jnp.take_along_axis(scores, inds, axis=-1)
        selected = selected / selected.sum(axis=-1, keepdims=True)
        selected = selected * ROUTE_SCALE
        onehot = jax.nn.one_hot(inds, E, dtype=selected.dtype)
        combine = jnp.einsum('bske,bsk->bse', onehot, selected)
        hg = jnp.einsum('bsd,eid->bsei', x, w_gate)
        hu = jnp.einsum('bsd,eid->bsei', x, w_up)
        h = jax.nn.silu(hg) * hu
        ye = jnp.einsum('bsei,edi->bsed', h, w_down)
        y = jnp.einsum('bsed,bse->bsd', ye, combine).astype(x.dtype)
        g = jnp.einsum('bsd,id->bsi', x, shared_gate_w)
        u = jnp.einsum('bsd,id->bsi', x, shared_up_w)
        y = y + jnp.einsum('bsi,di->bsd', jax.nn.silu(g) * u, shared_down_w)
        return y

    def _L1_attn_ref(x, Wqk, bqk, Wv, bv, Wn, bn, Wo, bo):
        import jax, jax.numpy as jnp
        import numpy as np
        D_MODEL = 256
        D_QK = 256
        NUM_HEADS = 16
        HEAD_DIM = D_QK // NUM_HEADS
        V_DIM = D_MODEL // NUM_HEADS
        B, S = (2, 512)
        b, s, _ = x.shape
        qk = x @ Wqk + bqk
        v = x @ Wv + bv
        n = x @ Wn + bn
        qk = qk.reshape(b, s, 2, NUM_HEADS, HEAD_DIM)
        q, k = (qk[:, :, 0], qk[:, :, 1])
        v = v.reshape(b, s, NUM_HEADS, V_DIM)
        scores = jnp.einsum('bthd,bshd->bhts', q, k)
        mask = jnp.tril(jnp.ones((s, s), dtype=scores.dtype))
        n_exp = jnp.exp(jnp.transpose(n, (0, 2, 1)))
        attn = scores * mask / n_exp[:, :, :, None]
        ctx = jnp.einsum('bhts,bshd->bthd', attn, v)
        ctx = ctx.reshape(b, s, D_MODEL)
        return ctx @ Wo + bo

    def _L1_xattn_ref(x, feature, Wq, bq, Aq, Bq, Wf, bf, Af, Bf, Wp, bp, Ap, Bp):
        import jax, jax.numpy as jnp
        import numpy as np
        N_EMBD = 256
        N_HEAD = 16
        R = 16
        SCALING = 1.0 / 16.0

        def lora_linear(x, W, b, A, B):
            return x @ W.T + b + x @ A.T @ B.T * SCALING
        Bsz, T, C = x.shape
        S = feature.shape[1]
        H = N_HEAD
        D = C // H
        q = lora_linear(x, Wq, bq, Aq, Bq).reshape(Bsz, T, H, D).transpose(0, 2, 1, 3)
        kv = lora_linear(feature, Wf, bf, Af, Bf)
        k, v = (kv[..., :C], kv[..., C:])
        k = k.reshape(Bsz, S, H, D).transpose(0, 2, 1, 3)
        v = v.reshape(Bsz, S, H, D).transpose(0, 2, 1, 3)
        att = jnp.einsum('bhtd,bhsd->bhts', q, k) * (1.0 / np.sqrt(D))
        mask = jnp.tril(jnp.ones((T, S), bool))
        att = jnp.where(mask, att, -jnp.inf)
        att = jax.nn.softmax(att, axis=-1)
        y = jnp.einsum('bhts,bhsd->bhtd', att, v)
        y = y.transpose(0, 2, 1, 3).reshape(Bsz, T, C)
        return lora_linear(y, Wp, bp, Ap, Bp)

    def _L1_ffn_ref(x, W_base, b_base, Wd1, bd1, Wd2, bd2, Wa_down, ba_down, Wa_up, ba_up):
        import jax, jax.numpy as jnp
        import numpy as np
        E = 8
        D = 256
        DO = 256
        R = 64
        H = 64
        B, T = (8, 512)
        base = jnp.einsum('btd,do->bto', x, W_base) + b_base
        h = jax.nn.relu(jnp.einsum('btd,edh->ebth', x, Wd1) + bd1[:, None, None, :])
        recon = jnp.einsum('ebth,ehd->ebtd', h, Wd2) + bd2[:, None, None, :]
        losses = jnp.mean((recon - x[None]) ** 2, axis=(2, 3))
        idx = jnp.argmin(losses, axis=0)
        a = jax.nn.relu(jnp.einsum('btd,bdr->btr', x, Wa_down[idx]) + ba_down[idx][:, None, :])
        adapter_out = jnp.einsum('btr,bro->bto', a, Wa_up[idx]) + ba_up[idx][:, None, :]
        return base + adapter_out
    x = x + _L0_attn_ref(_layernorm(x, axis=-1), L0_attn_rms_weight, L0_attn_W_in, L0_attn_gate_bias, L0_attn_W_out)
    x = x + _L0_xattn_ref(_layernorm(x, axis=-1), ctx_1024, L0_xattn_Wq, L0_xattn_Wkv, L0_xattn_Wproj, L0_xattn_b_proj)
    x = x + _L0_ffn_ref(_layernorm(x, axis=-1), L0_ffn_gate_w, L0_ffn_expert_bias, L0_ffn_w_gate, L0_ffn_w_up, L0_ffn_w_down, L0_ffn_shared_gate_w, L0_ffn_shared_up_w, L0_ffn_shared_down_w)
    x = x + _L1_attn_ref(_layernorm(x, axis=-1), L1_attn_Wqk, L1_attn_bqk, L1_attn_Wv, L1_attn_bv, L1_attn_Wn, L1_attn_bn, L1_attn_Wo, L1_attn_bo)
    x = x + _L1_xattn_ref(_layernorm(x, axis=-1), ctx_1024, L1_xattn_Wq, L1_xattn_bq, L1_xattn_Aq, L1_xattn_Bq, L1_xattn_Wf, L1_xattn_bf, L1_xattn_Af, L1_xattn_Bf, L1_xattn_Wp, L1_xattn_bp, L1_xattn_Ap, L1_xattn_Bp)
    x = x + _L1_ffn_ref(_layernorm(x, axis=-1), L1_ffn_W_base, L1_ffn_b_base, L1_ffn_Wd1, L1_ffn_bd1, L1_ffn_Wd2, L1_ffn_bd2, L1_ffn_Wa_down, L1_ffn_ba_down, L1_ffn_Wa_up, L1_ffn_ba_up)
    return x

_drawn_inputs = setup_inputs


def setup_inputs(seed=0):
    import zlib

    import numpy as np

    out = dict(_drawn_inputs(seed))
    spreads = {'L0_attn_rms_weight': (1.0, 0.6),
     'L0_xattn_b_proj': (0.0, 0.1),
     'L0_ffn_expert_bias': (0.0, 0.8),
     'L1_xattn_bq': (0.0, 2.0),
     'L1_xattn_Bq': (0.0, 2.0),
     'L1_xattn_bf': (0.0, 0.8),
     'L1_xattn_Bf': (0.0, 0.8),
     'L1_xattn_bp': (0.0, 0.655),
     'L1_xattn_Bp': (0.0, 0.8),
     'L1_ffn_b_base': (0.0, 0.3),
     'L1_ffn_bd1': (0.0, 0.1),
     'L1_ffn_bd2': (0.0, 0.1),
     'L1_ffn_ba_down': (0.0, 0.398),
     'L1_ffn_ba_up': (0.0, 0.291)}
    factors = {'L0_attn_gate_bias': 2.841,
     'L0_ffn_gate_w': 8.0,
     'L0_ffn_w_gate': 6.075,
     'L0_ffn_w_up': 5.953,
     'L0_ffn_w_down': 5.987,
     'L0_ffn_shared_gate_w': 6.069,
     'L0_ffn_shared_up_w': 5.927,
     'L0_ffn_shared_down_w': 5.967,
     'L1_attn_bn': 10.338,
     'L1_attn_bo': 23.722,
     'L1_xattn_Wq': 8.0,
     'L1_xattn_Aq': 26.56,
     'L1_xattn_Wf': 3.51,
     'L1_xattn_Af': 8.0,
     'L1_xattn_Ap': 8.0}
    for name, (base, spread) in spreads.items():
        noise = np.random.default_rng([zlib.crc32(name.encode()), seed]).standard_normal(out[name].shape)
        drawn = base * np.exp(spread * noise) if base else spread * noise
        out[name] = jnp.asarray(drawn.astype(out[name].dtype))
    for name, factor in factors.items():
        out[name] = (out[name] * factor).astype(out[name].dtype)
    return out
```

```python
from contextlib import ExitStack

import concourse.bass as bass
from concourse import mybir

ALU = mybir.AluOpType
ACT = mybir.ActivationFunctionType
F32 = mybir.dt.float32
F32R = mybir.dt.float32r
AX_X = mybir.AxisListType.X

P = 128
B, S, D = 4, 1024, 256
TOK = B * S
NT = TOK // P
KD = D // P
CH = 512
NC = TOK // CH
TPC = CH // P
EPS = 1e-5


def after(eng, sem, t, depth, per=1):
    if isinstance(t, int) and t < depth:
        return
    eng.wait_ge(sem, (t - depth + 1) * per)


def pipeline(eng, n, unroll, lags, step, per=None, ahead=False):
    most = max(lag[0] if isinstance(lag, tuple) else lag for lag in lags)
    head = -(-(most + 2) // unroll) * unroll
    tail = (n - head) % unroll + (unroll if ahead else 0)

    def at(i, off, whole):
        for lag in lags:
            item = off - (lag[0] if isinstance(lag, tuple) else lag)
            if whole or 0 <= item < n:
                more = () if per is None else (i * (unroll // per) + item // per,)
                step(i * unroll + item, item % unroll, lag, *more)

    for t in range(min(head, n + most)):
        at(0, t, False)
    if n - tail > head:
        with eng.Fori(0, (n - tail - head) // unroll) as i:
            for u in range(unroll):
                at(i, head + u, True)
    for t in range(max(head, n - tail), n + most):
        at(0, t, False)


class Core:

    def __init__(self, nc, ctx):
        self.nc, self.ctx = nc, ctx
        self.branch_sems = []
        self.x = self.sb("x_rows", [P, NT, D])
        self.ident = self.sb("ident", [P, P])
        self.head_of = self.sb("head_of", [P, 8])
        self.stats = self.sb("stats", [P, NT, 6])
        self.mean = self.sb("mean", [P, NT])
        self.rstd = self.sb("rstd", [P, NT])
        self.rstd_ln = self.sb("rstd_ln", [P, NT])

    def sb(self, name, shape, dt=F32, ctx=None):
        return (ctx or self.ctx).enter_context(self.nc.sbuf_tensor(name, shape, dt))

    def ps(self, name, shape, ctx):
        return ctx.enter_context(self.nc.psum_tensor(name, shape, F32))

    def sem(self, name):
        self.branch_sems.append(self.nc.alloc_semaphore(name=name))
        return self.branch_sems[-1]

    def end_branch(self):
        self.nc.clear_and_free_semaphores(self.branch_sems)
        self.branch_sems = []
        self.nc.all_engine_barrier()


def mm3(nc, out, lhs, rhs, start, stop, **kw):
    (lh, ll), (rh, rl) = lhs, rhs
    nc.tensor.matmul(out, lh, rh, start=start, stop=False, **kw)
    nc.tensor.matmul(out, lh, rl, start=False, stop=False, **kw)
    return nc.tensor.matmul(out, ll, rh, start=False, stop=stop, **kw)


def load_and_constants(core, x_in):
    nc = core.nc
    loaded, made, done = core.sem("x_loaded"), core.sem("zeroed"), core.sem("ident_made")
    with nc.Block() as block:
        @block.sync
        def _(sp):
            sp.dma_start(core.x[:], x_in.rearrange("b (t p) d -> p (b t) d", p=P)).then_inc(loaded, 16)
            sp.wait_ge(loaded, 16)

        @block.gpsimd
        def _(pool):
            nc.gpsimd.memset(core.ident[:], 0.0).then_inc(made, 1)
            pool.wait_ge(made, 1)
            nc.gpsimd.affine_select(out=core.ident[:], in_=core.ident[:], compare_op=ALU.not_equal, fill=1.0,
                                    base=0, pattern=[[-1, P]], channel_multiplier=1).then_inc(done, 1)
            nc.gpsimd.memset(core.head_of[:], 1.0).then_inc(made, 1)
            pool.wait_ge(made, 2)
            nc.gpsimd.affine_select(out=core.head_of[:], in_=core.head_of[:], compare_op=ALU.is_ge, fill=0.0,
                                    base=0, pattern=[[-16, 8]], channel_multiplier=1).then_inc(done, 1)
            pool.wait_ge(done, 2)
            nc.gpsimd.affine_select(out=core.head_of[:], in_=core.head_of[:], compare_op=ALU.is_ge, fill=0.0,
                                    base=15, pattern=[[16, 8]], channel_multiplier=-1).then_inc(done, 1)
            pool.wait_ge(done, 3)


def row_stats(core, tag, rms=False, weights=(), loads=(), zeros=(), ones=(), scaled=None):
    nc, x, st, mean, rstd = core.nc, core.x, core.stats, core.mean, core.rstd
    with ExitStack() as ctx:
        tmp = core.sb(f"{tag}_tmp", [P, 6, NT], ctx=ctx)
        stats_in, dve, rooted = core.sem(f"{tag}_stats"), core.sem(f"{tag}_dve"), core.sem(f"{tag}_sqrt")
        var_ready = core.sem(f"{tag}_var")
        gap, var, std, r1, r2 = (tmp[:, j, :] for j in range(5))
        w_in = [core.sem(f"{tag}_stage_w{n}_in") for n in range(len(weights))]
        w_high, w_low, in_, filled, w_scaled = (
            core.sem(f"{tag}_stage_{q}") for q in ("whigh", "wlow", "in", "filled", "wscaled"))
        with nc.Block() as block:
            @block.sync
            def _(sp):
                for arrived, (raw, source, _, _) in zip(w_in, weights):
                    sp.dma_start(raw, source).then_inc(arrived, 16)
                for place, source in loads:
                    sp.dma_start(place, source).then_inc(in_, 16)
                if loads:
                    sp.wait_ge(in_, 16 * len(loads))

            @block.gpsimd
            def _(pool):
                for place in zeros:
                    nc.gpsimd.memset(place, 0.0).then_inc(filled, 1)
                for place in ones:
                    nc.gpsimd.memset(place, 1.0).then_inc(filled, 1)
                for n, (raw, _, high, low) in enumerate(weights):
                    pool.wait_ge(w_high, n + 1)
                    nc.gpsimd.tensor_tensor(low, raw, high.bitcast(F32), ALU.subtract).then_inc(w_low, 1)
                if weights:
                    pool.wait_ge(w_low, len(weights))
                if zeros or ones:
                    pool.wait_ge(filled, len(zeros) + len(ones))

            @block.vector
            def _(v):
                links = [0]

                def link(ins):
                    links[0] += 1
                    ins.then_inc(dve, 1)
                    v.wait_ge(dve, links[0])

                with v.Fori(0, NT) as i:
                    nc.vector.bn_stats(st[:, i, :], x[:, i, :]).then_inc(stats_in, 1)
                v.wait_ge(stats_in, NT)
                link(nc.vector.tensor_tensor(gap, st[:, :, 1], st[:, :, 4], ALU.subtract))
                link(nc.vector.tensor_tensor(mean[:], st[:, :, 1], st[:, :, 4], ALU.add))
                link(nc.vector.tensor_scalar(mean[:], mean[:], 0.5, None, ALU.mult))
                link(nc.vector.tensor_tensor(var, st[:, :, 2], st[:, :, 5], ALU.add))
                link(nc.vector.tensor_scalar(var, var, 1.0 / D, None, ALU.mult))
                link(nc.vector.scalar_tensor_tensor(out=gap, in0=gap, scalar=0.25, in1=gap, op0=ALU.mult, op1=ALU.mult))
                link(nc.vector.tensor_tensor(var, var, gap, ALU.add))
                nc.vector.tensor_scalar(r2, var, EPS, None, ALU.add).then_inc(var_ready, 1)
                v.wait_ge(rooted, 1)
                nc.vector.reciprocal(rstd[:], std).then_inc(dve, 1)
                links[0] += 1
                v.wait_ge(dve, links[0])
                if rms:
                    link(nc.vector.tensor_copy(r1, rstd[:]))
                    link(nc.vector.tensor_copy(core.rstd_ln[:], rstd[:]))
                    link(nc.vector.tensor_tensor(var, var, r1, ALU.mult))
                    link(nc.vector.tensor_tensor(var, var, r1, ALU.mult))
                    nc.vector.tensor_scalar(r2, var, 1e-6, None, ALU.add).then_inc(var_ready, 1)
                    v.wait_ge(rooted, 2)
                    link(nc.vector.reciprocal(r2, std))
                    link(nc.vector.tensor_tensor(rstd[:], r1, r2, ALU.mult))

            @block.scalar
            def _(a):
                for n in range(2 if rms else 1):
                    a.wait_ge(var_ready, n + 1)
                    nc.scalar.activation(std, r2, ACT.Sqrt).then_inc(rooted, 1)
                for arrived, (raw, _, high, _) in zip(w_in, weights):
                    a.wait_ge(arrived, 16)
                    if scaled is not None and arrived is w_in[0]:
                        a.wait_ge(in_, 16 * len(loads))
                        for k in range(KD):
                            nc.scalar.activation(raw[:, k], raw[:, k], ACT.Copy, scale=scaled[:, k:k + 1]).then_inc(w_scaled, 1)
                        a.wait_ge(w_scaled, KD)
                    nc.scalar.activation(high, raw, ACT.Copy).then_inc(w_high, 1)


class Norm:

    def __init__(self, core, tag, ctx, turned_banks, whole=False, resident=None):
        self.core = core
        self.resident = resident
        self.xn = core.sb(f"{tag}_xn", [P, 2, TPC, D], ctx=ctx)
        if resident is None:
            self.xh = core.sb(f"{tag}_xh", [P, 2, KD, CH], F32R, ctx=ctx)
            self.xl = core.sb(f"{tag}_xl", [P, 2, KD, CH], F32R, ctx=ctx)
        self.turned = turned_banks
        self.whole = core.sb(f"{tag}_whole", [P, 2, KD, CH], ctx=ctx) if whole else None
        self.s_whole = core.sem(f"{tag}_xwhole") if whole else None
        self.normed, self.turn, self.high, self.low = (
            core.sem(f"{tag}_{n}") for n in ("normed", "turned", "xhigh", "xlow"))

    def hi(self, c, s):
        return self.resident[0][:, :, bass.ds(c * CH, CH)] if self.resident else self.xh[:, s]

    def lo(self, c, s):
        return self.resident[1][:, :, bass.ds(c * CH, CH)] if self.resident else self.xl[:, s]

    def normalise(self, v, c, s):
        core, nc = self.core, self.core.nc
        after(v, self.turn, c, 2)
        for j in range(TPC):
            t = c * TPC + j
            ins = nc.vector.tensor_scalar(self.xn[:, s, j, :], core.x[:, t, :], core.mean[:, bass.ds(t, 1)],
                                          core.rstd[:, bass.ds(t, 1)], ALU.subtract, ALU.mult)
        ins.then_inc(self.normed, 1)

    def transpose(self, pe, c, s):
        nc = self.core.nc
        pe.wait_ge(self.normed, c + 1)
        for k in range(KD):
            for j in range(TPC):
                ins = nc.tensor.transpose(self.turned[:, k, j * P:(j + 1) * P],
                                          self.xn[:, s, j, k * P:(k + 1) * P], self.core.ident[:])
        ins.then_inc(self.turn, 1)

    def take(self, a, c, s):
        nc = self.core.nc
        a.wait_ge(self.turn, c + 1)
        source = self.turned[:, 0:KD, :]
        if self.whole is not None:
            nc.scalar.activation(self.whole[:, s], source, ACT.Copy).then_inc(self.s_whole, 1)
            a.wait_ge(self.s_whole, c + 1)
            source = self.whole[:, s]
        nc.scalar.activation(self.hi(c, s), source, ACT.Copy).then_inc(self.high, 1)

    def take_low(self, v, c, s):
        v.wait_ge(self.high, c + 1)
        source = self.turned[:, 0:KD, :] if self.whole is None else self.whole[:, s]
        self.core.nc.vector.tensor_tensor(self.lo(c, s), source, self.hi(c, s).bitcast(F32),
                                          ALU.subtract).then_inc(self.low, 1)


def experts(core, moe_w, gate_w, expert_bias):
    nc, x = core.nc, core.x
    NE = moe_w.shape[0]
    ER = NE - 1
    with ExitStack() as ctx:
        XH = core.sb("moe_xh", [P, KD, TOK], F32R, ctx)
        XL = core.sb("moe_xl", [P, KD, TOK], F32R, ctx)
        comb = core.sb("moe_comb", [P, NE, NT], ctx=ctx)
        route(core, gate_w, expert_bias, XH, XL, comb)

        raw = core.sb("moe_raw", [P, 3, KD, D], ctx=ctx)
        wh = core.sb("moe_wh", [P, 2, 3, KD, D], F32R, ctx)
        wl = core.sb("moe_wl", [P, 2, 3, KD, D], F32R, ctx)
        act_g = core.sb("moe_act_g", [P, 2, CH], ctx=ctx)
        h = core.sb("moe_h", [P, 2, CH], ctx=ctx)
        hh = core.sb("moe_hh", [P, 2, 2, CH], F32R, ctx)
        hl = core.sb("moe_hl", [P, 2, 2, CH], F32R, ctx)
        gu = core.ps("moe_gu", [P, 2, 2, CH], ctx)
        y = core.ps("moe_y", [P, 2, TPC, D], ctx)
        s_raw, s_wh, s_wl = core.sem("moe_raw_in"), core.sem("moe_whigh"), core.sem("moe_wlow")
        s_gu, s_silu, s_h, s_hh, s_hl, s_y, s_acc = (
            core.sem(f"moe_{n}") for n in ("gu", "silu", "h", "hhigh", "hlow", "y", "acc"))
        n = NE * NC

        with nc.Block() as block:
            @block.sync
            def _(sp):
                def load(e):
                    after(sp, s_wh, e, 1)
                    after(sp, s_wl, e, 1)
                    sp.dma_start(raw[:], moe_w[e]).then_inc(s_raw, 16)

                load(0)
                with sp.Fori(1, NE) as e:
                    sp.wait_ge(s_wh, e)
                    sp.wait_ge(s_wl, e)
                    sp.dma_start(raw[:], moe_w[bass.ds(e, 1)].rearrange("o p a k n -> (o p) a k n")).then_inc(s_raw, 16)

            @block.gpsimd
            def _(pool):
                def low(e, u):
                    pool.wait_ge(s_wh, e + 1)
                    nc.gpsimd.tensor_tensor(wl[:, u], raw[:], wh[:, u].bitcast(F32), ALU.subtract).then_inc(s_wl, 1)

                pipeline(pool, NE, 2, [0], lambda e, u, lag: low(e, u))

            @block.scalar
            def _(a):
                def weights_high(e, u):
                    a.wait_ge(s_raw, (e + 1) * 16)
                    after(a, s_y, e, 2, NC)
                    nc.scalar.activation(wh[:, u], raw[:], ACT.Copy).then_inc(s_wh, 1)

                def step(t, u, e, more=True):
                    for ib in range(2):
                        a.wait_ge(s_gu, 2 * t + ib + 1)
                        after(a, s_h, t, 1, 2)
                        nc.scalar.activation(act_g[:, ib], gu[:, ib, 0, :], ACT.Silu).then_inc(s_silu, 1)
                    for ib in range(2):
                        a.wait_ge(s_h, 2 * t + ib + 1)
                        after(a, s_y, t, 2)
                        nc.scalar.activation(hh[:, u % 2, ib], h[:, ib], ACT.Copy).then_inc(s_hh, 1)
                    if u % NC == 2 and more:
                        weights_high(e + 1, (u // NC + 1) % 2)

                weights_high(0, 0)
                for t in range(NC):
                    step(t, t, 0)
                with a.Fori(0, (NE - 3) // 2) as i:
                    for r in range(NC, 3 * NC):
                        step(i * (2 * NC) + r, r % (2 * NC), i * 2 + r // NC)
                for t in range(n - 2 * NC, n):
                    step(t, t % (2 * NC), t // NC, t // NC + 1 < NE)

            @block.vector
            def _(v):
                def step(t, u, lag, e):
                    if lag == 0:
                        for ib in range(2):
                            v.wait_ge(s_silu, 2 * t + ib + 1)
                            after(v, s_hh, t, 1, 2)
                            after(v, s_hl, t, 1, 2)
                            nc.vector.tensor_tensor(h[:, ib], act_g[:, ib], gu[:, ib, 1, :], ALU.mult).then_inc(s_h, 1)
                        for ib in range(2):
                            v.wait_ge(s_hh, 2 * t + ib + 1)
                            nc.vector.tensor_tensor(hl[:, u % 2, ib], h[:, ib], hh[:, u % 2, ib].bitcast(F32),
                                                    ALU.subtract).then_inc(s_hl, 1)
                    else:
                        v.wait_ge(s_y, t + 1)
                        after(v, s_acc, t, 1)
                        c = u % NC
                        for j in range(TPC):
                            tile = c * TPC + j
                            w = comb[:].rearrange("p e t -> p (e t)")[:, bass.ds(e * NT + tile, 1)]
                            ins = nc.vector.scalar_tensor_tensor(out=x[:, tile, :], in0=y[:, u % 2, j, :], scalar=w,
                                                                 in1=x[:, tile, :], op0=ALU.mult, op1=ALU.add)
                        ins.then_inc(s_acc, 1)

                pipeline_body(v, n, step)

            @block.tensor
            def _(pe):
                def step(t, u, lag, e):
                    es = u // NC % 2
                    c = u % NC
                    if lag == 0:
                        if c == 0:
                            pe.wait_ge(s_wl, e + 1)
                        rhs = (XH, XL)
                        for ib in range(2):
                            after(pe, s_h, t, 1, 2)
                            for g in range(2):
                                for k in range(KD):
                                    ins = mm3(nc, gu[:, ib, g, :],
                                              [w[:, es, g, k, ib * P:(ib + 1) * P] for w in (wh, wl)],
                                              [r[:, k, c * CH:(c + 1) * CH] for r in rhs],
                                              start=(k == 0), stop=(k == KD - 1))
                            ins.then_inc(s_gu, 1)
                    else:
                        pe.wait_ge(s_hl, 2 * t + 2)
                        after(pe, s_acc, t, 2)
                        for j in range(TPC):
                            for ib in range(2):
                                ins = mm3(nc, y[:, u % 2, j, :],
                                          [r[:, u % 2, ib, j * P:(j + 1) * P] for r in (hh, hl)],
                                          [w[:, es, 2, ib, :] for w in (wh, wl)],
                                          start=(ib == 0), stop=(ib == 1))
                        ins.then_inc(s_y, 1)

                pipeline_body(pe, n, step)


def pipeline_body(eng, n, step):
    for t in range(NC):
        step(t, t, 0, 0)
        if t:
            step(t - 1, t - 1, 1, 0)
    with eng.Fori(0, (n - NC) // (2 * NC)) as i:
        for r in range(NC, 3 * NC):
            step(i * (2 * NC) + r, r % (2 * NC), 0, i * 2 + r // NC)
            step(i * (2 * NC) + (r - 1), (r - 1) % (2 * NC), 1, i * 2 + (r - 1) // NC)
    step(n - 1, (n - 1) % (2 * NC), 1, (n - 1) // NC)


def route(core, gate_w, expert_bias, XH, XL, comb):
    nc, x = core.nc, core.x
    E, K_TOP, ROUTE_SCALE = 16, 8, 2.826
    row_stats(core, "moe", False)
    with ExitStack() as ctx:
        turned = core.ps("moe_turned", [P, KD, CH], ctx)
        gates = core.ps("moe_gates", [P, 2, CH], ctx)
        gw = core.sb("moe_gw", [P, KD, E], ctx=ctx)
        bias = core.sb("moe_bias", [P, E], ctx=ctx)
        score, sel, left, top = (core.sb(f"moe_{q}", [P, NT, w], ctx=ctx)
                                 for q, w in (("score", E), ("sel", E), ("left", E), ("top", K_TOP)))
        total = core.sb("moe_total", [P, NT], ctx=ctx)
        norm = Norm(core, "moe", ctx, turned, whole=True, resident=(XH, XL))
        loaded, s_gates, s_gcopy, s_score, dve, s_top = (
            core.sem(f"moe_{q}") for q in ("gw_in", "gates", "gcopy", "score", "rdve", "top"))
        with nc.Block() as block:
            @block.sync
            def _(sp):
                sp.dma_start(gw[:], gate_w.rearrange("(k p) e -> p k e", p=P)).then_inc(loaded, 16)
                sp.dma_start(bias[:], expert_bias.partition_broadcast(P)).then_inc(loaded, 16)

            @block.tensor
            def _(pe):
                def step(c, u, lag):
                    if lag == 0:
                        after(pe, norm.s_whole, c, 1)
                        norm.transpose(pe, c, u)
                    else:
                        pe.wait_ge(norm.s_whole, c + 1)
                        after(pe, s_gcopy, c, 2)
                        for j in range(TPC):
                            for k in range(KD):
                                ins = nc.tensor.matmul(gates[:, u, j * E:(j + 1) * E],
                                                       norm.whole[:, u, k, j * P:(j + 1) * P], gw[:, k, :],
                                                       start=(k == 0), stop=(k == KD - 1))
                        ins.then_inc(s_gates, 1)
                pe.wait_ge(loaded, 32)
                pipeline(pe, NC, 2, [0, 1], step)

            @block.scalar
            def _(a):
                def step(c, u, lag):
                    after(a, s_gates, c, 2)
                    after(a, norm.low, c, 2)
                    norm.take(a, c, u)
                pipeline(a, NC, 2, [0], step)
                a.wait_ge(s_gcopy, NC)
                nc.scalar.activation(score[:], sel[:], ACT.Sigmoid).then_inc(s_score, 1)

            @block.vector
            def _(v):
                def step(c, u, lag):
                    if lag == 0:
                        norm.normalise(v, c, u)
                    elif lag == 1:
                        norm.take_low(v, c, u)
                    else:
                        v.wait_ge(s_gates, c + 1)
                        nc.vector.tensor_copy(sel[:, bass.ds(c * TPC, TPC), :],
                                              gates[:, u, 0:TPC * E].rearrange("p (j e) -> p j e", e=E)).then_inc(s_gcopy, 1)
                pipeline(v, NC, 2, [0, 1, 2], step)
                v.wait_ge(s_score, 1)
                v.wait_ge(loaded, 32)
                nc.vector.tensor_tensor(sel[:], score[:], bias[:].unsqueeze(1).to_broadcast([P, NT, E]),
                                        ALU.add).then_inc(dve, 1)
                v.wait_ge(dve, 1)
                for t in range(NT):
                    nc.vector.max(top[:, t, :], sel[:, t, :]).then_inc(s_top, 1)
                for t in range(NT):
                    v.wait_ge(s_top, t + 1)
                    nc.vector.match_replace(left[:, t, :], top[:, t, :], sel[:, t, :], -1e30).then_inc(s_top, 1)
                v.wait_ge(s_top, 2 * NT)
                nc.vector.tensor_tensor(left[:], left[:], sel[:], ALU.not_equal).then_inc(dve, 1)
                v.wait_ge(dve, 2)
                nc.vector.tensor_tensor(score[:], left[:], score[:], ALU.mult).then_inc(dve, 1)
                v.wait_ge(dve, 3)
                nc.vector.tensor_reduce(total[:], score[:], AX_X, ALU.add).then_inc(dve, 1)
                v.wait_ge(dve, 4)
                nc.vector.reciprocal(total[:], total[:]).then_inc(dve, 1)
                v.wait_ge(dve, 5)
                nc.vector.tensor_scalar(total[:], total[:], ROUTE_SCALE, None, ALU.mult).then_inc(dve, 1)
                v.wait_ge(dve, 6)
                nc.vector.tensor_tensor(comb[:, 0:E, :], score[:].rearrange("p t e -> p e t"),
                                        total[:].unsqueeze(1).to_broadcast([P, E, NT]), ALU.mult).then_inc(dve, 1)
                nc.vector.memset(comb[:, E:E + 1, :], 1.0).then_inc(dve, 1)
                v.wait_ge(dve, 8)


def picked_adapter(core, w, out):
    nc, x = core.nc, core.x
    E, H = 8, 64
    EB = E // 2
    SEQ_CH = S // CH
    with ExitStack() as ctx:
        XH = core.sb("ffn_xh", [P, KD, TOK], F32R, ctx)
        XL = core.sb("ffn_xl", [P, KD, TOK], F32R, ctx)
        bd1 = core.sb("ffn_bd1", [P, EB], ctx=ctx)
        bd2 = core.sb("ffn_bd2", [P, KD, E], ctx=ctx)
        w_base = core.sb("ffn_w_base", [P, KD, D], ctx=ctx)
        loss = core.sb("ffn_loss", [P, NC, E, KD], ctx=ctx)
        wad = core.sb("ffn_wad", [P, KD, E, H], ctx=ctx)
        wau = core.sb("ffn_wau", [H + 1, E, D], ctx=ctx)
        bad = core.sb("ffn_bad", [H, E], ctx=ctx)
        first = core.sb("ffn_first", [P, E], ctx=ctx)
        base_row = core.sb("ffn_base_row", [H + 1, D], ctx=ctx)
        ones = core.sb("ffn_ones", [P, P], ctx=ctx)
        with ExitStack() as inner:
            raw1 = core.sb("ffn_raw1", [P, KD, E * H], ctx=inner)
            raw2 = core.sb("ffn_raw2", [P, EB, D], ctx=inner)
            w1 = [core.sb(f"ffn_w1{q}", [P, KD, E * H], F32R, inner) for q in "hl"]
            w2 = [core.sb(f"ffn_w2{q}", [P, EB, D], F32R, inner) for q in "hl"]
            row_stats(core, "ffn", weights=[(raw1[:], w["Wd1"], w1[0][:], w1[1][:]), (raw2[:], w["Wd2"], w2[0][:], w2[1][:])],
                      loads=[(bd1[:], w["bd1"]), (bd2[:], w["bd2"]), (w_base[:], w["W_base"]), (wad[:], w["Wa_down"]),
                             (wau[0:H], w["Wa_up"]), (wau[H:H + 1], w["ba_up"]), (bad[:], w["ba_down"]),
                             (first[:], w["first"].partition_broadcast(P))],
                      zeros=[base_row[0:H]], ones=[ones[:]])
            h = core.sb("ffn_h", [P, 2, CH], ctx=inner)
            hh = core.sb("ffn_hh", [P, 2, EB, CH], F32R, inner)
            hl = core.sb("ffn_hl", [P, 2, EB, CH], F32R, inner)
            gap = core.sb("ffn_gap", [P, 3, CH], ctx=inner)
            junk = core.sb("ffn_junk", [P, 2, CH], ctx=inner)
            turned = core.ps("ffn_turned", [P, KD, CH], inner)
            hp = core.ps("ffn_hp", [P, 2, CH], inner)
            rp = core.ps("ffn_rp", [P, 2, CH], inner)
            bp = core.ps("ffn_bp", [P, TPC, D], inner)
            norm = Norm(core, "ffn", inner, turned, whole=True, resident=(XH, XL))
            s_hp, s_relu, s_hh, s_hl, s_rp, s_gap, s_sq, s_bp, s_bx, s_row = (
                core.sem(f"ffn_{q}") for q in ("hp", "relu", "hhigh", "hlow", "rp", "gap", "sq", "bp", "bx", "row"))
            NR = E * KD

            with nc.Block() as block:
                @block.sync
                def _(sp):
                    sp.dma_start(base_row[H:H + 1], w["b_base"].rearrange("(o n) -> o n", o=1)).then_inc(s_row, 16)
                    sp.wait_ge(s_row, 16)

                @block.tensor
                def _(pe):
                    def turn(c, u):
                        after(pe, norm.s_whole, c, 1)
                        norm.transpose(pe, c, u)

                    def rebuild(c, u):
                        pe.wait_ge(norm.low, c + 1)
                        for q in range(EB):
                            m = c * EB + q
                            after(pe, s_relu, m, 2)
                            for k in range(KD):
                                ins = mm3(nc, hp[:, q % 2, :], [v[:, k, q * P:(q + 1) * P] for v in w1],
                                          (norm.hi(c, u)[:, k], norm.lo(c, u)[:, k]), start=(k == 0), stop=(k == KD - 1))
                            ins.then_inc(s_hp, 1)
                        for j in range(TPC):
                            after(pe, s_bx, c, 1)
                            for k in range(KD):
                                ins = nc.tensor.matmul(bp[:, j, :], norm.whole[:, u, k, j * P:(j + 1) * P],
                                                       w_base[:, k, :], start=(k == 0), stop=(k == KD - 1))
                        ins.then_inc(s_bp, 1)
                        for e in range(E):
                            r = slice(H * (e % 2), H * (e % 2) + H)
                            pe.wait_ge(s_hl, c * EB + e // 2 + 1)
                            for k in range(KD):
                                m = c * NR + e * KD + k
                                if isinstance(c, int) and c == 0 and e == 0:
                                    pass
                                else:
                                    pe.wait_ge(s_gap, m - 1)
                                mm3(nc, rp[:, k, :], [v[r, e // 2, k * P:(k + 1) * P] for v in w2],
                                    (hh[r, u, e // 2, :], hl[r, u, e // 2, :]), start=True, stop=True).then_inc(s_rp, 1)

                    turn(0, 0)
                    turn_then = lambda c, u: (turn(c + 1, 1 - u), rebuild(c, u))
                    turn_then(0, 0)
                    turn_then(1, 1)
                    with pe.Fori(1, NC // 2 - 1) as i:
                        turn_then(i * 2, 0)
                        turn_then(i * 2 + 1, 1)
                    turn_then(NC - 2, 0)
                    rebuild(NC - 1, 1)

                @block.scalar
                def _(a):
                    def step(c, u, lag):
                        if lag == 0:
                            after(a, s_bp, c, 2)
                            after(a, s_gap, c, 2, NR)
                            after(a, norm.low, c, 2)
                            norm.take(a, c, u)
                            return
                        for q in range(EB):
                            m = c * EB + q
                            a.wait_ge(s_hp, m + 1)
                            after(a, s_hl, m, 2)
                            nc.scalar.activation(h[:, q % 2], hp[:, q % 2, :], ACT.Relu, bias=bd1[:, q:q + 1]).then_inc(s_relu, 1)
                            after(a, s_rp, c, 2, NR)
                            a.wait_ge(s_relu, m + 1)
                            nc.scalar.activation(hh[:, u, q], h[:, q % 2], ACT.Copy).then_inc(s_hh, 1)
                        for e in range(E):
                            for k in range(KD):
                                m = c * NR + e * KD + k
                                a.wait_ge(s_gap, m + 1)
                                after(a, s_sq, m if isinstance(c, int) else c * NR, 2) if isinstance(c, int) else a.wait_ge(s_sq, m - 1)
                                nc.scalar.activation(junk[:, k], gap[:, (e * KD + k) % 2], ACT.Square,
                                                     accum_out=loss[:].rearrange("p c e k -> p (c e k)")[:, bass.ds(m, 1)]).then_inc(s_sq, 1)
                    pipeline(a, NC, 2, [0, 1], step)

                @block.vector
                def _(v):
                    def step(c, u, lag):
                        if lag == 0:
                            norm.normalise(v, c, u)
                            return
                        if lag == 1:
                            norm.take_low(v, c, u)
                            return
                        for q in range(EB):
                            v.wait_ge(s_hh, c * EB + q + 1)
                            nc.vector.tensor_tensor(hl[:, u, q], h[:, q % 2], hh[:, u, q].bitcast(F32),
                                                    ALU.subtract).then_inc(s_hl, 1)
                        v.wait_ge(s_bp, c + 1)
                        for j in range(TPC):
                            t = c * TPC + j
                            ins = nc.vector.tensor_tensor(x[:, t, :], x[:, t, :], bp[:, j, :], ALU.add)
                        ins.then_inc(s_bx, 1)
                        for e in range(E):
                            for k in range(KD):
                                m = c * NR + e * KD + k
                                v.wait_ge(s_rp, m + 1)
                                if not (isinstance(c, int) and m < 2):
                                    v.wait_ge(s_sq, m - 1)
                                nc.vector.scalar_tensor_tensor(out=gap[:, (e * KD + k) % 2], in0=rp[:, k, :], scalar=bd2[:, k, e:e + 1],
                                                               in1=norm.whole[:, u, k], op0=ALU.add,
                                                               op1=ALU.subtract).then_inc(s_gap, 1)
                    pipeline(v, NC, 2, [0, 1, 2], step)

        pick = core.sb("ffn_pick", [P, 4, B, E], ctx=ctx)
        best = core.sb("ffn_best", [P, 2, B], ctx=ctx)
        dsel = core.sb("ffn_dsel", [P, B, KD, H], ctx=ctx)
        usel = core.sb("ffn_usel", [H + 1, B, D], ctx=ctx)
        dbias = core.sb("ffn_dbias", [H, B], ctx=ctx)
        bprod = core.sb("ffn_bprod", [H, B, E], ctx=ctx)
        dh, dl = (core.sb(f"ffn_d{q}", [P, B, KD, H], F32R, ctx) for q in "hl")
        uh, ul = (core.sb(f"ffn_u{q}", [H + 1, B, D], F32R, ctx) for q in "hl")
        a_ = core.sb("ffn_a", [H, 2, CH], ctx=ctx)
        ah = core.sb("ffn_ah", [H + 1, 2, CH], F32R, ctx)
        al = core.sb("ffn_al", [H + 1, 2, CH], F32R, ctx)
        tp = core.ps("ffn_total", [P, B * E], ctx)
        ap = core.ps("ffn_ap", [H, 2, CH], ctx)
        op = core.ps("ffn_op", [P, 2, TPC, D], ctx)
        s_sum, s_tot, dve, s_sel, s_high, s_low, s_rows = (
            core.sem(f"ffn_{q}") for q in ("sum", "tot", "pdve", "selected", "shigh", "slow", "arows"))
        s_ap, s_a, s_ah, s_al, s_op, s_x, s_out = (core.sem(f"ffn_{q}") for q in ("ap", "a", "ah", "al", "op", "x", "out"))
        total, cand, hot = pick[:, 0], pick[:, 1], pick[:, 2]
        out_v = out.rearrange("b (t p) d -> p (b t) d", p=P)
        with nc.Block() as block:
            @block.tensor
            def _(pe):
                pe.wait_ge(s_sum, 2)
                nc.tensor.matmul(tp[:], ones[:], pick[:, 3].rearrange("p b e -> p (b e)"), start=True, stop=True).then_inc(s_tot, 1)
                pe.wait_ge(s_low, 2)
                pe.wait_ge(s_rows, 2)
                for c in range(NC + 1):
                    if c < NC:
                        after(pe, s_a, c, 2)
                        for k in range(KD):
                            ins = mm3(nc, ap[:, c % 2, :], (dh[:, c // SEQ_CH, k, :], dl[:, c // SEQ_CH, k, :]),
                                      (XH[:, k, c * CH:(c + 1) * CH], XL[:, k, c * CH:(c + 1) * CH]),
                                      start=(k == 0), stop=(k == KD - 1))
                        ins.then_inc(s_ap, 1)
                    if c:
                        d = c - 1
                        pe.wait_ge(s_al, d + 1)
                        after(pe, s_x, d, 2)
                        for j in range(TPC):
                            ins = mm3(nc, op[:, d % 2, j, :], [q[:, d % 2, j * P:(j + 1) * P] for q in (ah, al)],
                                      (uh[:, d // SEQ_CH, :], ul[:, d // SEQ_CH, :]), start=True, stop=True)
                        ins.then_inc(s_op, 1)

            @block.gpsimd
            def _(pool):
                nc.gpsimd.memset(ah[H:H + 1].bitcast(F32), 1.0).then_inc(s_rows, 1)
                nc.gpsimd.memset(al[H:H + 1].bitcast(F32), 0.0).then_inc(s_rows, 1)

            @block.scalar
            def _(a):
                a.wait_ge(s_sel, 1)
                nc.scalar.activation(dh[:], dsel[:], ACT.Copy).then_inc(s_high, 1)
                a.wait_ge(s_sel, 2)
                nc.scalar.activation(uh[:], usel[:], ACT.Copy).then_inc(s_high, 1)
                for c in range(NC):
                    a.wait_ge(s_ap, c + 1)
                    after(a, s_al, c, 2)
                    nc.scalar.activation(a_[:, c % 2], ap[:, c % 2, :], ACT.Relu, bias=dbias[:, c // SEQ_CH:c // SEQ_CH + 1]).then_inc(s_a, 1)
                    after(a, s_op, c, 2)
                    a.wait_ge(s_a, c + 1)
                    nc.scalar.activation(ah[0:H, c % 2], a_[:, c % 2], ACT.Copy).then_inc(s_ah, 1)

            @block.vector
            def _(v):
                links = [0]

                def link(ins):
                    links[0] += 1
                    ins.then_inc(dve, 1)
                    v.wait_ge(dve, links[0])

                lv = loss[:].rearrange("p (b c) e k -> p b c e k", c=SEQ_CH)
                link(nc.vector.tensor_tensor(pick[:, 0], lv[:, :, 0, :, 0], lv[:, :, 0, :, 1], ALU.add))
                nc.vector.tensor_tensor(pick[:, 1], lv[:, :, 1, :, 0], lv[:, :, 1, :, 1], ALU.add).then_inc(s_sum, 1)
                v.wait_ge(s_sum, 1)
                nc.vector.tensor_tensor(pick[:, 3], pick[:, 0], pick[:, 1], ALU.add).then_inc(s_sum, 1)
                v.wait_ge(s_tot, 1)
                link(nc.vector.tensor_scalar(total, tp[:].rearrange("p (b e) -> p b e", e=E), -1.0, None, ALU.mult))
                link(nc.vector.tensor_reduce(best[:, 0], total, AX_X, ALU.max))
                link(nc.vector.tensor_tensor(cand, total, best[:, 0].unsqueeze(2).to_broadcast([P, B, E]), ALU.is_equal))
                link(nc.vector.tensor_tensor(cand, cand, first[:].unsqueeze(1).to_broadcast([P, B, E]), ALU.mult))
                link(nc.vector.tensor_reduce(best[:, 1], cand, AX_X, ALU.max))
                link(nc.vector.tensor_tensor(hot, cand, best[:, 1].unsqueeze(2).to_broadcast([P, B, E]), ALU.is_equal))
                link(nc.vector.tensor_tensor(bprod[:], hot[0:H], bad[:].unsqueeze(1).to_broadcast([H, B, E]), ALU.mult))
                nc.vector.tensor_reduce(dbias[:], bprod[:], AX_X, ALU.add).then_inc(dve, 1)
                links[0] += 1
                for e in range(E):
                    for b in range(B):
                        if e == 0:
                            ins = nc.vector.tensor_scalar(dsel[:, b], wad[:, :, e, :], hot[:, b, e:e + 1], None, ALU.mult)
                        else:
                            ins = nc.vector.scalar_tensor_tensor(out=dsel[:, b], in0=wad[:, :, e, :], scalar=hot[:, b, e:e + 1],
                                                                 in1=dsel[:, b], op0=ALU.mult, op1=ALU.add)
                    if e == E - 1:
                        ins.then_inc(s_sel, 1)
                    else:
                        link(ins)
                for e in range(E):
                    for b in range(B):
                        ins = nc.vector.scalar_tensor_tensor(out=usel[:, b, :], in0=wau[:, e, :], scalar=hot[0:H + 1, b, e:e + 1],
                                                             in1=base_row[:] if e == 0 else usel[:, b, :],
                                                             op0=ALU.mult, op1=ALU.add)
                    if e == E - 1:
                        ins.then_inc(s_sel, 1)
                    else:
                        link(ins)
                v.wait_ge(s_high, 1)
                nc.vector.tensor_tensor(dl[:], dsel[:], dh[:].bitcast(F32), ALU.subtract).then_inc(s_low, 1)
                v.wait_ge(s_high, 2)
                nc.vector.tensor_tensor(ul[:], usel[:], uh[:].bitcast(F32), ALU.subtract).then_inc(s_low, 1)
                for c in range(NC + 1):
                    if c < NC:
                        v.wait_ge(s_ah, c + 1)
                        after(v, s_op, c, 2)
                        nc.vector.tensor_tensor(al[0:H, c % 2], a_[:, c % 2], ah[0:H, c % 2].bitcast(F32),
                                                ALU.subtract).then_inc(s_al, 1)
                    if c:
                        d = c - 1
                        v.wait_ge(s_op, d + 1)
                        xv = x[:, d * TPC:(d + 1) * TPC, :]
                        nc.vector.tensor_tensor(xv, xv, op[:, d % 2], ALU.add).then_inc(s_x, 1)

            @block.sync
            def _(sp):
                for c in range(NC):
                    sp.wait_ge(s_x, c + 1)
                    sp.dma_start(out_v[:, c * TPC:(c + 1) * TPC, :], x[:, c * TPC:(c + 1) * TPC, :]).then_inc(s_out, 16)
                sp.wait_ge(s_out, 16 * NC)


def soft_attention(core, w):
    nc, x = core.nc, core.x
    H, E, L = 8, 128, w["ctxT"].shape[-1] // B
    HL = H * L
    HB = 4
    J = -(-(HL + 1) // P)
    SCALE = E ** -0.5
    with ExitStack() as ctx:
        ah, al = (core.sb(f"xa_a{q}", [P, KD, B, HL], F32R, ctx) for q in "hl")
        vw = core.sb("xa_vw", [P, B, J, D], ctx=ctx)
        with ExitStack() as inner:
            ctxT = core.sb("xa_ctxT", [P, KD, B * L], ctx=inner)
            wk, wv = (core.sb(f"xa_{q}", [P, KD, H, E], ctx=inner) for q in ("wk", "wv"))
            wqT, wproj = (core.sb(f"xa_{q}", [P, H, D], ctx=inner) for q in ("wqT", "wproj"))
            kvT = core.sb("xa_kvT", [P, 2, H, B * L], ctx=inner)
            row_stats(core, "xa", loads=[(ctxT[:], w["ctxT"]), (wk[:], w["Wk"]), (wqT[:], w["WqT"]), (wv[:], w["Wv"]),
                                         (wproj[:], w["Wproj"])], zeros=[vw[:]])
            vws = core.sb("xa_vws", [L, 2, B, D], ctx=inner)
            kv = core.ps("xa_kv", [P, 2, 512], inner)
            ap = core.ps("xa_ap", [P, 2, 512], inner)
            vp = core.ps("xa_vp", [P, 2, 2, 256], inner)
            s_kv, s_kvc, s_ap, s_ah, s_al, s_vp, s_vs, s_pack, s_row = (
                core.sem(f"xa_{q}") for q in ("kv", "kvcopy", "ap", "ahigh", "alow", "vp", "vs", "pack", "biasrow"))
            parts = []
            for hd in range(H):
                k0 = 0
                while k0 < L:
                    r = hd * L + k0
                    m = min(L - k0, P - r % P)
                    parts.append((hd, k0, m, r // P, r % P))
                    k0 += m
            s_packs = (s_pack, core.sem("xa_pack_odd"))
            sent = [sum(1 for q in parts if q[0] <= hd and q[0] % 2 == hd % 2) for hd in range(H)]
            with nc.Block() as block:
                @block.tensor
                def _(pe):
                    for m in range(2 * H):
                        after(pe, s_kvc, m, 2)
                        for k in range(KD):
                            ins = nc.tensor.matmul(kv[:, m % 2, 0:B * L], (wk, wv)[m // H][:, k, m % H, :], ctxT[:, k, :],
                                                   start=(k == 0), stop=(k == KD - 1))
                        ins.then_inc(s_kv, 1)
                    for m in range(2 * H):
                        after(pe, s_al, m, 2)
                        pe.wait_ge(s_kvc, m // 2 + 1)
                        nc.tensor.matmul(ap[:, m % 2, 0:B * L], wqT[:, m // 2, (m % 2) * P:(m % 2 + 1) * P], kvT[:, 0, m // 2, :],
                                         start=True, stop=True).then_inc(s_ap, 1)
                    pe.wait_ge(s_kvc, 2 * H)
                    for m in range(2 * H):
                        after(pe, s_vs, m, 2)
                        for q in range(2):
                            b = (m % 2) * 2 + q
                            ins = nc.tensor.matmul(vp[0:L, m % 2, q, :], kvT[:, 1, m // 2, b * L:(b + 1) * L], wproj[:, m // 2, :],
                                                   start=True, stop=True)
                        ins.then_inc(s_vp, 1)

                @block.scalar
                def _(a):
                    for m in range(2 * H):
                        a.wait_ge(s_kv, m + 1)
                        nc.scalar.activation(kvT[:, m // H, m % H, :], kv[:, m % 2, 0:B * L], ACT.Copy).then_inc(s_kvc, 1)
                    for m in range(2 * H):
                        a.wait_ge(s_ap, m + 1)
                        nc.scalar.activation(ah[:, m % 2, :, (m // 2) * L:(m // 2 + 1) * L],
                                             ap[:, m % 2, 0:B * L].rearrange("p (b l) -> p b l", b=B), ACT.Copy).then_inc(s_ah, 1)

                @block.vector
                def _(v):
                    for m in range(2 * H):
                        v.wait_ge(s_ah, m + 1)
                        part = (slice(None), m % 2, slice(None), slice((m // 2) * L, (m // 2 + 1) * L))
                        nc.vector.tensor_tensor(al[part], ap[:, m % 2, 0:B * L].rearrange("p (b l) -> p b l", b=B),
                                                ah[part].bitcast(F32), ALU.subtract).then_inc(s_al, 1)
                    for m in range(2 * H):
                        v.wait_ge(s_vp, m + 1)
                        if m // 2 >= 2:
                            v.wait_ge(s_packs[m // 2 % 2], 16 * sent[m // 2 - 2])
                        nc.vector.tensor_copy(vws[:, m // 2 % 2, (m % 2) * 2:(m % 2) * 2 + 2, :], vp[0:L, m % 2]).then_inc(s_vs, 1)

                @block.sync
                def _(sp):
                    for b in range(B):
                        sp.dma_start(vw[HL % P:HL % P + 1, b, HL // P, :], w["b_proj"].rearrange("(o n) -> o n", o=1)).then_inc(s_row, 16)
                    for hd, k0, m, j, r in parts:
                        sp.wait_ge(s_vs, 2 * hd + 2)
                        sp.dma_start(vw[r:r + m, :, j, :], vws[k0:k0 + m, hd % 2, :, :]).then_inc(s_packs[hd % 2], 16)
                    for q in range(2):
                        sp.wait_ge(s_packs[q], 16 * sent[H - 2 + q])
                    sp.wait_ge(s_row, 16 * B)

        NS = 4
        e = core.sb("xa_e", [P, NS, HL], ctx=ctx)
        pn = core.sb("xa_pn", [P, NS, J * P], ctx=ctx)
        pt = core.sb("xa_pt", [P, 2, J, P], ctx=ctx)
        top, total, inv = (core.sb(f"xa_{q}", [P, NS, H], ctx=ctx) for q in ("top", "total", "inv"))
        sp_ = core.ps("xa_s", [P, 2, 2, 512], ctx)
        pp = core.ps("xa_p", [P, 2, 512], ctx)
        op = core.ps("xa_o", [P, 2, 512], ctx)
        norm = Norm(core, "xa", ctx, None)
        s_s, s_top, s_sub, s_exp, s_sum, s_inv, s_pn, s_pt, s_ptc, s_o, s_x, s_pad = (
            core.sem(f"xa_{q}") for q in ("scores", "top", "sub", "exp", "sum", "inv", "pn", "pt", "ptcopy", "o", "x", "pad"))

        def slot_of(c_odd, pos):
            return (5 * c_odd + pos) % 2

        def s_view(slot):
            return sp_[:, slot, :, 0:HB * L].rearrange("p g (h l) -> p g h l", l=L)

        tiles = [slot_of(u // TPC, (0, 1, 3, 4)[u % TPC]) for u in range(2 * TPC)]

        with nc.Block() as block:
            @block.tensor
            def _(pe):
                norm.turned = sp_[:, 1]
                norm.transpose(pe, 0, 0)

                def step(t, u, lag, c):
                    if lag == 0:
                        j, cs = u % TPC, u // TPC
                        if j == 0:
                            pe.wait_ge(norm.low, c + 1)
                        if j == 3:
                            if isinstance(c, int) and c == NC - 1:
                                pe.wait_ge(s_sub, 4 * c + 1)
                            else:
                                pe.wait_ge(norm.low, c + 2)
                        elif isinstance(c, int) and c == 0 and j < 2:
                            pass
                        elif j < 2:
                            pe.wait_ge(s_sub, t - 1)
                        else:
                            pe.wait_ge(s_sub, t)
                        for g in range(2):
                            for k in range(KD):
                                cols = slice(g * HB * L, (g + 1) * HB * L)
                                xs = [q[:, cs, k, j * P:(j + 1) * P] for q in (norm.xh, norm.xl)]
                                av = [q[:, k].rearrange("p b n -> p (b n)")[:, bass.ds((t - u) * (HL // 8) + g * HB * L, HB * L)]
                                      for q in (ah, al)]
                                ins = mm3(nc, sp_[:, tiles[u], g, 0:HB * L], xs, av, start=(k == 0), stop=(k == KD - 1))
                        ins.then_inc(s_s, 1)
                        if j == 1 and not (isinstance(c, int) and c == NC - 1):
                            pe.wait_ge(s_sub, t)
                            norm.turned = sp_[:, slot_of(cs, 2)]
                            norm.transpose(pe, c + 1, 1 - cs)
                    elif lag == 2:
                        pe.wait_ge(s_pn, t + 1)
                        after(pe, s_ptc, t, 1)
                        for j in range(J):
                            ins = nc.tensor.transpose(pp[:, j // 4, (j % 4) * P:(j % 4 + 1) * P],
                                                      pn[:, u % NS, j * P:(j + 1) * P], core.ident[:])
                        ins.then_inc(s_pt, 1)
                    else:
                        pe.wait_ge(s_ptc, t + 1)
                        after(pe, s_x, t, 2)
                        for j in range(J):
                            rhs = vw[:].rearrange("p b j n -> p (b j n)")[:, bass.ds((t - u) * (J * D // 8) + j * D, D)]
                            ins = nc.tensor.matmul(op[:, u % 2, 0:D], pt[:, u % 2, j, :], rhs, start=(j == 0), stop=(j == J - 1))
                        ins.then_inc(s_o, 1)
                pe.wait_ge(s_pad, 2)
                pipeline(pe, NT, 2 * TPC, [0, 2, 3], step, per=TPC, ahead=True)

            @block.scalar
            def _(a):
                norm.turned = sp_[:, 1]
                norm.take(a, 0, 0)

                def step(t, u, lag, c):
                    if lag == 0:
                        j, cs = u % TPC, u // TPC
                        a.wait_ge(s_sub, t + 1)
                        nc.scalar.activation(e[:, u % NS], e[:, u % NS], ACT.Exp, scale=SCALE).then_inc(s_exp, 1)
                        if j == 1 and not (isinstance(c, int) and c == NC - 1):
                            norm.turned = sp_[:, slot_of(cs, 2)]
                            if not (isinstance(c, int) and c == 0):
                                a.wait_ge(s_s, 4 * c)
                            norm.take(a, c + 1, 1 - cs)
                    else:
                        a.wait_ge(s_pt, t + 1)
                        after(a, s_o, t, 2)
                        nc.scalar.activation(pt[:, u % 2], pp[:].rearrange("p g n -> p (g n)")[:, 0:J * P], ACT.Copy).then_inc(s_ptc, 1)
                pipeline(a, NT, 2 * TPC, [0, 2], step, per=TPC, ahead=True)

            @block.gpsimd
            def _(pool):
                nc.gpsimd.memset(pn[:, :, HL:HL + 1], 1.0).then_inc(s_pad, 1)
                nc.gpsimd.memset(pn[:, :, HL + 1:], 0.0).then_inc(s_pad, 1)

                def step(t, u, lag):
                    pool.wait_ge(s_inv, t + 1)
                    after(pool, s_pt, t, NS)
                    nc.gpsimd.tensor_tensor(pn[:, u % NS, 0:HL].rearrange("p (h l) -> p h l", l=L),
                                            e[:, u % NS].rearrange("p (h l) -> p h l", l=L),
                                            inv[:, u % NS].unsqueeze(2).to_broadcast([P, H, L]), ALU.mult).then_inc(s_pn, 1)
                pipeline(pool, NT, NS, [0], step)

            @block.vector
            def _(v):
                norm.normalise(v, 0, 0)
                norm.turned = sp_[:, 1]
                norm.take_low(v, 0, 0)

                def step(t, u, lag, c):
                    j, cs = u % TPC, u // TPC
                    if lag == 0:
                        last = isinstance(c, int) and c == NC - 1
                        if j == 0 and not last:
                            norm.normalise(v, c + 1, 1 - cs)
                        v.wait_ge(s_s, t + 1)
                        after(v, s_sum, t, NS)
                        nc.vector.tensor_reduce(top[:, u % NS].rearrange("p (g h) -> p g h", h=HB), s_view(tiles[u]),
                                                AX_X, ALU.max).then_inc(s_top, 1)
                        v.wait_ge(s_top, t + 1)
                        after(v, s_pn, t, NS)
                        nc.vector.tensor_tensor(e[:, u % NS].rearrange("p (g h l) -> p g h l", h=HB, l=L), s_view(tiles[u]),
                                                top[:, u % NS].rearrange("p (g h) -> p g h", h=HB).unsqueeze(3).to_broadcast([P, 2, HB, L]),
                                                ALU.subtract).then_inc(s_sub, 1)
                        if j == 1 and not last:
                            norm.turned = sp_[:, slot_of(cs, 2)]
                            norm.take_low(v, c + 1, 1 - cs)
                    elif lag == 1:
                        v.wait_ge(s_exp, t + 1)
                        nc.vector.tensor_reduce(total[:, u % NS], e[:, u % NS].rearrange("p (h l) -> p h l", l=L),
                                                AX_X, ALU.add).then_inc(s_sum, 1)
                        v.wait_ge(s_sum, t + 1)
                        nc.vector.reciprocal(inv[:, u % NS], total[:, u % NS]).then_inc(s_inv, 1)
                    else:
                        v.wait_ge(s_o, t + 1)
                        nc.vector.tensor_tensor(x[:, t, :], op[:, u % 2, 0:D], x[:, t, :], ALU.add).then_inc(s_x, 1)
                pipeline(v, NT, 2 * TPC, [0, 1, 4], step, per=TPC, ahead=True)


def gated_chunks(core, w):
    nc, x = core.nc, core.x
    NH, DH, SCAN = 16, 16, 64
    HB = P // DH
    NCK = S // SCAN
    SCALE = DH ** -0.5
    NW = NH * NCK
    PROJ = 8
    with ExitStack() as ctx:
        z = core.sb("gc_z", [P, KD, TOK], ctx=ctx)
        run_x = core.sb("gc_run_x", [P, KD, TOK], ctx=ctx)
        q = core.sb("gc_q", [P, TOK], ctx=ctx)
        lse = core.sb("gc_lse", [P, NT, NH], ctx=ctx)
        ck = core.sb("gc_ck", [P, KD, TOK // SCAN], ctx=ctx)
        woh, wol = (core.sb(f"gc_wo{n}", [P, KD, D], F32R, ctx) for n in "hl")
        head_row = core.sb("gc_head_row", [NH, KD, P], ctx=ctx)
        with ExitStack() as inner:
            wih, wil = (core.sb(f"gc_wi{n}", [P, KD, PROJ * P], F32R, inner) for n in "hl")
            gbias = core.sb("gc_gbias", [P, KD], ctx=inner)
            onep = core.sb("gc_onep", [P, NT], ctx=inner)
            mr = core.sb("gc_mr", [P, NT], ctx=inner)
            with ExitStack() as first:
                rawi = core.sb("gc_rawi", [P, KD, PROJ * P], ctx=first)
                rawo = core.sb("gc_rawo", [P, KD, D], ctx=first)
                rms = core.sb("gc_rms", [P, KD], ctx=first)
                row_stats(core, "gc", rms=True, weights=[(rawi[:], w["W_in"], wih[:], wil[:]), (rawo[:], w["W_out"], woh[:], wol[:])],
                          loads=[(rms[:], w["rms_weight"]), (gbias[:], w["gate_bias"]), (head_row[:], w["head_row"])], scaled=rms)
            g = core.sb("gc_g", [P, KD, CH], ctx=inner)
            vx, vk, rk = (core.sb(f"gc_{n}", [P, KD, CH], ctx=inner) for n in ("vx", "vk", "rk"))
            prod = core.sb("gc_prod", [P, 2, KD, CH], ctx=inner)
            turned = core.ps("gc_turned", [P, KD, CH], inner)
            gz = core.ps("gc_gz", [P, KD, CH], inner)
            xp = core.ps("gc_xp", [P, KD, CH], inner)
            kq = core.ps("gc_kq", [P, 2, CH], inner)
            norm = Norm(core, "gc", inner, turned)
            s_rows, s_xup, s_gp, s_kp, s_xp, s_qp, s_zp, s_g, s_z, s_q, s_vx, s_vk, s_cut, s_rx, s_rk, s_ck, s_prod, s_lse, s_lcopy = (
                core.sem(f"gc_{n}") for n in ("rows", "xup", "gp", "kp", "xp", "qp", "zp", "g", "z", "q", "vx", "vk", "cut",
                                              "rx", "rk", "ck", "prod", "lse", "lcopy"))

            def cols(c):
                return bass.ds(c * CH, CH)

            with nc.Block() as block:
                @block.tensor
                def _(pe):
                    def block_of(out, m, cs):
                        for k in range(KD):
                            ins = mm3(nc, out, [v[:, k, m * P:(m + 1) * P] for v in (wih, wil)],
                                      [v[:, cs, k] for v in (norm.xh, norm.xl)], start=(k == 0), stop=(k == KD - 1))
                        return ins

                    def step(c, u, lag):
                        if lag == 0:
                            after(pe, norm.low, c, 1)
                            after(pe, s_lcopy, c, 3)
                            norm.transpose(pe, c, u)
                        elif lag == 1:
                            pe.wait_ge(norm.low, c + 1)
                            after(pe, s_z, c, 1)
                            block_of(gz[:, 0, :], 4, u)
                            block_of(gz[:, 1, :], 5, u).then_inc(s_gp, 1)
                            after(pe, s_vk, c, 1)
                            block_of(kq[:, 0, :], 7, u).then_inc(s_kp, 1)
                            after(pe, s_vx, c, 1)
                            block_of(xp[:, 0, :], 2, u)
                            block_of(xp[:, 1, :], 3, u).then_inc(s_xp, 1)
                            after(pe, s_q, c, 1)
                            block_of(kq[:, 1, :], 6, u).then_inc(s_qp, 1)
                            pe.wait_ge(s_g, c + 1)
                            block_of(gz[:, 0, :], 0, u)
                            block_of(gz[:, 1, :], 1, u).then_inc(s_zp, 1)
                        else:
                            pe.wait_ge(s_prod, c + 1)
                            after(pe, s_lcopy, c, 1)
                            if isinstance(c, int):
                                pe.wait_ge(norm.low, min(c + 3, NC))
                            else:
                                pe.wait_ge(norm.low, c + 3)
                            for j in range(TPC):
                                for k in range(KD):
                                    ins = nc.tensor.matmul(turned[:, 0, j * NH + k * HB:j * NH + (k + 1) * HB],
                                                           prod[:, u, k, j * P:(j + 1) * P], core.head_of[:], start=True, stop=True)
                            ins.then_inc(s_lse, 1)
                    pipeline(pe, NC, 2, [0, 1, 2], step)

                @block.scalar
                def _(a):
                    def step(c, u, lag):
                        if lag == 0:
                            after(a, s_zp, c, 2)
                            norm.take(a, c, u)
                        else:
                            a.wait_ge(s_gp, c + 1)
                            after(a, s_rk, c, 1)
                            after(a, s_rx, c, 1)
                            for k in range(KD):
                                ins = nc.scalar.activation(g[:, k], gz[:, k, :], ACT.Sigmoid, bias=gbias[:, k:k + 1])
                            ins.then_inc(s_g, 1)
                            a.wait_ge(s_qp, c + 1)
                            nc.scalar.activation(q[:, cols(c)], kq[:, 1, :], ACT.Copy).then_inc(s_q, 1)
                            a.wait_ge(s_zp, c + 1)
                            nc.scalar.activation(z[:, :, cols(c)], gz[:], ACT.Sigmoid).then_inc(s_z, 1)
                    pipeline(a, NC, 2, [0, 1], step)

                @block.gpsimd
                def _(pool):
                    def step(c, u, lag):
                        pool.wait_ge(s_rk, c + 1)
                        pool.wait_ge(s_q, c + 1)
                        after(pool, s_lse, c, 2)
                        nc.gpsimd.tensor_tensor(prod[:, u], rk[:], q[:, cols(c)].unsqueeze(1).to_broadcast([P, KD, CH]),
                                                ALU.mult).then_inc(s_prod, 1)
                    pipeline(pool, NC, 2, [0], step)

                @block.vector
                def _(v):
                    nc.vector.tensor_scalar(onep[:], core.rstd_ln[:], 1.0, None, ALU.add).then_inc(s_rows, 1)
                    nc.vector.scalar_tensor_tensor(out=mr[:], in0=core.mean[:], scalar=-1.0, in1=core.rstd_ln[:],
                                                   op0=ALU.mult, op1=ALU.mult).then_inc(s_rows, 1)
                    v.wait_ge(s_rows, 2)

                    def step(c, u, lag):
                        if lag == 0:
                            norm.normalise(v, c, u)
                            v.wait_ge(norm.normed, c + 1)
                            for j in range(TPC):
                                t = c * TPC + j
                                nc.vector.tensor_scalar(x[:, t, :], x[:, t, :], onep[:, bass.ds(t, 1)], mr[:, bass.ds(t, 1)],
                                                        ALU.mult, ALU.add).then_inc(s_xup, 1)
                            norm.take_low(v, c, u)
                        elif lag == 1:
                            v.wait_ge(s_g, c + 1)
                            v.wait_ge(s_kp, c + 1)
                            after(v, s_rk, c, 1)
                            after(v, s_rx, c, 1)
                            nc.vector.scalar_tensor_tensor(out=vk[:], in0=g[:], scalar=1.0,
                                                           in1=kq[:, 0, :].unsqueeze(1).to_broadcast([P, KD, CH]),
                                                           op0=ALU.subtract, op1=ALU.mult).then_inc(s_vk, 1)
                            v.wait_ge(s_xp, c + 1)
                            nc.vector.scalar_tensor_tensor(out=vx[:], in0=g[:], scalar=1.0, in1=xp[:],
                                                           op0=ALU.subtract, op1=ALU.mult).then_inc(s_vx, 1)
                            v.wait_ge(s_vk, c + 1)
                            v.wait_ge(s_vx, c + 1)
                            nc.vector.memset(g[:].rearrange("p k (n s) -> p k n s", s=SCAN)[:, :, :, 0:1], 0.0).then_inc(s_cut, 1)
                            v.wait_ge(s_cut, c + 1)
                            after(v, s_prod, c, 1)
                            after(v, s_ck, c, 1)
                            nc.vector.tensor_tensor_scan(rk[:].rearrange("p k n -> p (k n)"), g[:].rearrange("p k n -> p (k n)"),
                                                         vk[:].rearrange("p k n -> p (k n)"), 0.0, ALU.mult, ALU.subtract).then_inc(s_rk, 1)
                            for k in range(KD):
                                ins = nc.vector.tensor_tensor_scan(run_x[:, k, cols(c)], g[:, k], vx[:, k], 0.0, ALU.mult, ALU.subtract)
                            ins.then_inc(s_rx, 1)
                            v.wait_ge(s_rk, c + 1)
                            nc.vector.tensor_copy(ck[:, :, bass.ds(c * (CH // SCAN), CH // SCAN)],
                                                  rk[:].rearrange("p k (n s) -> p k n s", s=SCAN)[:, :, :, 0]).then_inc(s_ck, 1)
                        else:
                            v.wait_ge(s_lse, c + 1)
                            nc.vector.tensor_copy(lse[:, bass.ds(c * TPC, TPC), :],
                                                  turned[:, 0, 0:TPC * NH].rearrange("p (j h) -> p j h", h=NH)).then_inc(s_lcopy, 1)
                    pipeline(v, NC, 2, [0, 1, 2], step)

        kb = core.sb("gc_kb", [P, B, KD, HB * NCK], ctx=ctx)
        xb = core.sb("gc_xb", [P, B, KD, P], ctx=ctx)
        maskb = core.sb("gc_maskb", [P, S // P, NCK], ctx=ctx)
        with ExitStack() as inner:
            xpre = core.sb("gc_xpre", [P, B, KD, P], ctx=inner)
            bp = core.ps("gc_bp", [P, B * KD, P], inner)
            s_kb, s_xpre, s_bp, s_xb, s_mask = (core.sem(f"gc_{n}") for n in ("kb", "xpre", "bp", "xb", "mask"))
            with nc.Block() as block:
                @block.vector
                def _(v):
                    heads = core.head_of[:].unsqueeze(2).to_broadcast([P, HB, NCK])
                    for b in range(B):
                        for k in range(KD):
                            first_rows = run_x[:, k, b * S:(b + 1) * S].rearrange("p (n s) -> p n s", s=SCAN)[:, :, 0]
                            nc.vector.tensor_tensor(xpre[:, b, k].rearrange("p (h n) -> p h n", h=HB),
                                                    first_rows.unsqueeze(1).to_broadcast([P, HB, NCK]), heads, ALU.mult).then_inc(s_xpre, 1)
                    for b in range(B):
                        for k in range(KD):
                            nc.vector.tensor_tensor(kb[:, b, k].rearrange("p (h n) -> p h n", h=HB),
                                                    ck[:, k, b * NCK:(b + 1) * NCK].unsqueeze(1).to_broadcast([P, HB, NCK]),
                                                    heads, ALU.mult).then_inc(s_kb, 1)
                    v.wait_ge(s_kb, B * KD)

                @block.tensor
                def _(pe):
                    for m in range(B * KD):
                        pe.wait_ge(s_xpre, m + 1)
                        ins = nc.tensor.transpose(bp[:, m, :], xpre[:, m // KD, m % KD, :], core.ident[:])
                    ins.then_inc(s_bp, 1)

                @block.scalar
                def _(a):
                    a.wait_ge(s_bp, 1)
                    nc.scalar.activation(xb[:].rearrange("p b k n -> p (b k) n"), bp[:], ACT.Copy).then_inc(s_xb, 1)
                    a.wait_ge(s_xb, 1)

                @block.gpsimd
                def _(pool):
                    nc.gpsimd.memset(maskb[:], 0.0).then_inc(s_mask, 1)
                    pool.wait_ge(s_mask, 1)
                    for half in range(P // SCAN):
                        rows = slice(half * SCAN, (half + 1) * SCAN)
                        nc.gpsimd.affine_select(out=maskb[rows], in_=maskb[rows], compare_op=ALU.is_gt, fill=-1e30, base=half,
                                                pattern=[[P // SCAN, S // P], [-1, NCK]], channel_multiplier=0).then_inc(s_mask, 1)
                    pool.wait_ge(s_mask, 3)

        qs = core.sb("gc_qs", [P, 2, CH], ctx=ctx)
        wt = core.sb("gc_wt", [P, 2, TPC, NW + NH], ctx=ctx)
        wn = core.sb("gc_wn", [P, 2, TPC, NW + NH], ctx=ctx)
        top, total, inv = (core.sb(f"gc_{n}", [P, 2, TPC, NH], ctx=ctx) for n in ("top", "total", "inv"))
        wts = core.sb("gc_wts", [P, KD, CH], ctx=ctx)
        wis = core.sb("gc_wis", [NH, CH], ctx=ctx)
        xcur = core.sb("gc_xcur", [P, KD, P], ctx=ctx)
        y1, y2 = (core.sb(f"gc_{n}", [P, KD, CH], ctx=ctx) for n in ("y1", "y2"))
        yh, yl = (core.sb(f"gc_{n}", [P, 2, KD, CH], F32R, ctx) for n in ("yh", "yl"))
        sr = core.ps("gc_sr", [P, 2, CH], ctx)
        wo_ = core.ps("gc_wo_", [P, 2, CH], ctx)
        wip = core.ps("gc_wip", [NH, CH], ctx)
        op = core.ps("gc_op", [P, KD, CH], ctx)
        (s_qs, s_s, s_mk, s_m1, s_top, s_sub, s_exp, s_t1, s_sum, s_inv, s_wn, s_wnl, s_wt, s_wtc, s_xc, s_r, s_o, s_y1, s_y2,
         s_y, s_yh, s_yl, s_out, s_x) = (core.sem(f"gb_{n}") for n in (
             "qs", "s", "mask", "m1", "top", "sub", "exp", "t1", "sum", "inv", "wn", "wnl", "wt", "wtc", "xcur", "r", "o",
             "y1", "y2", "y", "yh", "yl", "out", "x"))

        def heads(v, n=NCK):
            return v.rearrange("p j (h n) -> p j h n", n=n)

        with nc.Block() as block:
            @block.gpsimd
            def _(pool):
                def step(c, u, lag):
                    if lag[1] == "query":
                        after(pool, s_s, c, 2)
                        nc.gpsimd.tensor_copy(qs[:, u], q[:, bass.ds(c * CH, CH)]).then_inc(s_qs, 1)
                    else:
                        pool.wait_ge(s_inv, c + 1)
                        after(pool, s_wt, c, 2)
                        nc.gpsimd.tensor_tensor(heads(wn[:, u, :, 0:NW]), heads(wt[:, u, :, 0:NW]),
                                                inv[:, u].unsqueeze(3).to_broadcast([P, TPC, NH, NCK]), ALU.mult).then_inc(s_wn, 1)
                pipeline(pool, NC, 2, [(0, "query"), (1, "divide")], step)

            @block.tensor
            def _(pe):
                def step(c, u, lag, b):
                    if lag == 0:
                        pe.wait_ge(s_qs, c + 1)
                        after(pe, s_mk, c, 1)
                        for j in range(TPC):
                            ins = nc.tensor.matmul(sr[:, j // 2, (j % 2) * NW:(j % 2 + 1) * NW], qs[:, u, j * P:(j + 1) * P],
                                                   kb[:].rearrange("p b k n -> p (b k n)")[:, bass.ds(b * NW, NW)], start=True, stop=True)
                        ins.then_inc(s_s, 1)
                    elif lag == 1:
                        pe.wait_ge(s_wn, c + 1)
                        pe.wait_ge(s_wnl, c + 1)
                        after(pe, s_wtc, c, 1)
                        after(pe, s_x, c, 1)
                        for j in range(TPC):
                            for k in range(KD):
                                nc.tensor.transpose(wo_[:, k, j * P:(j + 1) * P], wn[:, u, j, k * P:(k + 1) * P], core.ident[:])
                            ins = nc.tensor.transpose(wip[:, j * P:(j + 1) * P], wn[:, u, j, NW:NW + NH], core.ident[:])
                        ins.then_inc(s_wt, 1)
                        pe.wait_ge(s_wtc, c + 1)
                        for k in range(KD):
                            ins = nc.tensor.matmul(wo_[:, k, :], head_row[:, k, :], wis[:], start=True, stop=True)
                        ins.then_inc(s_r, 1)
                        after(pe, s_y2, c, 1)
                        pe.wait_ge(s_xc, b + 1)
                        for k in range(KD):
                            ins = nc.tensor.matmul(op[:, k, :], xcur[:, k, :], wts[:, k, :], start=True, stop=True)
                        ins.then_inc(s_o, 1)
                        pe.wait_ge(s_yl, c + 1)
                        for j in range(TPC):
                            for k in range(KD):
                                ins = mm3(nc, wo_[:, j // 2, (j % 2) * D:(j % 2 + 1) * D], [v[:, u, k, j * P:(j + 1) * P] for v in (yh, yl)],
                                          (woh[:, k, :], wol[:, k, :]), start=(k == 0), stop=(k == KD - 1))
                        ins.then_inc(s_out, 1)
                pipeline(pe, NC, 2, [0, 1], step, per=2)

            @block.scalar
            def _(a):
                def step(c, u, lag, b):
                    if lag == 0:
                        a.wait_ge(s_sub, 2 * c + 2)
                        nc.scalar.activation(wt[:, u], wt[:, u], ACT.Exp, scale=SCALE).then_inc(s_exp, 1)
                    else:
                        if u == 0:
                            after(a, s_o, c, 1)
                            nc.scalar.activation(xcur[:].rearrange("p k n -> p (k n)"),
                                                 xb[:].rearrange("p b k n -> p (b k n)")[:, bass.ds(b * (KD * P), KD * P)],
                                                 ACT.Copy).then_inc(s_xc, 1)
                        a.wait_ge(s_wt, c + 1)
                        after(a, s_o, c, 1)
                        nc.scalar.activation(wis[:], wip[:], ACT.Copy)
                        nc.scalar.activation(wts[:], wo_[:], ACT.Copy).then_inc(s_wtc, 1)
                        a.wait_ge(s_y, c + 1)
                        after(a, s_out, c, 2)
                        nc.scalar.activation(yh[:, u], y2[:], ACT.Copy).then_inc(s_yh, 1)
                pipeline(a, NC, 2, [0, 1], step, per=2)

            @block.vector
            def _(v):
                def step(c, u, lag):
                    cols = bass.ds(c * CH, CH)
                    if lag[1] == "scores":
                        l = lse[:, bass.ds(c * TPC, TPC), :]
                        v.wait_ge(s_s, c + 1)
                        after(v, s_wn, c, 2)
                        after(v, s_wnl, c, 2)
                        for half in range(2):
                            tiles = slice(half * 2, half * 2 + 2)
                            m = maskb[:, u * TPC + half * 2:u * TPC + half * 2 + 2, :].unsqueeze(2).to_broadcast([P, 2, NH, NCK])
                            ins = nc.vector.tensor_tensor(heads(wt[:, u, tiles, 0:NW]),
                                                          heads(sr[:, half, :].rearrange("p (j n) -> p j n", j=2)), m, ALU.add)
                        ins.then_inc(s_mk, 1)
                        v.wait_ge(s_mk, c + 1)
                        nc.vector.tensor_reduce(top[:, u], heads(wt[:, u, :, 0:NW]), AX_X, ALU.max).then_inc(s_m1, 1)
                        v.wait_ge(s_m1, c + 1)
                        nc.vector.tensor_tensor(top[:, u], top[:, u], l, ALU.max).then_inc(s_top, 1)
                        v.wait_ge(s_top, c + 1)
                        nc.vector.tensor_tensor(heads(wt[:, u, :, 0:NW]), heads(wt[:, u, :, 0:NW]),
                                                top[:, u].unsqueeze(3).to_broadcast([P, TPC, NH, NCK]), ALU.subtract).then_inc(s_sub, 1)
                        nc.vector.tensor_tensor(wt[:, u, :, NW:], l, top[:, u], ALU.subtract).then_inc(s_sub, 1)
                    elif lag[1] == "sum":
                        v.wait_ge(s_exp, c + 1)
                        nc.vector.tensor_reduce(total[:, u], heads(wt[:, u, :, 0:NW]), AX_X, ALU.add).then_inc(s_t1, 1)
                        v.wait_ge(s_t1, c + 1)
                        nc.vector.tensor_tensor(total[:, u], total[:, u], wt[:, u, :, NW:], ALU.add).then_inc(s_sum, 1)
                        v.wait_ge(s_sum, c + 1)
                        nc.vector.reciprocal(inv[:, u], total[:, u]).then_inc(s_inv, 1)
                        v.wait_ge(s_inv, c + 1)
                        after(v, s_wt, c, 2)
                        nc.vector.tensor_tensor(wn[:, u, :, NW:], wt[:, u, :, NW:], inv[:, u], ALU.mult).then_inc(s_wnl, 1)
                    else:
                        v.wait_ge(s_r, c + 1)
                        nc.vector.tensor_tensor(y1[:], wo_[:], run_x[:, :, cols], ALU.mult).then_inc(s_y1, 1)
                        v.wait_ge(s_o, c + 1)
                        v.wait_ge(s_y1, c + 1)
                        nc.vector.tensor_tensor(y1[:], op[:], y1[:], ALU.add).then_inc(s_y2, 1)
                        v.wait_ge(s_y2, c + 1)
                        after(v, s_yl, c, 1)
                        nc.vector.tensor_tensor(y2[:], y1[:], z[:, :, cols], ALU.mult).then_inc(s_y, 1)
                        v.wait_ge(s_yh, c + 1)
                        nc.vector.tensor_tensor(yl[:, u], y2[:], yh[:, u].bitcast(F32), ALU.subtract).then_inc(s_yl, 1)
                        v.wait_ge(s_out, c + 1)
                        xv = x[:, bass.ds(c * TPC, TPC), :]
                        nc.vector.tensor_tensor(xv, wo_[:].rearrange("p g (j n) -> p (g j) n", n=D), xv, ALU.add).then_inc(s_x, 1)
                pipeline(v, NC, 2, [(0, "scores"), (0, "sum"), (1, "rest")], step)


def linear_attention(core, w):
    nc, x = core.nc, core.x
    NH, DH = 16, 16
    TPS = S // P
    FILLS = 4
    with ExitStack() as ctx:
        wqk = [core.sb(f"la_wqk{n}", [P, KD, 2 * D], F32R, ctx) for n in "hl"]
        wkv = [core.sb(f"la_wkv{n}", [P, KD, 2 * D], F32R, ctx) for n in "hl"]
        wn = [core.sb(f"la_wn{n}", [P, KD, NH], F32R, ctx) for n in "hl"]
        wo = core.sb("la_wo", [P, KD, D], ctx=ctx)
        bq = core.sb("la_bq", [P, KD], ctx=ctx)
        bqm = core.sb("la_bqm", [P, 2, KD], ctx=ctx)
        bk = core.sb("la_bk", [P, KD], ctx=ctx)
        bkv = core.sb("la_bkv", [P, 2 * D], ctx=ctx)
        bn = core.sb("la_bn", [P, NH], ctx=ctx)
        bo = core.sb("la_bo", [P, D], ctx=ctx)
        par = core.sb("la_par", [P, 2], ctx=ctx)
        tri = core.sb("la_tri", [P, P], ctx=ctx)
        same = core.sb("la_same", [P, P], ctx=ctx)
        with ExitStack() as inner:
            rqk, rkv = (core.sb(f"la_raw{n}", [P, KD, 2 * D], ctx=inner) for n in ("qk", "kv"))
            rn_ = core.sb("la_rawn", [P, KD, NH], ctx=inner)
            row_stats(core, "la", weights=[(rqk[:], w["Wqk"], wqk[0][:], wqk[1][:]), (rkv[:], w["Wkv"], wkv[0][:], wkv[1][:]),
                                           (rn_[:], w["Wn"], wn[0][:], wn[1][:])],
                      loads=[(wo[:], w["Wo"]), (bq[:], w["bq"]), (bk[:], w["bk"]), (bkv[:], w["bkv"].partition_broadcast(P)),
                             (bn[:], w["bn"].partition_broadcast(P)), (bo[:], w["bo"].partition_broadcast(P)), (par[:], w["parity"])],
                      ones=[tri[:]])
        NQ = 3
        qT = core.sb("la_qT", [P, 2, KD, NQ, CH], ctx=ctx)
        kT = core.sb("la_kT", [P, 2, KD, CH], ctx=ctx)
        kv = core.sb("la_kv", [P, 2, TPC, 2 * D], ctx=ctx)
        nb = core.sb("la_nb", [P, 2, TPC, NH], ctx=ctx)
        rn = core.sb("la_rn", [P, 2, TPC, NH], ctx=ctx)
        am = core.sb("la_am", [P, 2, FILLS, CH], ctx=ctx)
        sraw = core.sb("la_sraw", [P, KD, P], ctx=ctx)
        sblk = core.sb("la_sblk", [P, KD, P], ctx=ctx)
        cn = core.sb("la_cn", [P, 2, D], ctx=ctx)
        yT = core.sb("la_yT", [P, 2, KD, P], ctx=ctx)
        proj = core.ps("la_proj", [P, 2, CH], ctx)
        sc = core.ps("la_sc", [P, 2, CH], ctx)
        cp = core.ps("la_cp", [P, 2, CH], ctx)
        st = core.ps("la_st", [P, CH], ctx)
        yo = core.ps("la_yo", [P, CH], ctx)
        norm = Norm(core, "la", ctx, proj)
        (s_made, s_qk, s_qke, s_kv, s_kvb, s_n, s_nb, s_rn, s_sc, s_am, s_c, s_st, s_sr, s_sb, s_cn, s_yT, s_yTc, s_o, s_x, s_xb) = (
            core.sem(f"la_{n}") for n in ("made", "qk", "qkcopy", "kv", "kvbias", "n", "nbias", "rn", "sc", "am", "c", "st", "sraw",
                                          "sblk", "cn", "yT", "yTcopy", "o", "x", "xbias"))

        with nc.Block() as block:
            @block.tensor
            def _(pe):
                def prepare(part, c, s):
                    xs = (norm.xh, norm.xl)
                    if part == 0:
                        after(pe, s_kvb, c, 1, TPC)
                        after(pe, s_nb, c, 1)
                        norm.transpose(pe, c, s)
                    elif part == 1:
                        pe.wait_ge(norm.low, c + 1)
                        for m in range(4):
                            if m >= 2:
                                pe.wait_ge(s_qke, 4 * c + m - 1)
                            col = (m % 2) * D + (m // 2) * P
                            for k in range(KD):
                                ins = mm3(nc, proj[:, m % 2, :], [v[:, k, col:col + P] for v in wqk],
                                          [v[:, s, k] for v in xs], start=(k == 0), stop=(k == KD - 1))
                            ins.then_inc(s_qk, 1)
                    else:
                        for j in (0, 1) if part == 2 else (2, 3):
                            if j < 2:
                                pe.wait_ge(s_qke, 4 * c + j + 3)
                            else:
                                pe.wait_ge(s_kvb, 4 * c + j - 1)
                            for k in range(KD):
                                ins = mm3(nc, proj[:, j % 2, :], [v[:, s, k, j * P:(j + 1) * P] for v in xs],
                                          [v[:, k] for v in wkv], start=(k == 0), stop=(k == KD - 1))
                            ins.then_inc(s_kv, 1)
                        if part == 3:
                            pe.wait_ge(s_kvb, 4 * c + 3)
                            for j in range(TPC):
                                for k in range(KD):
                                    ins = mm3(nc, proj[:, 0, j * NH:(j + 1) * NH], [v[:, s, k, j * P:(j + 1) * P] for v in xs],
                                              [v[:, k] for v in wn], start=(k == 0), stop=(k == KD - 1))
                            ins.then_inc(s_n, 1)

                def step(t, u, lag, c):
                    j, cs = u % TPC, u // TPC
                    tile = slice(j * P, (j + 1) * P)
                    if lag[1] == "scores":
                        if j == 0:
                            pe.wait_ge(s_qke, 4 * c + 4)
                        for f in range(FILLS):
                            if isinstance(t, int) and 4 * t + f < 2:
                                pass
                            else:
                                pe.wait_ge(s_am, 4 * t + f - 1)
                            r = slice(32 * f, 32 * f + 32)
                            for k in range(KD):
                                ins = nc.tensor.matmul(sc[:, f % 2, k * 256:(k + 1) * 256], kT[r, cs, k, tile],
                                                       qT[r, cs, k, 1:3, tile], start=True, stop=True)
                            ins.then_inc(s_sc, 1)
                    elif lag[1] == "turn":
                        pe.wait_ge(s_cn, t + 1)
                        after(pe, s_x, t, 1)
                        for k in range(KD):
                            ins = nc.tensor.transpose(yo[:, k * P:(k + 1) * P], cn[:, u % 2, k * P:(k + 1) * P], core.ident[:])
                        ins.then_inc(s_yT, 1)
                    elif lag[1] == "prepare":
                        if not (isinstance(c, int) and c == NC - 1):
                            prepare(j, c + 1, 1 - cs)
                    elif lag[1] == "context":
                        if j == 0:
                            pe.wait_ge(s_kvb, 4 * c + 4)
                        after(pe, s_cn, t, 2)
                        if u:
                            pe.wait_ge(s_sb, t)
                            for k in range(KD):
                                nc.tensor.matmul(cp[:, u % 2, k * P:(k + 1) * P], qT[:, cs, k, 0, tile], sblk[:, k, :],
                                                 start=(k == 0), stop=False, skip_group_check=True)
                        for f in range(FILLS):
                            pe.wait_ge(s_am, 4 * t + f + 1)
                            for q in range(4):
                                h = 8 * (q // 2) + 2 * f + q % 2
                                ins = nc.tensor.matmul(cp[:, u % 2, h * DH:(h + 1) * DH], am[:, u % 2, f, q * P:(q + 1) * P],
                                                       kv[:, cs, j, D + h * DH:D + (h + 1) * DH], start=(u == 0 and h == 0),
                                                       stop=(h == NH - 1), skip_group_check=True)
                        ins.then_inc(s_c, 1)
                        after(pe, s_sr, t, 1)
                        for k in range(KD):
                            ins = nc.tensor.matmul(st[:, k * P:(k + 1) * P], kv[:, cs, j, k * P:(k + 1) * P],
                                                   kv[:, cs, j, D + k * P:D + (k + 1) * P], start=True, stop=True)
                        ins.then_inc(s_st, 1)
                    else:
                        pe.wait_ge(s_yTc, t + 1)
                        for k in range(KD):
                            ins = nc.tensor.matmul(yo[:, 0:D], yT[:, u % 2, k, :], wo[:, k, :], start=(k == 0), stop=(k == KD - 1))
                        ins.then_inc(s_o, 1)

                for part in range(4):
                    prepare(part, 0, 0)
                pipeline(pe, NT, TPS, [(0, "scores"), (1, "turn"), (0, "prepare"), (0, "context"), (1, "out")], step, per=TPC, ahead=True)

            @block.scalar
            def _(a):
                def prepare(part, c, s):
                    if part == 0:
                        after(a, s_n, c, 2)
                        norm.take(a, c, s)
                    elif part == 1:
                        after(a, s_st, c, 2, TPC)
                        for m in range(4):
                            a.wait_ge(s_qk, 4 * c + m + 1)
                            k = m // 2
                            if m % 2:
                                ins = nc.scalar.activation(kT[:, s, k], proj[:, 1, :], ACT.Identity, bias=bk[:, k:k + 1])
                            else:
                                nc.scalar.activation(qT[:, s, k, 0], proj[:, 0, :], ACT.Identity, bias=bq[:, k:k + 1])
                                for odd in range(2):
                                    ins = nc.scalar.activation(qT[:, s, k, 1 + odd], proj[:, 0, :], ACT.Identity,
                                                               bias=bqm[:, odd, k:k + 1], scale=par[:, odd:odd + 1])
                            ins.then_inc(s_qke, 1)
                    elif part == 3:
                        a.wait_ge(s_nb, c + 1)
                        after(a, s_cn, c, 2, TPC)
                        nc.scalar.activation(rn[:, s], nb[:, s], ACT.Exp, scale=-1.0).then_inc(s_rn, 1)

                def step(t, u, lag, c):
                    j, cs = u % TPC, u // TPC
                    if lag == 0:
                        if not (isinstance(c, int) and c == NC - 1):
                            prepare(j, c + 1, 1 - cs)
                    else:
                        a.wait_ge(s_yT, t + 1)
                        after(a, s_o, t, 2)
                        nc.scalar.activation(yT[:, u % 2].rearrange("p k n -> p (k n)"), yo[:, 0:D], ACT.Copy).then_inc(s_yTc, 1)
                a.wait_ge(s_made, 3)
                for part in range(4):
                    prepare(part, 0, 0)
                pipeline(a, NT, TPS, [1, 0], step, per=TPC, ahead=True)

            @block.gpsimd
            def _(pool):
                nc.gpsimd.affine_select(out=tri[:], in_=tri[:], compare_op=ALU.is_ge, fill=0.0, base=0,
                                        pattern=[[1, P]], channel_multiplier=-1).then_inc(s_made, 1)
                nc.gpsimd.tensor_copy(same[:].rearrange("p (h d) -> p h d", d=DH),
                                      core.head_of[:].unsqueeze(2).to_broadcast([P, P // DH, DH])).then_inc(s_made, 1)
                nc.gpsimd.tensor_tensor(bqm[:], par[:].unsqueeze(2).to_broadcast([P, 2, KD]),
                                        bq[:].unsqueeze(1).to_broadcast([P, 2, KD]), ALU.mult).then_inc(s_made, 1)
                pool.wait_ge(s_made, 3)

                def pstep(t, u, lag, c):
                    if lag == 0:
                        if u % TPC == 0:
                            pool.wait_ge(norm.normed, c + 1)
                        nc.gpsimd.tensor_tensor(x[:, t, :], x[:, t, :], bo[:], ALU.add).then_inc(s_xb, 1)
                    else:
                        pool.wait_ge(s_sr, t + 1)
                        pool.wait_ge(s_c, t + 1)
                        nc.gpsimd.tensor_tensor(sblk[:], sraw[:], same[:].unsqueeze(1).to_broadcast([P, KD, P]),
                                                ALU.mult).then_inc(s_sb, 1)
                pipeline(pool, NT, TPS, [0, 1], pstep, per=TPC)

            @block.vector
            def _(v):
                def prepare(part, c, s):
                    if part == 0:
                        norm.take_low(v, c, s)
                    elif part >= 2:
                        for j in (0, 1) if part == 2 else (2, 3):
                            v.wait_ge(s_kv, 4 * c + j + 1)
                            after(v, s_st, c, 2, TPC)
                            nc.vector.tensor_tensor(kv[:, s, j], proj[:, j % 2, :], bkv[:], ALU.add).then_inc(s_kvb, 1)
                        if part == 3:
                            v.wait_ge(s_n, c + 1)
                            after(v, s_rn, c, 2)
                            nc.vector.tensor_tensor(nb[:, s], proj[:, 0, 0:TPC * NH].rearrange("p (j h) -> p j h", h=NH),
                                                    bn[:].unsqueeze(1).to_broadcast([P, TPC, NH]), ALU.add).then_inc(s_nb, 1)

                def mask(t, u, f):
                    v.wait_ge(s_sc, 4 * t + f + 1)
                    if f == 0:
                        after(v, s_c, t, 2)
                    nc.vector.tensor_tensor(am[:, u % 2, f].rearrange("p (h n) -> p h n", n=P),
                                            sc[:, f % 2, :].rearrange("p (h n) -> p h n", n=P),
                                            tri[:].unsqueeze(1).to_broadcast([P, 4, P]), ALU.mult).then_inc(s_am, 1)

                def step(t, u, lag, c):
                    j, cs = u % TPC, u // TPC
                    last = isinstance(c, int) and c == NC - 1
                    if lag[1] == "mask01":
                        mask(t, u, 0)
                        mask(t, u, 1)
                        if j == 0 and not last:
                            norm.normalise(v, c + 1, 1 - cs)
                    elif lag[1] == "state":
                        v.wait_ge(s_st, t + 1)
                        after(v, s_sb, t, 1)
                        sp_ = st[:, 0:D].rearrange("p (k n) -> p k n", k=KD)
                        if u == 0:
                            nc.vector.tensor_copy(sraw[:], sp_).then_inc(s_sr, 1)
                        else:
                            nc.vector.tensor_tensor(sraw[:], sp_, sraw[:], ALU.add).then_inc(s_sr, 1)
                        v.wait_ge(s_c, t + 1)
                        if j == 0:
                            v.wait_ge(s_rn, c + 1)
                        after(v, s_yT, t, 2)
                        nc.vector.tensor_tensor(cn[:, u % 2].rearrange("p (h d) -> p h d", d=DH),
                                                cp[:, u % 2, 0:D].rearrange("p (h d) -> p h d", d=DH),
                                                rn[:, cs, j].unsqueeze(2).to_broadcast([P, NH, DH]), ALU.mult).then_inc(s_cn, 1)
                    elif lag[1] == "mask23":
                        mask(t, u, 2)
                        mask(t, u, 3)
                    elif lag[1] == "prepare":
                        if not last:
                            prepare(j, c + 1, 1 - cs)
                    else:
                        v.wait_ge(s_o, t + 1)
                        v.wait_ge(s_xb, t + 1)
                        nc.vector.tensor_tensor(x[:, t, :], yo[:, 0:D], x[:, t, :], ALU.add).then_inc(s_x, 1)
                norm.normalise(v, 0, 0)
                v.wait_ge(s_made, 3)
                for part in range(4):
                    prepare(part, 0, 0)
                pipeline(v, NT, TPS, [(0, "mask01"), (1, "state"), (0, "mask23"), (2, "add"), (0, "prepare")], step, per=TPC, ahead=True)


def lora_attention(core, w):
    nc, x = core.nc, core.x
    NH, DH, L, RANK = 16, 16, w["ctxT"].shape[-1] // B, 16
    HH = NH // 2
    HB = 4
    HL = HH * L
    J = -(-HL // P)
    VW = DH + 1
    VJ = 52
    SCALE = DH ** -0.5
    TPS = S // P
    with ExitStack() as ctx:
        wq = [core.sb(f"lo_wq{n}", [P, KD, D], F32R, ctx) for n in "hl"]
        wp = core.sb("lo_wp", [P, KD, D], ctx=ctx)
        kb = [core.sb(f"lo_kb{n}", [P, B, 2, HL], F32R, ctx) for n in "hl"]
        vp = core.sb("lo_vp", [P, B, 2 * J, VJ], ctx=ctx)
        bq = core.sb("lo_bq", [P, KD], ctx=ctx)
        bp = core.sb("lo_bp", [P, D], ctx=ctx)
        causal = core.sb("lo_causal", [P, HB, L], ctx=ctx)
        parts = []
        for h in range(NH):
            k0 = 0
            while k0 < L:
                r = h % HH * L + k0
                m = min(L - k0, P - r % P)
                parts.append((h, k0, m, h // HH * J + r // P, r % P))
                k0 += m
        heads_of = [sorted({q[0] for q in parts if q[3] == j}) for j in range(2 * J)]
        with ExitStack() as inner:
            ctxT = core.sb("lo_ctxT", [P, KD, B * L], ctx=inner)
            raw = core.sb("lo_raw", [P, KD, 4 * D], ctx=inner)
            aT = core.sb("lo_a", [RANK, 3, D], ctx=inner)
            bT = core.sb("lo_b", [RANK, 4 * D], ctx=inner)
            weff = core.sb("lo_weff", [P, KD, 4 * D], ctx=inner)
            bfk = core.sb("lo_bfk", [P, KD], ctx=inner)
            bfv = core.sb("lo_bfv", [L, D], ctx=inner)
            kT = core.sb("lo_kT", [P, KD, B * L], ctx=inner)
            kblk = core.sb("lo_kblk", [P, 2, HL], ctx=inner)
            v1 = core.sb("lo_v1", [L, B, NH, VW], ctx=inner)
            row_stats(core, "lo", loads=[(ctxT[:], w["ctxT"]), (raw[:], w["W"]), (aT[:], w["A"]), (bT[:], w["B"]), (bfk[:], w["bfk"]),
                                         (bfv[:], w["bfv"].partition_broadcast(L)), (bq[:], w["bq"]),
                                         (bp[:], w["bp"].partition_broadcast(P))],
                      zeros=[vp[:], causal[:]], ones=[v1[:]])
            lp = core.ps("lo_lp", [P, 2, 512], inner)
            kp = core.ps("lo_kp", [P, KD, 512], inner)
            vps = core.ps("lo_vps", [P, 2, 512], inner)
            s_lp, s_w, s_wh, s_wl, s_kp, s_kT, s_kb, s_kh, s_kl, s_vp, s_v, s_pack, s_causal = (
                core.sem(f"lo_{n}") for n in ("lp", "w", "wh", "wl", "kp", "kT", "kb", "kh", "kl", "vp", "v", "pack", "causal"))
            with nc.Block() as block:
                @block.tensor
                def _(pe):
                    for m in range(4 * KD):
                        part, k = m // KD, m % KD
                        after(pe, s_w, m, 2)
                        nc.tensor.matmul(lp[:, m % 2, 0:D], aT[:, (0, 1, 1, 2)[part], k * P:(k + 1) * P],
                                         bT[:, part * D:(part + 1) * D], start=True, stop=True).then_inc(s_lp, 1)
                    for g in range(KD):
                        pe.wait_ge(s_w, 2 * KD)
                        for k in range(KD):
                            ins = nc.tensor.matmul(kp[:, g, 0:B * L], weff[:, k, D + g * P:D + (g + 1) * P], ctxT[:, k, :],
                                                   start=(k == 0), stop=(k == KD - 1))
                        ins.then_inc(s_kp, 1)
                    pe.wait_ge(s_w, 3 * KD)
                    for b in range(B):
                        after(pe, s_v, b, 2)
                        for k in range(KD):
                            ins = nc.tensor.matmul(vps[0:L, b % 2, 0:D], ctxT[:, k, b * L:(b + 1) * L], weff[:, k, 2 * D:3 * D],
                                                   start=(k == 0), stop=(k == KD - 1))
                        ins.then_inc(s_vp, 1)

                @block.scalar
                def _(a):
                    for g in range(KD):
                        a.wait_ge(s_kp, g + 1)
                        nc.scalar.activation(kT[:, g], kp[:, g, 0:B * L], ACT.Identity, bias=bfk[:, g:g + 1]).then_inc(s_kT, 1)
                    a.wait_ge(s_w, 4 * KD)
                    nc.scalar.activation(wq[0][:], weff[:, :, 0:D], ACT.Copy).then_inc(s_wh, 1)
                    nc.scalar.activation(wp[:], weff[:, :, 3 * D:], ACT.Copy).then_inc(s_wh, 1)
                    for m in range(2 * B):
                        a.wait_ge(s_kb, m + 1)
                        nc.scalar.activation(kb[0][:, m // 2, m % 2], kblk[:, m % 2], ACT.Copy).then_inc(s_kh, 1)
                    a.wait_ge(s_wh, 2)

                @block.vector
                def _(v):
                    for m in range(4 * KD):
                        part, k = m // KD, m % KD
                        v.wait_ge(s_lp, m + 1)
                        cols = slice(part * D, (part + 1) * D)
                        nc.vector.scalar_tensor_tensor(out=weff[:, k, cols], in0=lp[:, m % 2, 0:D], scalar=1.0 / 16.0,
                                                       in1=raw[:, k, cols], op0=ALU.mult, op1=ALU.add).then_inc(s_w, 1)
                    for m in range(2 * B + 1):
                        if m < 2 * B:
                            b, g = m // 2, m % 2
                            v.wait_ge(s_kT, g + 1)
                            after(v, s_kl, m, 2)
                            nc.vector.tensor_tensor(kblk[:, g].rearrange("p (h l) -> p h l", l=L),
                                                    kT[:, g, b * L:(b + 1) * L].unsqueeze(1).to_broadcast([P, HH, L]),
                                                    core.head_of[:].unsqueeze(2).to_broadcast([P, HH, L]), ALU.mult).then_inc(s_kb, 1)
                        if m:
                            b, g = (m - 1) // 2, (m - 1) % 2
                            v.wait_ge(s_kh, m)
                            nc.vector.tensor_tensor(kb[1][:, b, g], kblk[:, g], kb[0][:, b, g].bitcast(F32),
                                                    ALU.subtract).then_inc(s_kl, 1)
                    v.wait_ge(s_wh, 1)
                    nc.vector.tensor_tensor(wq[1][:], weff[:, :, 0:D], wq[0][:].bitcast(F32), ALU.subtract).then_inc(s_wl, 1)
                    for b in range(B):
                        v.wait_ge(s_vp, b + 1)
                        nc.vector.tensor_tensor(v1[:, b, :, 0:DH], vps[0:L, b % 2, 0:D].rearrange("p (h d) -> p h d", d=DH),
                                                bfv[:].rearrange("p (h d) -> p h d", d=DH), ALU.add).then_inc(s_v, 1)
                    v.wait_ge(s_wl, 1)
                    v.wait_ge(s_kl, 2 * B)

                @block.gpsimd
                def _(pool):
                    nc.gpsimd.affine_select(out=causal[:], in_=causal[:], compare_op=ALU.is_ge, fill=-1e30, base=0,
                                            pattern=[[0, HB], [-1, L]], channel_multiplier=1).then_inc(s_causal, 1)
                    pool.wait_ge(s_causal, 1)

                @block.sync
                def _(sp):
                    sp.wait_ge(s_v, B)
                    for h, k0, m, j, r in parts:
                        at = (h - heads_of[j][0]) * VW
                        sp.dma_start(vp[r:r + m, :, j, at:at + VW], v1[k0:k0 + m, :, h, :]).then_inc(s_pack, 16)
                    sp.wait_ge(s_pack, 16 * len(parts))

        NS = 4
        e = core.sb("lo_e", [P, NS, J * P], ctx=ctx)
        pt = core.sb("lo_pt", [P, 2, J, P], ctx=ctx)
        top = core.sb("lo_top", [P, NS, HH], ctx=ctx)
        inv = core.sb("lo_inv", [P, 2, NH], ctx=ctx)
        qf = core.sb("lo_qf", [P, KD, CH], ctx=ctx)
        q = [core.sb(f"lo_q{n}", [P, 2, KD, CH], F32R, ctx) for n in "hl"]
        yn = core.sb("lo_yn", [P, 2, D], ctx=ctx)
        yT = core.sb("lo_yT", [P, 2, KD, P], ctx=ctx)
        sc = core.ps("lo_sc", [P, 2, 2, 512], ctx)
        pp = core.ps("lo_pp", [P, 2, 512], ctx)
        yp = core.ps("lo_yp", [P, 512], ctx)
        yo = core.ps("lo_yo", [P, 512], ctx)
        norm = Norm(core, "lo", ctx, None)
        (s_pad, s_s, s_top, s_sub, s_exp, s_pt, s_ptc, s_y, s_inv, s_yn, s_yT, s_yTc, s_o, s_x, s_xb, s_q, s_qf, s_qh, s_ql) = (
            core.sem(f"lp_{n}") for n in ("pad", "s", "top", "sub", "exp", "pt", "ptcopy", "y", "inv", "yn", "yT", "yTcopy", "o", "x",
                                          "xbias", "q", "qcopy", "qhigh", "qlow"))
        SLOT = [(0, 1), (0, 1), (1, 0), (0, 1)]
        T_SLOT, Q_SLOT = 0, 1

        def is_last(c):
            return isinstance(c, int) and c == NC - 1

        with nc.Block() as block:
            @block.tensor
            def _(pe):
                def queries(c, s):
                    pe.wait_ge(norm.low, c + 1)
                    for g in range(2):
                        for k in range(KD):
                            ins = mm3(nc, sc[:, Q_SLOT, g, :], [v[:, k, g * P:(g + 1) * P] for v in wq],
                                      [v[:, s, k] for v in (norm.xh, norm.xl)], start=(k == 0), stop=(k == KD - 1))
                    ins.then_inc(s_q, 1)

                def scores(t, u, g, c):
                    j, cs = u % TPC, u // TPC
                    if j == 0 and g == 0:
                        pe.wait_ge(s_ql, c + 1)
                    if (j, g) == (2, 1) and not is_last(c):
                        pe.wait_ge(norm.low, c + 2)
                    elif (j, g) == (3, 1) and not is_last(c):
                        pe.wait_ge(s_qf, c + 2)
                    elif (j, g) in ((2, 1), (3, 1)):
                        pe.wait_ge(s_sub, 2 * t - 1)
                    elif isinstance(t, int) and 2 * t + g < 2:
                        pass
                    elif (j, g) in ((2, 0), (3, 0)):
                        pe.wait_ge(s_sub, 2 * t)
                    else:
                        pe.wait_ge(s_sub, 2 * t + g - 1)
                    for half in range(2):
                        out = sc[:, SLOT[j][g], half, 0:HB * L]
                        rhs = [v[:].rearrange("p b g n -> p (b g n)")[:, bass.ds((t - u) * (2 * HL // 8) + g * HL + half * HB * L, HB * L)]
                               for v in kb]
                        ins = mm3(nc, out, [v[:, cs, g, j * P:(j + 1) * P] for v in q], rhs, start=True, stop=(u != 0))
                        if u == 0:
                            ins = nc.tensor.matmul(out, core.ident[:], causal[:].rearrange("p h l -> p (h l)"), start=False, stop=True)
                    ins.then_inc(s_s, 1)

                def turn(t, u, g):
                    m = 2 * t + g
                    pe.wait_ge(s_exp, m + 1)
                    if not (isinstance(t, int) and m == 0):
                        pe.wait_ge(s_ptc, m)
                    for j in range(J):
                        ins = nc.tensor.transpose(pp[:, j // 4, (j % 4) * P:(j % 4 + 1) * P],
                                                  e[:, (2 * u + g) % NS, j * P:(j + 1) * P], core.ident[:])
                    ins.then_inc(s_pt, 1)

                def values(t, u, g):
                    pe.wait_ge(s_ptc, 2 * t + g + 1)
                    if g == 0:
                        after(pe, s_yn, t, 1)
                    for j in range(J):
                        hs = heads_of[g * J + j]
                        rhs = vp[:].rearrange("p b j n -> p (b j n)")[
                            :, bass.ds((t - u) * (2 * J * VJ // 8) + (g * J + j) * VJ, len(hs) * VW)]
                        ins = nc.tensor.matmul(yp[:, hs[0] * VW:(hs[-1] + 1) * VW], pt[:, g, j, :], rhs,
                                               start=(g == 0 and j == 0), stop=(g == 1 and j == J - 1), skip_group_check=True)
                    ins.then_inc(s_y, 1)

                def step(t, u, lag, c):
                    j, cs = u % TPC, u // TPC
                    if lag[1] == "out_turn":
                        pe.wait_ge(s_yn, t + 1)
                        after(pe, s_x, t, 1)
                        for k in range(KD):
                            ins = nc.tensor.transpose(yo[:, k * P:(k + 1) * P], yn[:, u % 2, k * P:(k + 1) * P], core.ident[:])
                        ins.then_inc(s_yT, 1)
                    elif lag[1] == "s0":
                        scores(t, u, 0, c)
                    elif lag[1] == "t0":
                        turn(t, u, 0)
                    elif lag[1] == "s1":
                        if j == 3 and False:
                            pass
                        scores(t, u, 1, c)
                    elif lag[1] == "v0t1":
                        values(t, u, 0)
                        turn(t, u, 1)
                    elif lag[1] == "next":
                        if not is_last(c) and j == 1:
                            pe.wait_ge(s_sub, 2 * t + 1)
                            norm.turned = sc[:, T_SLOT]
                            norm.transpose(pe, c + 1, 1 - cs)
                        if not is_last(c) and j == 2:
                            pe.wait_ge(s_sub, 2 * t + 1)
                            queries(c + 1, 1 - cs)
                    elif lag[1] == "v1":
                        values(t, u, 1)
                    else:
                        pe.wait_ge(s_yTc, t + 1)
                        for k in range(KD):
                            ins = nc.tensor.matmul(yo[:, 0:D], yT[:, u % 2, k, :], wp[:, k, :], start=(k == 0), stop=(k == KD - 1))
                        ins.then_inc(s_o, 1)

                norm.turned = sc[:, T_SLOT]
                norm.transpose(pe, 0, 0)
                queries(0, 0)
                pe.wait_ge(s_qf, 1)
                pe.wait_ge(s_pad, 1)
                pipeline(pe, NT, TPS, [(2, "out_turn"), (0, "s0"), (1, "t0"), (0, "s1"), (1, "v0t1"), (0, "next"), (1, "v1"), (2, "out")],
                         step, per=TPC, ahead=True)

            @block.scalar
            def _(a):
                def chunk_queries(c, s):
                    a.wait_ge(s_q, c + 1)
                    after(a, s_ql, c, 1)
                    for g in range(2):
                        ins = nc.scalar.activation(qf[:, g], sc[:, Q_SLOT, g, :], ACT.Identity, bias=bq[:, g:g + 1])
                    ins.then_inc(s_qf, 1)
                    a.wait_ge(s_qf, c + 1)
                    after(a, s_s, c, 2, 2 * TPC)
                    nc.scalar.activation(q[0][:, s], qf[:], ACT.Copy).then_inc(s_qh, 1)

                def step(t, u, lag, c):
                    j, cs = u % TPC, u // TPC
                    if lag[1] in ("e0", "e1"):
                        m = 2 * t + int(lag[1][1])
                        slot = (2 * u + int(lag[1][1])) % NS
                        a.wait_ge(s_sub, m + 1)
                        nc.scalar.activation(e[:, slot, 0:HL], e[:, slot, 0:HL], ACT.Exp, scale=SCALE).then_inc(s_exp, 1)
                    elif lag[1] in ("p0", "p1"):
                        g = int(lag[1][1])
                        a.wait_ge(s_pt, 2 * t + g + 1)
                        after(a, s_y, t, 1, 2)
                        nc.scalar.activation(pt[:, g], pp[:].rearrange("p g n -> p (g n)")[:, 0:J * P], ACT.Copy).then_inc(s_ptc, 1)
                    elif lag[1] == "next":
                        if not is_last(c) and j == 1:
                            norm.turned = sc[:, T_SLOT]
                            after(a, s_q, c + 1, 2)
                            norm.take(a, c + 1, 1 - cs)
                        if not is_last(c) and j == 2:
                            chunk_queries(c + 1, 1 - cs)
                    else:
                        a.wait_ge(s_yT, t + 1)
                        after(a, s_o, t, 2)
                        nc.scalar.activation(yT[:, u % 2].rearrange("p k n -> p (k n)"), yo[:, 0:D], ACT.Copy).then_inc(s_yTc, 1)
                norm.turned = sc[:, T_SLOT]
                norm.take(a, 0, 0)
                chunk_queries(0, 0)
                pipeline(a, NT, TPS, [(2, "y"), (0, "e0"), (1, "p0"), (0, "e1"), (1, "p1"), (0, "next")], step, per=TPC, ahead=True)

            @block.gpsimd
            def _(pool):
                nc.gpsimd.memset(e[:, :, HL:], 0.0).then_inc(s_pad, 1)

                def step(t, u, lag, c):
                    if u % TPC == 0:
                        pool.wait_ge(norm.normed, c + 1)
                    nc.gpsimd.tensor_tensor(x[:, t, :], x[:, t, :], bp[:], ALU.add).then_inc(s_xb, 1)
                pipeline(pool, NT, TPS, [0], step, per=TPC)

            @block.vector
            def _(v):
                def queries_low(c, s):
                    v.wait_ge(s_qh, c + 1)
                    nc.vector.tensor_tensor(q[1][:, s], qf[:], q[0][:, s].bitcast(F32), ALU.subtract).then_inc(s_ql, 1)

                def softmax(t, u, g):
                    m, slot = 2 * t + g, (2 * u + g) % NS
                    view = sc[:, SLOT[u % TPC][g], :, 0:HB * L].rearrange("p b (h l) -> p b h l", l=L)
                    tops = top[:, slot].rearrange("p (b h) -> p b h", h=HB)
                    v.wait_ge(s_s, m + 1)
                    nc.vector.tensor_reduce(tops, view, AX_X, ALU.max).then_inc(s_top, 1)
                    v.wait_ge(s_top, m + 1)
                    after(v, s_pt, t, 2, 2)
                    nc.vector.tensor_tensor(e[:, slot, 0:HL].rearrange("p (b h l) -> p b h l", h=HB, l=L), view,
                                            tops.unsqueeze(3).to_broadcast([P, 2, HB, L]), ALU.subtract).then_inc(s_sub, 1)

                def step(t, u, lag, c):
                    j, cs = u % TPC, u // TPC
                    if lag[1] == "softmax":
                        if j == 0 and not is_last(c):
                            norm.normalise(v, c + 1, 1 - cs)
                        for g in range(2):
                            softmax(t, u, g)
                    elif lag[1] == "next":
                        if not is_last(c) and j == 1:
                            norm.turned = sc[:, T_SLOT]
                            norm.take_low(v, c + 1, 1 - cs)
                        if not is_last(c) and j == 2:
                            queries_low(c + 1, 1 - cs)
                    elif lag[1] == "divide":
                        v.wait_ge(s_y, 2 * t + 2)
                        yv = yp[:, 0:NH * VW].rearrange("p (h d) -> p h d", d=VW)
                        nc.vector.reciprocal(inv[:, u % 2], yv[:, :, DH]).then_inc(s_inv, 1)
                        v.wait_ge(s_inv, t + 1)
                        after(v, s_yT, t, 2)
                        nc.vector.tensor_tensor(yn[:, u % 2].rearrange("p (h d) -> p h d", d=DH), yv[:, :, 0:DH],
                                                inv[:, u % 2].unsqueeze(2).to_broadcast([P, NH, DH]), ALU.mult).then_inc(s_yn, 1)
                    else:
                        v.wait_ge(s_o, t + 1)
                        v.wait_ge(s_xb, t + 1)
                        nc.vector.tensor_tensor(x[:, t, :], yo[:, 0:D], x[:, t, :], ALU.add).then_inc(s_x, 1)
                norm.normalise(v, 0, 0)
                norm.turned = sc[:, T_SLOT]
                norm.take_low(v, 0, 0)
                queries_low(0, 0)
                pipeline(v, NT, TPS, [(0, "softmax"), (0, "next"), (1, "divide"), (2, "add")], step, per=TPC, ahead=True)


def decoder(nc, out, w):
    with ExitStack() as ctx:
        core = Core(nc, ctx)
        load_and_constants(core, w["x"])
        gated_chunks(core, w["gated"])
        core.end_branch()
        soft_attention(core, w["soft"])
        core.end_branch()
        experts(core, w["moe"]["weights"], w["moe"]["gate_w"], w["moe"]["expert_bias"])
        core.end_branch()
        linear_attention(core, w["linear"])
        core.end_branch()
        lora_attention(core, w["lora"])
        core.end_branch()
        picked_adapter(core, w["adapter"], out)



def kernel(**inputs):
    import numpy as np
    import concourse.bacc as _bacc
    from concourse.bass_utils import run_bass_kernel_spmd as _run

    a = {name: np.asarray(v) for name, v in inputs.items()}

    def feature_rows(m):
        return m.reshape(KD, P, -1).transpose(1, 0, 2)

    def column(b):
        return b.reshape(-1, P).T

    head_row = (np.arange(D).reshape(1, KD, P) // 16 == np.arange(16).reshape(16, 1, 1)).astype(np.float32)
    parity = ((np.arange(P)[:, None] // 16) % 2 == np.arange(2)).astype(np.float32)
    first = np.arange(8, 0, -1).astype(np.float32)

    context = a["ctx_1024"].reshape(-1, D).T.reshape(KD, P, -1).transpose(1, 0, 2)
    W_in = a["L0_attn_W_in"]
    wide, q, k = W_in[:, 0:3 * D], W_in[:, 3 * D:3 * D + 32], W_in[:, 3 * D + 32:]
    Wkv, Wqk = a["L0_xattn_Wkv"], a["L1_attn_Wqk"]

    def with_shared(routed, shared):
        return np.concatenate([routed, shared[None]]).transpose(0, 2, 1)

    expert_weights = np.stack([with_shared(a["L0_ffn_w_gate"], a["L0_ffn_shared_gate_w"]),
                               with_shared(a["L0_ffn_w_up"], a["L0_ffn_shared_up_w"]),
                               with_shared(a["L0_ffn_w_down"], a["L0_ffn_shared_down_w"])], 1)

    def per_head(m):
        return m.reshape(KD, P, 8, P).transpose(1, 0, 2, 3)

    operands = {
        "gated": dict(
            W_in=feature_rows(np.concatenate([wide] + [q] * 4 + [k] * 4, axis=1)),
            W_out=feature_rows(a["L0_attn_W_out"]), rms_weight=column(a["L0_attn_rms_weight"]),
            gate_bias=column(a["L0_attn_gate_bias"]), head_row=head_row),
        "soft": dict(
            ctxT=context, Wk=per_head(Wkv[:, :, 0:P]), Wv=per_head(Wkv[:, :, P:]),
            WqT=a["L0_xattn_Wq"].transpose(2, 1, 0), Wproj=a["L0_xattn_Wproj"].transpose(1, 0, 2),
            b_proj=a["L0_xattn_b_proj"]),
        "moe": dict(
            weights=expert_weights.reshape(-1, 3, KD, P, D).transpose(0, 3, 1, 2, 4),
            gate_w=a["L0_ffn_gate_w"].T, expert_bias=a["L0_ffn_expert_bias"]),
        "linear": dict(
            Wqk=feature_rows(Wqk), Wkv=feature_rows(np.concatenate([Wqk[:, D:], a["L1_attn_Wv"]], axis=1)),
            Wn=feature_rows(a["L1_attn_Wn"]), Wo=feature_rows(a["L1_attn_Wo"]),
            bq=column(a["L1_attn_bqk"][0:D]), bk=column(a["L1_attn_bqk"][D:]),
            bkv=np.concatenate([a["L1_attn_bqk"][D:], a["L1_attn_bv"]]), bn=a["L1_attn_bn"], bo=a["L1_attn_bo"],
            parity=parity),
        "lora": dict(
            W=feature_rows(np.concatenate([a["L1_xattn_Wq"], a["L1_xattn_Wf"], a["L1_xattn_Wp"]]).T),
            A=np.stack([a["L1_xattn_Aq"], a["L1_xattn_Af"], a["L1_xattn_Ap"]], axis=1),
            B=np.concatenate([a["L1_xattn_Bq"], a["L1_xattn_Bf"], a["L1_xattn_Bp"]]).T,
            bfk=column(a["L1_xattn_bf"][0:D]), bfv=a["L1_xattn_bf"][D:], bq=column(a["L1_xattn_bq"]),
            bp=a["L1_xattn_bp"]),
        "adapter": dict(
            Wd1=feature_rows(a["L1_ffn_Wd1"].transpose(1, 0, 2)), Wd2=a["L1_ffn_Wd2"].reshape(4, P, D).transpose(1, 0, 2),
            bd1=column(a["L1_ffn_bd1"]), bd2=feature_rows(a["L1_ffn_bd2"].T), W_base=feature_rows(a["L1_ffn_W_base"]),
            Wa_down=a["L1_ffn_Wa_down"].transpose(1, 0, 2).reshape(KD, P, 8, 64).transpose(1, 0, 2, 3),
            Wa_up=a["L1_ffn_Wa_up"].transpose(1, 0, 2), ba_up=a["L1_ffn_ba_up"][None],
            ba_down=a["L1_ffn_ba_down"].T, first=first, b_base=a["L1_ffn_b_base"]),
    }
    operands["adapter"]["Wd1"] = operands["adapter"]["Wd1"].reshape(P, KD, -1)

    nc = _bacc.Bacc("TRN2", target_bir_lowering=False, num_devices=1)
    arrays, aps = {}, {}

    def operand(name, value):
        arrays[name] = np.ascontiguousarray(value)
        return nc.dram_tensor(name, arrays[name].shape, F32, kind="ExternalInput").ap()

    for tag, group in operands.items():
        aps[tag] = {name: operand(f"{tag}_{name}_dram", value) for name, value in group.items()}
    aps["lora"]["ctxT"] = aps["soft"]["ctxT"]
    aps["x"] = operand("x_dram", a["x"])
    out = nc.dram_tensor("out_dram", a["x"].shape, F32, kind="ExternalOutput").ap()
    decoder(nc, out, aps)
    r = _run(nc, [arrays], core_ids=[0])
    return r.results[0]["out_dram"]
```

```python
from contextlib import ExitStack

import concourse.bass as bass
from concourse import mybir

ALU = mybir.AluOpType
ACT = mybir.ActivationFunctionType
F32 = mybir.dt.float32
F32R = mybir.dt.float32r
AX_X = mybir.AxisListType.X

P = 128
B, S, D = 4, 1024, 256
TOK = B * S
NT = TOK // P
KD = D // P
CH = 512
NC = TOK // CH
TPC = CH // P
EPS = 1e-5


def after(eng, sem, t, depth, per=1):
    if isinstance(t, int) and t < depth:
        return
    eng.wait_ge(sem, (t - depth + 1) * per)


def pipeline(eng, n, unroll, lags, step, per=None, ahead=False):
    most = max(lag[0] if isinstance(lag, tuple) else lag for lag in lags)
    head = -(-(most + 2) // unroll) * unroll
    tail = (n - head) % unroll + (unroll if ahead else 0)

    def at(i, off, whole):
        for lag in lags:
            item = off - (lag[0] if isinstance(lag, tuple) else lag)
            if whole or 0 <= item < n:
                more = () if per is None else (i * (unroll // per) + item // per,)
                step(i * unroll + item, item % unroll, lag, *more)

    for t in range(min(head, n + most)):
        at(0, t, False)
    if n - tail > head:
        with eng.Fori(0, (n - tail - head) // unroll) as i:
            for u in range(unroll):
                at(i, head + u, True)
    for t in range(max(head, n - tail), n + most):
        at(0, t, False)


class Core:

    def __init__(self, nc, ctx):
        self.nc, self.ctx = nc, ctx
        self.branch_sems = []
        self.arriving = []
        self.counted = False
        self.x = self.sb("x_rows", [P, NT, D])
        self.ident = self.sb("ident", [P, P])
        self.head_of = self.sb("head_of", [P, 8])
        self.stats = self.sb("stats", [P, NT, 6])
        self.mean = self.sb("mean", [P, NT])
        self.rstd = self.sb("rstd", [P, NT])
        self.rstd_ln = self.sb("rstd_ln", [P, NT])

    def sb(self, name, shape, dt=F32, ctx=None):
        return (ctx or self.ctx).enter_context(self.nc.sbuf_tensor(name, shape, dt))

    def ps(self, name, shape, ctx):
        return ctx.enter_context(self.nc.psum_tensor(name, shape, F32))

    def sem(self, name):
        self.branch_sems.append(self.nc.alloc_semaphore(name=name))
        return self.branch_sems[-1]

    def end_branch(self):
        self.nc.clear_and_free_semaphores(self.branch_sems)
        self.branch_sems = []
        self.nc.all_engine_barrier()


def mm3(nc, out, lhs, rhs, start, stop, **kw):
    (lh, ll), (rh, rl) = lhs, rhs
    nc.tensor.matmul(out, lh, rh, start=start, stop=False, **kw)
    nc.tensor.matmul(out, lh, rl, start=False, stop=False, **kw)
    return nc.tensor.matmul(out, ll, rh, start=False, stop=stop, **kw)


def load_and_constants(core, x_in):
    nc = core.nc
    core.arriving = [core.sem(f"x_in{c}") for c in range(NC)]
    core.x_in = x_in.rearrange("b (t p) d -> p (b t) d", p=P)
    made, done = core.sem("zeroed"), core.sem("ident_made")
    with nc.Block() as block:
        @block.gpsimd
        def _(pool):
            nc.gpsimd.memset(core.ident[:], 0.0).then_inc(made, 1)
            pool.wait_ge(made, 1)
            nc.gpsimd.affine_select(out=core.ident[:], in_=core.ident[:], compare_op=ALU.not_equal, fill=1.0,
                                    base=0, pattern=[[-1, P]], channel_multiplier=1).then_inc(done, 1)
            nc.gpsimd.memset(core.head_of[:], 1.0).then_inc(made, 1)
            pool.wait_ge(made, 2)
            nc.gpsimd.affine_select(out=core.head_of[:], in_=core.head_of[:], compare_op=ALU.is_ge, fill=0.0,
                                    base=0, pattern=[[-16, 8]], channel_multiplier=1).then_inc(done, 1)
            pool.wait_ge(done, 2)
            nc.gpsimd.affine_select(out=core.head_of[:], in_=core.head_of[:], compare_op=ALU.is_ge, fill=0.0,
                                    base=15, pattern=[[16, 8]], channel_multiplier=-1).then_inc(done, 1)
            pool.wait_ge(done, 3)


def row_stats(core, tag, rms=False, weights=(), loads=(), zeros=(), ones=(), scaled=None):
    nc, x, st, mean, rstd = core.nc, core.x, core.stats, core.mean, core.rstd
    with ExitStack() as ctx:
        tmp = core.sb(f"{tag}_tmp", [P, 6, NT], ctx=ctx)
        stats_in, dve, rooted = core.sem(f"{tag}_stats"), core.sem(f"{tag}_dve"), core.sem(f"{tag}_sqrt")
        var_ready = core.sem(f"{tag}_var")
        gap, var, std, r1, r2 = (tmp[:, j, :] for j in range(5))
        w_in = [core.sem(f"{tag}_stage_w{n}_in") for n in range(len(weights))]
        w_high, w_low, in_, filled, w_scaled = (
            core.sem(f"{tag}_stage_{q}") for q in ("whigh", "wlow", "in", "filled", "wscaled"))
        with nc.Block() as block:
            @block.sync
            def _(sp):
                for arrived, (raw, source, _, _) in zip(w_in, weights):
                    sp.dma_start(raw, source).then_inc(arrived, 16)
                for place, source in loads:
                    sp.dma_start(place, source).then_inc(in_, 16)
                for c, arrived in enumerate(core.arriving):
                    tiles = slice(c * TPC, (c + 1) * TPC)
                    sp.dma_start(x[:, tiles, :], core.x_in[:, tiles, :]).then_inc(arrived, 16)
                if loads:
                    sp.wait_ge(in_, 16 * len(loads))

            @block.gpsimd
            def _(pool):
                for place in zeros:
                    nc.gpsimd.memset(place, 0.0).then_inc(filled, 1)
                for place in ones:
                    nc.gpsimd.memset(place, 1.0).then_inc(filled, 1)
                for n, (raw, _, high, low) in enumerate(weights):
                    pool.wait_ge(w_high, n + 1)
                    nc.gpsimd.tensor_tensor(low, raw, high.bitcast(F32), ALU.subtract).then_inc(w_low, 1)
                if weights:
                    pool.wait_ge(w_low, len(weights))
                if zeros or ones:
                    pool.wait_ge(filled, len(zeros) + len(ones))

            @block.vector
            def _(v):
                links = [0]

                def link(ins):
                    links[0] += 1
                    ins.then_inc(dve, 1)
                    v.wait_ge(dve, links[0])

                for c, arrived in enumerate(core.arriving):
                    v.wait_ge(arrived, 16)
                    for t in range(c * TPC, (c + 1) * TPC):
                        nc.vector.bn_stats(st[:, t, :], x[:, t, :]).then_inc(stats_in, 1)
                if core.arriving:
                    v.wait_ge(stats_in, NT)
                    core.arriving = []
                elif not core.counted:
                    with v.Fori(0, NT // 8) as i:
                        for u in range(8):
                            nc.vector.bn_stats(st[:, i * 8 + u, :], x[:, i * 8 + u, :]).then_inc(stats_in, 1)
                    v.wait_ge(stats_in, NT)
                link(nc.vector.tensor_tensor(gap, st[:, :, 1], st[:, :, 4], ALU.subtract))
                link(nc.vector.tensor_tensor(mean[:], st[:, :, 1], st[:, :, 4], ALU.add))
                link(nc.vector.tensor_scalar(mean[:], mean[:], 0.5, None, ALU.mult))
                link(nc.vector.tensor_tensor(var, st[:, :, 2], st[:, :, 5], ALU.add))
                link(nc.vector.tensor_scalar(var, var, 1.0 / D, None, ALU.mult))
                link(nc.vector.scalar_tensor_tensor(out=gap, in0=gap, scalar=0.25, in1=gap, op0=ALU.mult, op1=ALU.mult))
                link(nc.vector.tensor_tensor(var, var, gap, ALU.add))
                nc.vector.tensor_scalar(r2, var, EPS, None, ALU.add).then_inc(var_ready, 1)
                v.wait_ge(rooted, 1)
                nc.vector.reciprocal(rstd[:], std).then_inc(dve, 1)
                links[0] += 1
                v.wait_ge(dve, links[0])
                if rms:
                    link(nc.vector.tensor_copy(r1, rstd[:]))
                    link(nc.vector.tensor_copy(core.rstd_ln[:], rstd[:]))
                    link(nc.vector.tensor_tensor(var, var, r1, ALU.mult))
                    link(nc.vector.tensor_tensor(var, var, r1, ALU.mult))
                    nc.vector.tensor_scalar(r2, var, 1e-6, None, ALU.add).then_inc(var_ready, 1)
                    v.wait_ge(rooted, 2)
                    link(nc.vector.reciprocal(r2, std))
                    link(nc.vector.tensor_tensor(rstd[:], r1, r2, ALU.mult))

            @block.scalar
            def _(a):
                for arrived, (raw, _, high, _) in zip(w_in, weights):
                    a.wait_ge(arrived, 16)
                    if scaled is not None and arrived is w_in[0]:
                        a.wait_ge(in_, 16 * len(loads))
                        for k in range(KD):
                            nc.scalar.activation(raw[:, k], raw[:, k], ACT.Copy, scale=scaled[:, k:k + 1]).then_inc(w_scaled, 1)
                        a.wait_ge(w_scaled, KD)
                    nc.scalar.activation(high, raw, ACT.Copy).then_inc(w_high, 1)
                for n in range(2 if rms else 1):
                    a.wait_ge(var_ready, n + 1)
                    nc.scalar.activation(std, r2, ACT.Sqrt).then_inc(rooted, 1)


class Norm:

    def __init__(self, core, tag, ctx, turned_banks, whole=False, resident=None):
        self.core = core
        self.resident = resident
        self.xn = core.sb(f"{tag}_xn", [P, 2, TPC, D], ctx=ctx)
        if resident is None:
            self.xh = core.sb(f"{tag}_xh", [P, 2, KD, CH], F32R, ctx=ctx)
            self.xl = core.sb(f"{tag}_xl", [P, 2, KD, CH], F32R, ctx=ctx)
        self.turned = turned_banks
        self.whole = core.sb(f"{tag}_whole", [P, 2, KD, CH], ctx=ctx) if whole else None
        self.s_whole = core.sem(f"{tag}_xwhole") if whole else None
        self.normed, self.turn, self.high, self.low = (
            core.sem(f"{tag}_{n}") for n in ("normed", "turned", "xhigh", "xlow"))

    def hi(self, c, s):
        return self.resident[0][:, :, bass.ds(c * CH, CH)] if self.resident else self.xh[:, s]

    def lo(self, c, s):
        return self.resident[1][:, :, bass.ds(c * CH, CH)] if self.resident else self.xl[:, s]

    def normalise(self, v, c, s):
        core, nc = self.core, self.core.nc
        after(v, self.turn, c, 2)
        for j in range(TPC):
            t = c * TPC + j
            ins = nc.vector.tensor_scalar(self.xn[:, s, j, :], core.x[:, t, :], core.mean[:, bass.ds(t, 1)],
                                          core.rstd[:, bass.ds(t, 1)], ALU.subtract, ALU.mult)
        ins.then_inc(self.normed, 1)

    def transpose(self, pe, c, s):
        nc = self.core.nc
        pe.wait_ge(self.normed, c + 1)
        for k in range(KD):
            for j in range(TPC):
                ins = nc.tensor.transpose(self.turned[:, k, j * P:(j + 1) * P],
                                          self.xn[:, s, j, k * P:(k + 1) * P], self.core.ident[:])
        ins.then_inc(self.turn, 1)

    def take(self, a, c, s):
        nc = self.core.nc
        a.wait_ge(self.turn, c + 1)
        source = self.turned[:, 0:KD, :]
        if self.whole is not None:
            nc.scalar.activation(self.whole[:, s], source, ACT.Copy).then_inc(self.s_whole, 1)
            a.wait_ge(self.s_whole, c + 1)
            source = self.whole[:, s]
        nc.scalar.activation(self.hi(c, s), source, ACT.Copy).then_inc(self.high, 1)

    def take_low(self, v, c, s):
        v.wait_ge(self.high, c + 1)
        source = self.turned[:, 0:KD, :] if self.whole is None else self.whole[:, s]
        self.core.nc.vector.tensor_tensor(self.lo(c, s), source, self.hi(c, s).bitcast(F32),
                                          ALU.subtract).then_inc(self.low, 1)


def experts(core, moe_w, gate_w, expert_bias):
    nc, x = core.nc, core.x
    NE = moe_w.shape[0]
    with ExitStack() as ctx:
        XH = core.sb("moe_xh", [P, KD, TOK], F32R, ctx)
        XL = core.sb("moe_xl", [P, KD, TOK], F32R, ctx)
        comb = core.sb("moe_comb", [P, NE, NT], ctx=ctx)
        raw = core.sb("moe_raw", [P, 3, KD, D], ctx=ctx)
        wh = core.sb("moe_wh", [P, 2, 3, KD, D], F32R, ctx)
        wl = core.sb("moe_wl", [P, 2, 3, KD, D], F32R, ctx)
        route(core, gate_w, expert_bias, XH, XL, comb, (raw[:], moe_w[0], wh[:, 0], wl[:, 0]))

        act_g = core.sb("moe_act_g", [P, 2, CH], ctx=ctx)
        h = core.sb("moe_h", [P, 2, CH], ctx=ctx)
        hh = core.sb("moe_hh", [P, 2, 2, CH], F32R, ctx)
        hl = core.sb("moe_hl", [P, 2, 2, CH], F32R, ctx)
        gu = core.ps("moe_gu", [P, 2, 2, CH], ctx)
        y = core.ps("moe_y", [P, 2, TPC, D], ctx)
        s_raw, s_wh, s_wl = core.sem("moe_raw_in"), core.sem("moe_whigh"), core.sem("moe_wlow")
        s_gu, s_silu, s_h, s_hh, s_hl, s_y, s_acc = (
            core.sem(f"moe_{n}") for n in ("gu", "silu", "h", "hhigh", "hlow", "y", "acc"))
        n = NE * NC

        with nc.Block() as block:
            @block.sync
            def _(sp):
                sp.dma_start(raw[:], moe_w[1]).then_inc(s_raw, 16)
                with sp.Fori(2, NE) as e:
                    sp.wait_ge(s_wh, e - 1)
                    sp.wait_ge(s_wl, e - 1)
                    sp.dma_start(raw[:], moe_w[bass.ds(e, 1)].rearrange("o p a k n -> (o p) a k n")).then_inc(s_raw, 16)

            @block.gpsimd
            def _(pool):
                def low(t, u, lag):
                    pool.wait_ge(s_wh, t + 1)
                    nc.gpsimd.tensor_tensor(wl[:, 1 - u], raw[:], wh[:, 1 - u].bitcast(F32), ALU.subtract).then_inc(s_wl, 1)

                pipeline(pool, NE - 1, 2, [0], low)

            @block.scalar
            def _(a):
                def weights_high(e, u):
                    a.wait_ge(s_raw, e * 16)
                    after(a, s_y, e, 2, NC)
                    nc.scalar.activation(wh[:, u], raw[:], ACT.Copy).then_inc(s_wh, 1)

                def step(t, u, e, more=True):
                    for ib in range(2):
                        a.wait_ge(s_gu, 2 * t + ib + 1)
                        after(a, s_h, t, 1, 2)
                        nc.scalar.activation(act_g[:, ib], gu[:, ib, 0, :], ACT.Silu).then_inc(s_silu, 1)
                    for ib in range(2):
                        a.wait_ge(s_h, 2 * t + ib + 1)
                        after(a, s_y, t, 2)
                        nc.scalar.activation(hh[:, u % 2, ib], h[:, ib], ACT.Copy).then_inc(s_hh, 1)
                    if u % NC == 2 and more:
                        weights_high(e + 1, (u // NC + 1) % 2)

                for t in range(NC):
                    step(t, t, 0)
                with a.Fori(0, (NE - 3) // 2) as i:
                    for r in range(NC, 3 * NC):
                        step(i * (2 * NC) + r, r % (2 * NC), i * 2 + r // NC)
                for t in range(n - 2 * NC, n):
                    step(t, t % (2 * NC), t // NC, t // NC + 1 < NE)

            @block.vector
            def _(v):
                def step(t, u, lag, e):
                    if lag == 0:
                        for ib in range(2):
                            v.wait_ge(s_silu, 2 * t + ib + 1)
                            after(v, s_hh, t, 1, 2)
                            after(v, s_hl, t, 1, 2)
                            nc.vector.tensor_tensor(h[:, ib], act_g[:, ib], gu[:, ib, 1, :], ALU.mult).then_inc(s_h, 1)
                        for ib in range(2):
                            v.wait_ge(s_hh, 2 * t + ib + 1)
                            nc.vector.tensor_tensor(hl[:, u % 2, ib], h[:, ib], hh[:, u % 2, ib].bitcast(F32),
                                                    ALU.subtract).then_inc(s_hl, 1)
                    else:
                        v.wait_ge(s_y, t + 1)
                        after(v, s_acc, t, 1)
                        c = u % NC
                        for j in range(TPC):
                            tile = c * TPC + j
                            w = comb[:].rearrange("p e t -> p (e t)")[:, bass.ds(e * NT + tile, 1)]
                            ins = nc.vector.scalar_tensor_tensor(out=x[:, tile, :], in0=y[:, u % 2, j, :], scalar=w,
                                                                 in1=x[:, tile, :], op0=ALU.mult, op1=ALU.add)
                        ins.then_inc(s_acc, 1)

                pipeline_body(v, n, step)

            @block.tensor
            def _(pe):
                def step(t, u, lag, e):
                    es = u // NC % 2
                    c = u % NC
                    if lag == 0:
                        if c == 0 and not (isinstance(e, int) and e == 0):
                            pe.wait_ge(s_wl, e)
                        rhs = (XH, XL)
                        for ib in range(2):
                            after(pe, s_h, t, 1, 2)
                            for g in range(2):
                                for k in range(KD):
                                    ins = mm3(nc, gu[:, ib, g, :],
                                              [w[:, es, g, k, ib * P:(ib + 1) * P] for w in (wh, wl)],
                                              [r[:, k, c * CH:(c + 1) * CH] for r in rhs],
                                              start=(k == 0), stop=(k == KD - 1))
                            ins.then_inc(s_gu, 1)
                    else:
                        pe.wait_ge(s_hl, 2 * t + 2)
                        after(pe, s_acc, t, 2)
                        for j in range(TPC):
                            for ib in range(2):
                                ins = mm3(nc, y[:, u % 2, j, :],
                                          [r[:, u % 2, ib, j * P:(j + 1) * P] for r in (hh, hl)],
                                          [w[:, es, 2, ib, :] for w in (wh, wl)],
                                          start=(ib == 0), stop=(ib == 1))
                        ins.then_inc(s_y, 1)

                pipeline_body(pe, n, step)


def pipeline_body(eng, n, step):
    for t in range(NC):
        step(t, t, 0, 0)
        if t:
            step(t - 1, t - 1, 1, 0)
    with eng.Fori(0, (n - NC) // (2 * NC)) as i:
        for r in range(NC, 3 * NC):
            step(i * (2 * NC) + r, r % (2 * NC), 0, i * 2 + r // NC)
            step(i * (2 * NC) + (r - 1), (r - 1) % (2 * NC), 1, i * 2 + (r - 1) // NC)
    step(n - 1, (n - 1) % (2 * NC), 1, (n - 1) // NC)


def route(core, gate_w, expert_bias, XH, XL, comb, first_expert):
    nc = core.nc
    E, K_TOP, ROUTE_SCALE = 16, 8, 2.826
    with ExitStack() as ctx:
        gw = core.sb("moe_gw", [P, KD, E], ctx=ctx)
        gwh, gwl = (core.sb(f"moe_gw{n}", [P, KD, E], F32R, ctx) for n in "hl")
        bias = core.sb("moe_bias", [P, E], ctx=ctx)
        row_stats(core, "moe", weights=[(gw[:], gate_w.rearrange("(k p) e -> p k e", p=P), gwh[:], gwl[:]), first_expert],
                  loads=[(bias[:], expert_bias.partition_broadcast(P))])
        turned = core.ps("moe_turned", [P, 2, KD, CH], ctx)
        gates = core.ps("moe_gates", [P, 2, CH], ctx)
        rows = core.ps("moe_gate_rows", [P, NT, E], ctx)
        gT = core.sb("moe_gT", [E, TOK], ctx=ctx)
        score, sel, left, top = (core.sb(f"moe_{q}", [P, NT, w], ctx=ctx)
                                 for q, w in (("score", E), ("sel", E), ("left", E), ("top", K_TOP)))
        total = core.sb("moe_total", [P, NT], ctx=ctx)
        norm = Norm(core, "moe", ctx, None, resident=(XH, XL))
        s_gates, s_gcopy, s_rows, s_score, dve, s_top = (
            core.sem(f"moe_{q}") for q in ("gates", "gcopy", "grows", "score", "rdve", "top"))
        with nc.Block() as block:
            @block.tensor
            def _(pe):
                def step(c, u, lag):
                    if lag == 0:
                        after(pe, norm.low, c, 2)
                        norm.turned = turned[:, u]
                        norm.transpose(pe, c, u)
                    else:
                        pe.wait_ge(norm.low, c + 1)
                        after(pe, s_gcopy, c, 2)
                        for k in range(KD):
                            ins = mm3(nc, gates[0:E, u, :], (gwh[:, k], gwl[:, k]), [r[:, k, :] for r in (norm.hi(c, u), norm.lo(c, u))],
                                      start=(k == 0), stop=(k == KD - 1))
                        ins.then_inc(s_gates, 1)
                pipeline(pe, NC, 2, [0, 1], step)
                pe.wait_ge(s_gcopy, NC)
                for t in range(NT):
                    ins = nc.tensor.transpose(rows[:, t, :], gT[:, t * P:(t + 1) * P], core.ident[0:E, 0:E])
                ins.then_inc(s_rows, 1)

            @block.scalar
            def _(a):
                def step(c, u, lag):
                    if lag == 0:
                        norm.turned = turned[:, u]
                        norm.take(a, c, u)
                    else:
                        a.wait_ge(s_gates, c + 1)
                        nc.scalar.activation(gT[:, bass.ds(c * CH, CH)], gates[0:E, u, :], ACT.Copy).then_inc(s_gcopy, 1)
                pipeline(a, NC, 2, [0, 1], step)
                a.wait_ge(s_rows, 1)
                nc.scalar.activation(score[:], rows[:], ACT.Sigmoid).then_inc(s_score, 1)

            @block.vector
            def _(v):
                def step(c, u, lag):
                    if lag == 0:
                        norm.normalise(v, c, u)
                    else:
                        norm.turned = turned[:, u]
                        norm.take_low(v, c, u)
                pipeline(v, NC, 2, [0, 1], step)
                v.wait_ge(s_score, 1)
                nc.vector.tensor_tensor(sel[:], score[:], bias[:].unsqueeze(1).to_broadcast([P, NT, E]),
                                        ALU.add).then_inc(dve, 1)
                v.wait_ge(dve, 1)
                for t in range(NT):
                    nc.vector.max(top[:, t, :], sel[:, t, :]).then_inc(s_top, 1)
                for t in range(NT):
                    v.wait_ge(s_top, t + 1)
                    nc.vector.match_replace(left[:, t, :], top[:, t, :], sel[:, t, :], -1e30).then_inc(s_top, 1)
                v.wait_ge(s_top, 2 * NT)
                nc.vector.tensor_tensor(left[:], left[:], sel[:], ALU.not_equal).then_inc(dve, 1)
                v.wait_ge(dve, 2)
                nc.vector.tensor_tensor(score[:], left[:], score[:], ALU.mult).then_inc(dve, 1)
                v.wait_ge(dve, 3)
                nc.vector.tensor_reduce(total[:], score[:], AX_X, ALU.add).then_inc(dve, 1)
                v.wait_ge(dve, 4)
                nc.vector.reciprocal(total[:], total[:]).then_inc(dve, 1)
                v.wait_ge(dve, 5)
                nc.vector.tensor_scalar(total[:], total[:], ROUTE_SCALE, None, ALU.mult).then_inc(dve, 1)
                v.wait_ge(dve, 6)
                nc.vector.tensor_tensor(comb[:, 0:E, :], score[:].rearrange("p t e -> p e t"),
                                        total[:].unsqueeze(1).to_broadcast([P, E, NT]), ALU.mult).then_inc(dve, 1)
                nc.vector.memset(comb[:, E:E + 1, :], 1.0).then_inc(dve, 1)
                v.wait_ge(dve, 8)


def picked_adapter(core, w, out):
    nc, x = core.nc, core.x
    E, H = 8, 64
    EB = E // 2
    SEQ_CH = S // CH
    with ExitStack() as ctx:
        XH = core.sb("ffn_xh", [P, KD, TOK], F32R, ctx)
        XL = core.sb("ffn_xl", [P, KD, TOK], F32R, ctx)
        bd1 = core.sb("ffn_bd1", [P, EB], ctx=ctx)
        bd2 = core.sb("ffn_bd2", [P, KD, E], ctx=ctx)
        w_base = core.sb("ffn_w_base", [P, KD, D], ctx=ctx)
        loss = core.sb("ffn_loss", [P, NC, E, KD], ctx=ctx)
        wad = core.sb("ffn_wad", [P, KD, E, H], ctx=ctx)
        wau = core.sb("ffn_wau", [H + 1, E, D], ctx=ctx)
        bad = core.sb("ffn_bad", [H, E], ctx=ctx)
        first = core.sb("ffn_first", [P, E], ctx=ctx)
        base_row = core.sb("ffn_base_row", [H + 1, D], ctx=ctx)
        ones = core.sb("ffn_ones", [P, P], ctx=ctx)
        with ExitStack() as inner:
            w1 = [core.sb(f"ffn_w1{q}", [P, KD, E * H], F32R, inner) for q in "hl"]
            w2 = [core.sb(f"ffn_w2{q}", [P, E, D], F32R, inner) for q in "hl"]
            with ExitStack() as staging:
                raw1 = core.sb("ffn_raw1", [P, KD, E * H], ctx=staging)
                raw2 = core.sb("ffn_raw2", [P, E, D], ctx=staging)
                row_stats(core, "ffn", weights=[(raw1[:], w["Wd1"], w1[0][:], w1[1][:]), (raw2[:], w["Wd2"], w2[0][:], w2[1][:])],
                          loads=[(bd1[:], w["bd1"]), (bd2[:], w["bd2"]), (w_base[:], w["W_base"]), (wad[:], w["Wa_down"]),
                                 (wau[0:H], w["Wa_up"]), (wau[H:H + 1], w["ba_up"]), (bad[:], w["ba_down"]),
                                 (first[:], w["first"].partition_broadcast(P))],
                          zeros=[base_row[0:H]], ones=[ones[:]])
            h = core.sb("ffn_h", [P, 2, CH], ctx=inner)
            hh = core.sb("ffn_hh", [P, 2, EB, CH], F32R, inner)
            hl = core.sb("ffn_hl", [P, 2, EB, CH], F32R, inner)
            gap = core.sb("ffn_gap", [P, 3, CH], ctx=inner)
            junk = core.sb("ffn_junk", [P, 2, CH], ctx=inner)
            turned = core.ps("ffn_turned", [P, KD, CH], inner)
            hp = core.ps("ffn_hp", [P, 2, CH], inner)
            rp = core.ps("ffn_rp", [P, 2, CH], inner)
            bp = core.ps("ffn_bp", [P, TPC, D], inner)
            norm = Norm(core, "ffn", inner, turned, whole=True, resident=(XH, XL))
            s_hp, s_relu, s_hh, s_hl, s_rp, s_gap, s_sq, s_bp, s_bx, s_row = (
                core.sem(f"ffn_{q}") for q in ("hp", "relu", "hhigh", "hlow", "rp", "gap", "sq", "bp", "bx", "row"))
            NR = E * KD
            banks = [rp[:, 0, :], rp[:, 1, :], hp[:, 0, :], hp[:, 1, :]]

            with nc.Block() as block:
                @block.sync
                def _(sp):
                    sp.dma_start(base_row[H:H + 1], w["b_base"].rearrange("(o n) -> o n", o=1)).then_inc(s_row, 16)
                    sp.wait_ge(s_row, 16)

                @block.tensor
                def _(pe):
                    def turn(c, u):
                        after(pe, norm.s_whole, c, 1)
                        norm.transpose(pe, c, u)

                    def rebuild(c, u):
                        pe.wait_ge(norm.low, c + 1)
                        for q in range(EB):
                            m = c * EB + q
                            if q >= 2:
                                pe.wait_ge(s_relu, m - 1)
                            elif not (isinstance(c, int) and c == 0):
                                pe.wait_ge(s_gap, c * NR + q - 1)
                            for k in range(KD):
                                ins = mm3(nc, hp[:, q % 2, :], [v[:, k, q * P:(q + 1) * P] for v in w1],
                                          (norm.hi(c, u)[:, k], norm.lo(c, u)[:, k]), start=(k == 0), stop=(k == KD - 1))
                            ins.then_inc(s_hp, 1)
                        for j in range(TPC):
                            after(pe, s_bx, c, 1)
                            for k in range(KD):
                                ins = nc.tensor.matmul(bp[:, j, :], norm.whole[:, u, k, j * P:(j + 1) * P],
                                                       w_base[:, k, :], start=(k == 0), stop=(k == KD - 1))
                        ins.then_inc(s_bp, 1)
                        for e in range(E):
                            pe.wait_ge(s_hl, c * EB + e // 2 + 1)
                            for k in range(KD):
                                n = e * KD + k
                                m = c * NR + n
                                if n in (2, 3):
                                    pe.wait_ge(s_relu, c * EB + n + 1)
                                elif not (isinstance(c, int) and m < 2):
                                    pe.wait_ge(s_gap, m - 3)
                                mm3(nc, banks[n % 4], [v[:, e, k * P:(k + 1) * P] for v in w2],
                                    (hh[:, u, e // 2, :], hl[:, u, e // 2, :]), start=True, stop=True).then_inc(s_rp, 1)

                    turn(0, 0)
                    def turn_then(c, u):
                        turn(c + 1, 1 - u)
                        rebuild(c, u)

                    turn_then(0, 0)
                    turn_then(1, 1)
                    with pe.Fori(1, NC // 2 - 1) as i:
                        turn_then(i * 2, 0)
                        turn_then(i * 2 + 1, 1)
                    turn_then(NC - 2, 0)
                    rebuild(NC - 1, 1)

                @block.scalar
                def _(a):
                    def step(c, u, lag):
                        if lag[1] == "take":
                            after(a, s_bp, c, 2)
                            after(a, s_gap, c, 2, NR)
                            after(a, norm.low, c, 2)
                            norm.take(a, c, u)
                            return
                        for q in range(EB) if lag[1] == "hidden" else ():
                            m = c * EB + q
                            a.wait_ge(s_hp, m + 1)
                            after(a, s_hl, m, 2)
                            nc.scalar.activation(h[:, q % 2], hp[:, q % 2, :], ACT.Relu, bias=bd1[:, q:q + 1]).then_inc(s_relu, 1)
                            after(a, s_rp, c, 2, NR)
                            a.wait_ge(s_relu, m + 1)
                            nc.scalar.activation(hh[:, u, q], h[:, q % 2], ACT.Copy).then_inc(s_hh, 1)
                        for e in range(E) if lag[1] == "square" else ():
                            for k in range(KD):
                                m = c * NR + e * KD + k
                                a.wait_ge(s_gap, m + 1)
                                after(a, s_sq, m, 2)
                                nc.scalar.activation(junk[:, k], gap[:, (e * KD + k) % 2], ACT.Square,
                                                     accum_out=loss[:].rearrange("p c e k -> p (c e k)")[:, bass.ds(m, 1)]).then_inc(s_sq, 1)
                    pipeline(a, NC, 2, [(1, "hidden"), (0, "take"), (1, "square")], step)

                @block.vector
                def _(v):
                    def step(c, u, lag):
                        if lag[1] == "normalise":
                            norm.normalise(v, c, u)
                            return
                        if lag[1] == "low":
                            norm.take_low(v, c, u)
                            return
                        if lag[1] == "hidden":
                            for q in range(EB):
                                v.wait_ge(s_hh, c * EB + q + 1)
                                nc.vector.tensor_tensor(hl[:, u, q], h[:, q % 2], hh[:, u, q].bitcast(F32),
                                                        ALU.subtract).then_inc(s_hl, 1)
                            return
                        v.wait_ge(s_bp, c + 1)
                        for j in range(TPC):
                            t = c * TPC + j
                            ins = nc.vector.tensor_tensor(x[:, t, :], x[:, t, :], bp[:, j, :], ALU.add)
                        ins.then_inc(s_bx, 1)
                        for e in range(E):
                            for k in range(KD):
                                m = c * NR + e * KD + k
                                v.wait_ge(s_rp, m + 1)
                                if not (isinstance(c, int) and m < 2):
                                    v.wait_ge(s_sq, m - 1)
                                nc.vector.scalar_tensor_tensor(out=gap[:, (e * KD + k) % 2], in0=banks[(e * KD + k) % 4], scalar=bd2[:, k, e:e + 1],
                                                               in1=norm.whole[:, u, k], op0=ALU.add,
                                                               op1=ALU.subtract).then_inc(s_gap, 1)
                    pipeline(v, NC, 2, [(0, "normalise"), (2, "hidden"), (1, "low"), (2, "gaps")], step)

        pick = core.sb("ffn_pick", [P, 4, B, E], ctx=ctx)
        best = core.sb("ffn_best", [P, 2, B], ctx=ctx)
        dsel = core.sb("ffn_dsel", [P, B, KD, H], ctx=ctx)
        usel = core.sb("ffn_usel", [H + 1, B, D], ctx=ctx)
        uprod = core.sb("ffn_uprod", [H + 1, D], ctx=ctx)
        dbias = core.sb("ffn_dbias", [H, B], ctx=ctx)
        bprod = core.sb("ffn_bprod", [H, B, E], ctx=ctx)
        dh, dl = (core.sb(f"ffn_d{q}", [P, B, KD, H], F32R, ctx) for q in "hl")
        uh, ul = (core.sb(f"ffn_u{q}", [H + 1, B, D], F32R, ctx) for q in "hl")
        a_ = core.sb("ffn_a", [H, 2, CH], ctx=ctx)
        ah = core.sb("ffn_ah", [H + 1, 2, CH], F32R, ctx)
        al = core.sb("ffn_al", [H + 1, 2, CH], F32R, ctx)
        tp = core.ps("ffn_total", [P, B * E], ctx)
        ap = core.ps("ffn_ap", [H, 2, CH], ctx)
        op = core.ps("ffn_op", [P, 2, TPC, D], ctx)
        s_sum, s_tot, dve, s_down, s_up_even, s_up_odd, s_high, s_low, s_rows = (
            core.sem(f"ffn_{q}") for q in ("sum", "tot", "pdve", "down_picked", "up_even", "up_odd", "shigh", "slow", "arows"))
        s_ap, s_a, s_ah, s_al, s_op, s_x, s_out = (core.sem(f"ffn_{q}") for q in ("ap", "a", "ah", "al", "op", "x", "out"))
        total, cand, hot = pick[:, 0], pick[:, 1], pick[:, 2]
        out_v = out.rearrange("b (t p) d -> p (b t) d", p=P)
        with nc.Block() as block:
            @block.tensor
            def _(pe):
                pe.wait_ge(s_sum, 2)
                nc.tensor.matmul(tp[:], ones[:], pick[:, 3].rearrange("p b e -> p (b e)"), start=True, stop=True).then_inc(s_tot, 1)
                pe.wait_ge(s_low, 1)
                for c in range(NC + 1):
                    if c < NC:
                        after(pe, s_a, c, 2)
                        for k in range(KD):
                            ins = mm3(nc, ap[:, c % 2, :], (dh[:, c // SEQ_CH, k, :], dl[:, c // SEQ_CH, k, :]),
                                      (XH[:, k, c * CH:(c + 1) * CH], XL[:, k, c * CH:(c + 1) * CH]),
                                      start=(k == 0), stop=(k == KD - 1))
                        ins.then_inc(s_ap, 1)
                    if c:
                        d = c - 1
                        pe.wait_ge(s_al, d + 1)
                        if d == 0:
                            pe.wait_ge(s_rows, 2)
                        if d % SEQ_CH == 0:
                            pe.wait_ge(s_low, d // SEQ_CH + 2)
                        after(pe, s_x, d, 2)
                        for j in range(TPC):
                            ins = mm3(nc, op[:, d % 2, j, :], [q[:, d % 2, j * P:(j + 1) * P] for q in (ah, al)],
                                      (uh[:, d // SEQ_CH, :], ul[:, d // SEQ_CH, :]), start=True, stop=True)
                        ins.then_inc(s_op, 1)

            @block.gpsimd
            def _(pool):
                nc.gpsimd.memset(ah[H:H + 1].bitcast(F32), 1.0).then_inc(s_rows, 1)
                nc.gpsimd.memset(al[H:H + 1].bitcast(F32), 0.0).then_inc(s_rows, 1)
                pool.wait_ge(s_rows, 2)
                pool.wait_ge(dve, 7)
                steps = 0
                for b in range(0, B, 2):
                    for e in range(E):
                        if steps:
                            pool.wait_ge(s_up_even, steps)
                        nc.gpsimd.tensor_tensor(uprod[:], wau[:, e, :], hot[0:H + 1, b, e:e + 1].to_broadcast([H + 1, D]),
                                                ALU.mult).then_inc(s_up_even, 1)
                        pool.wait_ge(s_up_even, steps + 1)
                        nc.gpsimd.tensor_tensor(usel[:, b, :], uprod[:], base_row[:] if e == 0 else usel[:, b, :],
                                                ALU.add).then_inc(s_up_even, 1)
                        steps += 2

            @block.scalar
            def _(a):
                def up_high(b):
                    if b % 2:
                        a.wait_ge(s_up_odd, (b // 2 + 1) * E)
                    else:
                        a.wait_ge(s_up_even, (b // 2 + 1) * 2 * E)
                    nc.scalar.activation(uh[:, b], usel[:, b], ACT.Copy).then_inc(s_high, 1)

                a.wait_ge(s_down, 1)
                nc.scalar.activation(dh[:], dsel[:], ACT.Copy).then_inc(s_high, 1)
                up_high(0)
                for c in range(NC):
                    a.wait_ge(s_ap, c + 1)
                    after(a, s_al, c, 2)
                    nc.scalar.activation(a_[:, c % 2], ap[:, c % 2, :], ACT.Relu, bias=dbias[:, c // SEQ_CH:c // SEQ_CH + 1]).then_inc(s_a, 1)
                    after(a, s_op, c, 2)
                    a.wait_ge(s_a, c + 1)
                    nc.scalar.activation(ah[0:H, c % 2], a_[:, c % 2], ACT.Copy).then_inc(s_ah, 1)
                    if c % SEQ_CH == SEQ_CH - 1 and c < NC - 1:
                        up_high(c // SEQ_CH + 1)

            @block.vector
            def _(v):
                links = [0]

                def link(ins):
                    links[0] += 1
                    ins.then_inc(dve, 1)
                    v.wait_ge(dve, links[0])

                lv = loss[:].rearrange("p (b c) e k -> p b c e k", c=SEQ_CH)
                link(nc.vector.tensor_tensor(pick[:, 0], lv[:, :, 0, :, 0], lv[:, :, 0, :, 1], ALU.add))
                nc.vector.tensor_tensor(pick[:, 1], lv[:, :, 1, :, 0], lv[:, :, 1, :, 1], ALU.add).then_inc(s_sum, 1)
                v.wait_ge(s_sum, 1)
                nc.vector.tensor_tensor(pick[:, 3], pick[:, 0], pick[:, 1], ALU.add).then_inc(s_sum, 1)
                v.wait_ge(s_tot, 1)
                link(nc.vector.tensor_scalar(total, tp[:].rearrange("p (b e) -> p b e", e=E), -1.0, None, ALU.mult))
                link(nc.vector.tensor_reduce(best[:, 0], total, AX_X, ALU.max))
                link(nc.vector.tensor_tensor(cand, total, best[:, 0].unsqueeze(2).to_broadcast([P, B, E]), ALU.is_equal))
                link(nc.vector.tensor_tensor(cand, cand, first[:].unsqueeze(1).to_broadcast([P, B, E]), ALU.mult))
                link(nc.vector.tensor_reduce(best[:, 1], cand, AX_X, ALU.max))
                link(nc.vector.tensor_tensor(hot, cand, best[:, 1].unsqueeze(2).to_broadcast([P, B, E]), ALU.is_equal))
                link(nc.vector.tensor_tensor(bprod[:], hot[0:H], bad[:].unsqueeze(1).to_broadcast([H, B, E]), ALU.mult))
                nc.vector.tensor_reduce(dbias[:], bprod[:], AX_X, ALU.add).then_inc(dve, 1)
                links[0] += 1
                for e in range(E):
                    for b in range(B):
                        if e == 0:
                            ins = nc.vector.tensor_scalar(dsel[:, b], wad[:, :, e, :], hot[:, b, e:e + 1], None, ALU.mult)
                        else:
                            ins = nc.vector.scalar_tensor_tensor(out=dsel[:, b], in0=wad[:, :, e, :], scalar=hot[:, b, e:e + 1],
                                                                 in1=dsel[:, b], op0=ALU.mult, op1=ALU.add)
                    if e == E - 1:
                        ins.then_inc(s_down, 1)
                    else:
                        link(ins)
                v.wait_ge(s_high, 1)
                nc.vector.tensor_tensor(dl[:], dsel[:], dh[:].bitcast(F32), ALU.subtract).then_inc(s_low, 1)

                def up_rows(b):
                    for e in range(E):
                        n = b // 2 * E + e
                        if e:
                            v.wait_ge(s_up_odd, n)
                        nc.vector.scalar_tensor_tensor(out=usel[:, b, :], in0=wau[:, e, :], scalar=hot[0:H + 1, b, e:e + 1],
                                                       in1=base_row[:] if e == 0 else usel[:, b, :],
                                                       op0=ALU.mult, op1=ALU.add).then_inc(s_up_odd, 1)

                def up_low(b):
                    v.wait_ge(s_high, b + 2)
                    nc.vector.tensor_tensor(ul[:, b], usel[:, b], uh[:, b].bitcast(F32), ALU.subtract).then_inc(s_low, 1)

                up_low(0)
                for c in range(NC + 1):
                    if c < NC:
                        v.wait_ge(s_ah, c + 1)
                        after(v, s_op, c, 2)
                        nc.vector.tensor_tensor(al[0:H, c % 2], a_[:, c % 2], ah[0:H, c % 2].bitcast(F32),
                                                ALU.subtract).then_inc(s_al, 1)
                        if c % SEQ_CH == 0 and c // SEQ_CH < B // 2:
                            up_rows(2 * (c // SEQ_CH) + 1)
                        if c % SEQ_CH == SEQ_CH - 1 and c < NC - 1:
                            up_low(c // SEQ_CH + 1)
                    if c:
                        d = c - 1
                        v.wait_ge(s_op, d + 1)
                        xv = x[:, d * TPC:(d + 1) * TPC, :]
                        nc.vector.tensor_tensor(xv, xv, op[:, d % 2], ALU.add).then_inc(s_x, 1)

            @block.sync
            def _(sp):
                for c in range(NC):
                    sp.wait_ge(s_x, c + 1)
                    sp.dma_start(out_v[:, c * TPC:(c + 1) * TPC, :], x[:, c * TPC:(c + 1) * TPC, :]).then_inc(s_out, 16)
                sp.wait_ge(s_out, 16 * NC)


def soft_attention(core, w):
    nc, x = core.nc, core.x
    H, E, L = 8, 128, w["ctxT"].shape[-1] // B
    HL = H * L
    HB = 4
    J = -(-(HL + 1) // P)
    SCALE = E ** -0.5
    with ExitStack() as ctx:
        ah, al = (core.sb(f"xa_a{q}", [P, KD, B, HL], F32R, ctx) for q in "hl")
        vw = core.sb("xa_vw", [P, B, J, D], ctx=ctx)
        with ExitStack() as inner:
            ctxT = core.sb("xa_ctxT", [P, KD, B * L], ctx=inner)
            wk, wv = (core.sb(f"xa_{q}", [P, KD, H, E], ctx=inner) for q in ("wk", "wv"))
            wqT, wproj = (core.sb(f"xa_{q}", [P, H, D], ctx=inner) for q in ("wqT", "wproj"))
            kvT = core.sb("xa_kvT", [P, 2, H, B * L], ctx=inner)
            row_stats(core, "xa", loads=[(ctxT[:], w["ctxT"]), (wk[:], w["Wk"]), (wqT[:], w["WqT"]), (wv[:], w["Wv"]),
                                         (wproj[:], w["Wproj"])], zeros=[vw[:]])
            vws = core.sb("xa_vws", [L, 2, B, D], ctx=inner)
            kv = core.ps("xa_kv", [P, 2, 512], inner)
            ap = core.ps("xa_ap", [P, 2, 512], inner)
            vp = core.ps("xa_vp", [P, 2, 2, 256], inner)
            s_kv, s_kvc, s_ap, s_ah, s_al, s_vp, s_vs, s_pack, s_row = (
                core.sem(f"xa_{q}") for q in ("kv", "kvcopy", "ap", "ahigh", "alow", "vp", "vs", "pack", "biasrow"))
            parts = []
            for hd in range(H):
                k0 = 0
                while k0 < L:
                    r = hd * L + k0
                    m = min(L - k0, P - r % P)
                    parts.append((hd, k0, m, r // P, r % P))
                    k0 += m
            s_packs = (s_pack, core.sem("xa_pack_odd"))
            sent = [sum(1 for q in parts if q[0] <= hd and q[0] % 2 == hd % 2) for hd in range(H)]
            with nc.Block() as block:
                @block.tensor
                def _(pe):
                    for m in range(2 * H):
                        after(pe, s_kvc, m, 2)
                        for k in range(KD):
                            ins = nc.tensor.matmul(kv[:, m % 2, 0:B * L], (wk, wv)[m // H][:, k, m % H, :], ctxT[:, k, :],
                                                   start=(k == 0), stop=(k == KD - 1))
                        ins.then_inc(s_kv, 1)
                    for m in range(2 * H):
                        after(pe, s_al, m, 2)
                        pe.wait_ge(s_kvc, m // 2 + 1)
                        nc.tensor.matmul(ap[:, m % 2, 0:B * L], wqT[:, m // 2, (m % 2) * P:(m % 2 + 1) * P], kvT[:, 0, m // 2, :],
                                         start=True, stop=True).then_inc(s_ap, 1)
                    pe.wait_ge(s_kvc, 2 * H)
                    for m in range(2 * H):
                        after(pe, s_vs, m, 2)
                        for q in range(2):
                            b = (m % 2) * 2 + q
                            ins = nc.tensor.matmul(vp[0:L, m % 2, q, :], kvT[:, 1, m // 2, b * L:(b + 1) * L], wproj[:, m // 2, :],
                                                   start=True, stop=True)
                        ins.then_inc(s_vp, 1)

                @block.scalar
                def _(a):
                    for m in range(2 * H):
                        a.wait_ge(s_kv, m + 1)
                        nc.scalar.activation(kvT[:, m // H, m % H, :], kv[:, m % 2, 0:B * L], ACT.Copy).then_inc(s_kvc, 1)
                    for m in range(2 * H):
                        a.wait_ge(s_ap, m + 1)
                        nc.scalar.activation(ah[:, m % 2, :, (m // 2) * L:(m // 2 + 1) * L],
                                             ap[:, m % 2, 0:B * L].rearrange("p (b l) -> p b l", b=B), ACT.Copy).then_inc(s_ah, 1)

                @block.vector
                def _(v):
                    for m in range(2 * H):
                        v.wait_ge(s_ah, m + 1)
                        part = (slice(None), m % 2, slice(None), slice((m // 2) * L, (m // 2 + 1) * L))
                        nc.vector.tensor_tensor(al[part], ap[:, m % 2, 0:B * L].rearrange("p (b l) -> p b l", b=B),
                                                ah[part].bitcast(F32), ALU.subtract).then_inc(s_al, 1)
                    for m in range(2 * H):
                        v.wait_ge(s_vp, m + 1)
                        if m // 2 >= 2:
                            v.wait_ge(s_packs[m // 2 % 2], 16 * sent[m // 2 - 2])
                        nc.vector.tensor_copy(vws[:, m // 2 % 2, (m % 2) * 2:(m % 2) * 2 + 2, :], vp[0:L, m % 2]).then_inc(s_vs, 1)

                @block.sync
                def _(sp):
                    for b in range(B):
                        sp.dma_start(vw[HL % P:HL % P + 1, b, HL // P, :], w["b_proj"].rearrange("(o n) -> o n", o=1)).then_inc(s_row, 16)
                    for hd, k0, m, j, r in parts:
                        sp.wait_ge(s_vs, 2 * hd + 2)
                        sp.dma_start(vw[r:r + m, :, j, :], vws[k0:k0 + m, hd % 2, :, :]).then_inc(s_packs[hd % 2], 16)
                    for q in range(2):
                        sp.wait_ge(s_packs[q], 16 * sent[H - 2 + q])
                    sp.wait_ge(s_row, 16 * B)

        NS = 4
        e = core.sb("xa_e", [P, NS, HL], ctx=ctx)
        pn = core.sb("xa_pn", [P, NS, J * P], ctx=ctx)
        pt = core.sb("xa_pt", [P, 2, J, P], ctx=ctx)
        top, total, inv = (core.sb(f"xa_{q}", [P, NS, H], ctx=ctx) for q in ("top", "total", "inv"))
        sp_ = core.ps("xa_s", [P, 2, 2, 512], ctx)
        pp = core.ps("xa_p", [P, 2, 512], ctx)
        op = core.ps("xa_o", [P, 2, 512], ctx)
        norm = Norm(core, "xa", ctx, None)
        s_counted = core.sem("xa_counted")
        s_s, s_top, s_sub, s_exp, s_sum, s_inv, s_pn, s_pt, s_ptc, s_o, s_x, s_pad = (
            core.sem(f"xa_{q}") for q in ("scores", "top", "sub", "exp", "sum", "inv", "pn", "pt", "ptcopy", "o", "x", "pad"))

        def slot_of(c_odd, pos):
            return (5 * c_odd + pos) % 2

        def s_view(slot):
            return sp_[:, slot, :, 0:HB * L].rearrange("p g (h l) -> p g h l", l=L)

        tiles = [slot_of(u // TPC, (0, 1, 3, 4)[u % TPC]) for u in range(2 * TPC)]

        with nc.Block() as block:
            @block.tensor
            def _(pe):
                norm.turned = sp_[:, 1]
                norm.transpose(pe, 0, 0)

                def step(t, u, lag, c):
                    if lag == 0:
                        j, cs = u % TPC, u // TPC
                        if j == 0:
                            pe.wait_ge(norm.low, c + 1)
                        if j == 3:
                            if isinstance(c, int) and c == NC - 1:
                                pe.wait_ge(s_sub, 4 * c + 1)
                            else:
                                pe.wait_ge(norm.low, c + 2)
                        elif isinstance(c, int) and c == 0 and j < 2:
                            pass
                        elif j < 2:
                            pe.wait_ge(s_sub, t - 1)
                        else:
                            pe.wait_ge(s_sub, t)
                        for g in range(2):
                            for k in range(KD):
                                cols = slice(g * HB * L, (g + 1) * HB * L)
                                xs = [q[:, cs, k, j * P:(j + 1) * P] for q in (norm.xh, norm.xl)]
                                av = [q[:, k].rearrange("p b n -> p (b n)")[:, bass.ds((t - u) * (HL // 8) + g * HB * L, HB * L)]
                                      for q in (ah, al)]
                                ins = mm3(nc, sp_[:, tiles[u], g, 0:HB * L], xs, av, start=(k == 0), stop=(k == KD - 1))
                        ins.then_inc(s_s, 1)
                        if j == 1 and not (isinstance(c, int) and c == NC - 1):
                            pe.wait_ge(s_sub, t)
                            norm.turned = sp_[:, slot_of(cs, 2)]
                            norm.transpose(pe, c + 1, 1 - cs)
                    elif lag == 2:
                        pe.wait_ge(s_pn, t + 1)
                        after(pe, s_ptc, t, 1)
                        for j in range(J):
                            ins = nc.tensor.transpose(pp[:, j // 4, (j % 4) * P:(j % 4 + 1) * P],
                                                      pn[:, u % NS, j * P:(j + 1) * P], core.ident[:])
                        ins.then_inc(s_pt, 1)
                    else:
                        pe.wait_ge(s_ptc, t + 1)
                        after(pe, s_x, t, 2)
                        for j in range(J):
                            rhs = vw[:].rearrange("p b j n -> p (b j n)")[:, bass.ds((t - u) * (J * D // 8) + j * D, D)]
                            ins = nc.tensor.matmul(op[:, u % 2, 0:D], pt[:, u % 2, j, :], rhs, start=(j == 0), stop=(j == J - 1))
                        ins.then_inc(s_o, 1)
                pe.wait_ge(s_pad, 2)
                pipeline(pe, NT, 2 * TPC, [0, 2, 3], step, per=TPC, ahead=True)

            @block.scalar
            def _(a):
                norm.turned = sp_[:, 1]
                norm.take(a, 0, 0)

                def step(t, u, lag, c):
                    if lag == 0:
                        j, cs = u % TPC, u // TPC
                        a.wait_ge(s_sub, t + 1)
                        nc.scalar.activation(e[:, u % NS], e[:, u % NS], ACT.Exp, scale=SCALE).then_inc(s_exp, 1)
                        if j == 1 and not (isinstance(c, int) and c == NC - 1):
                            norm.turned = sp_[:, slot_of(cs, 2)]
                            if not (isinstance(c, int) and c == 0):
                                a.wait_ge(s_s, 4 * c)
                            norm.take(a, c + 1, 1 - cs)
                    else:
                        a.wait_ge(s_pt, t + 1)
                        after(a, s_o, t, 2)
                        nc.scalar.activation(pt[:, u % 2], pp[:].rearrange("p g n -> p (g n)")[:, 0:J * P], ACT.Copy).then_inc(s_ptc, 1)
                pipeline(a, NT, 2 * TPC, [2, 0], step, per=TPC, ahead=True)

            @block.gpsimd
            def _(pool):
                nc.gpsimd.memset(pn[:, :, HL:HL + 1], 1.0).then_inc(s_pad, 1)
                nc.gpsimd.memset(pn[:, :, HL + 1:], 0.0).then_inc(s_pad, 1)

                def step(t, u, lag):
                    pool.wait_ge(s_inv, t + 1)
                    after(pool, s_pt, t, NS)
                    nc.gpsimd.tensor_tensor(pn[:, u % NS, 0:HL].rearrange("p (h l) -> p h l", l=L),
                                            e[:, u % NS].rearrange("p (h l) -> p h l", l=L),
                                            inv[:, u % NS].unsqueeze(2).to_broadcast([P, H, L]), ALU.mult).then_inc(s_pn, 1)
                pipeline(pool, NT, NS, [0], step)

            @block.vector
            def _(v):
                norm.normalise(v, 0, 0)
                norm.turned = sp_[:, 1]
                norm.take_low(v, 0, 0)

                def step(t, u, lag, c):
                    j, cs = u % TPC, u // TPC
                    if lag == 0:
                        last = isinstance(c, int) and c == NC - 1
                        if j == 0 and not last:
                            norm.normalise(v, c + 1, 1 - cs)
                        v.wait_ge(s_s, t + 1)
                        after(v, s_sum, t, NS)
                        nc.vector.tensor_reduce(top[:, u % NS].rearrange("p (g h) -> p g h", h=HB), s_view(tiles[u]),
                                                AX_X, ALU.max).then_inc(s_top, 1)
                        v.wait_ge(s_top, t + 1)
                        after(v, s_pn, t, NS)
                        nc.vector.tensor_tensor(e[:, u % NS].rearrange("p (g h l) -> p g h l", h=HB, l=L), s_view(tiles[u]),
                                                top[:, u % NS].rearrange("p (g h) -> p g h", h=HB).unsqueeze(3).to_broadcast([P, 2, HB, L]),
                                                ALU.subtract).then_inc(s_sub, 1)
                        if j == 1 and not last:
                            norm.turned = sp_[:, slot_of(cs, 2)]
                            norm.take_low(v, c + 1, 1 - cs)
                    elif lag == 1:
                        v.wait_ge(s_exp, t + 1)
                        nc.vector.tensor_reduce(total[:, u % NS], e[:, u % NS].rearrange("p (h l) -> p h l", l=L),
                                                AX_X, ALU.add).then_inc(s_sum, 1)
                        v.wait_ge(s_sum, t + 1)
                        nc.vector.reciprocal(inv[:, u % NS], total[:, u % NS]).then_inc(s_inv, 1)
                    else:
                        v.wait_ge(s_o, t + 1)
                        nc.vector.tensor_tensor(x[:, t, :], op[:, u % 2, 0:D], x[:, t, :], ALU.add).then_inc(s_x, 1)
                        v.wait_ge(s_x, t + 1)
                        nc.vector.bn_stats(core.stats[:, t, :], x[:, t, :]).then_inc(s_counted, 1)
                pipeline(v, NT, 2 * TPC, [4, 0, 1], step, per=TPC, ahead=True)
                v.wait_ge(s_counted, NT)


def gated_chunks(core, w):
    nc, x = core.nc, core.x
    NH, DH, SCAN = 16, 16, 64
    HB = P // DH
    NCK = S // SCAN
    SCALE = DH ** -0.5
    NW = NH * NCK
    PROJ = 8
    with ExitStack() as ctx:
        z = core.sb("gc_z", [P, KD, TOK], ctx=ctx)
        run_x = core.sb("gc_run_x", [P, KD, TOK], ctx=ctx)
        q = core.sb("gc_q", [P, TOK], ctx=ctx)
        lse = core.sb("gc_lse", [P, NT, NH], ctx=ctx)
        ck = core.sb("gc_ck", [P, KD, TOK // SCAN], ctx=ctx)
        woh, wol = (core.sb(f"gc_wo{n}", [P, KD, D], F32R, ctx) for n in "hl")
        head_row = core.sb("gc_head_row", [NH, KD, P], ctx=ctx)
        with ExitStack() as inner:
            wih, wil = (core.sb(f"gc_wi{n}", [P, KD, PROJ * P], F32R, inner) for n in "hl")
            gbias = core.sb("gc_gbias", [P, KD], ctx=inner)
            onep = core.sb("gc_onep", [P, NT], ctx=inner)
            mr = core.sb("gc_mr", [P, NT], ctx=inner)
            with ExitStack() as first:
                rawi = core.sb("gc_rawi", [P, KD, PROJ * P], ctx=first)
                rawo = core.sb("gc_rawo", [P, KD, D], ctx=first)
                rms = core.sb("gc_rms", [P, KD], ctx=first)
                row_stats(core, "gc", rms=True, weights=[(rawi[:], w["W_in"], wih[:], wil[:]), (rawo[:], w["W_out"], woh[:], wol[:])],
                          loads=[(rms[:], w["rms_weight"]), (gbias[:], w["gate_bias"]), (head_row[:], w["head_row"])], scaled=rms)
            g = core.sb("gc_g", [P, KD, CH], ctx=inner)
            vx, vk, rk = (core.sb(f"gc_{n}", [P, KD, CH], ctx=inner) for n in ("vx", "vk", "rk"))
            prod = core.sb("gc_prod", [P, 2, KD, CH], ctx=inner)
            turned = core.ps("gc_turned", [P, KD, CH], inner)
            gz = core.ps("gc_gz", [P, KD, CH], inner)
            xp = core.ps("gc_xp", [P, KD, CH], inner)
            kq = core.ps("gc_kq", [P, 2, CH], inner)
            norm = Norm(core, "gc", inner, turned)
            s_rows, s_xup, s_gp, s_kp, s_xp, s_qp, s_zp, s_g, s_z, s_q, s_vx, s_vk, s_cut, s_rx, s_rk, s_ck, s_prod, s_lse, s_lcopy = (
                core.sem(f"gc_{n}") for n in ("rows", "xup", "gp", "kp", "xp", "qp", "zp", "g", "z", "q", "vx", "vk", "cut",
                                              "rx", "rk", "ck", "prod", "lse", "lcopy"))

            def cols(c):
                return bass.ds(c * CH, CH)

            with nc.Block() as block:
                @block.tensor
                def _(pe):
                    def block_of(out, m, cs):
                        for k in range(KD):
                            ins = mm3(nc, out, [v[:, k, m * P:(m + 1) * P] for v in (wih, wil)],
                                      [v[:, cs, k] for v in (norm.xh, norm.xl)], start=(k == 0), stop=(k == KD - 1))
                        return ins

                    def step(c, u, lag):
                        if lag == 0:
                            after(pe, norm.low, c, 1)
                            after(pe, s_lcopy, c, 3)
                            norm.transpose(pe, c, u)
                        elif lag == 1:
                            pe.wait_ge(norm.low, c + 1)
                            after(pe, s_z, c, 1)
                            block_of(gz[:, 0, :], 4, u)
                            block_of(gz[:, 1, :], 5, u).then_inc(s_gp, 1)
                            after(pe, s_vk, c, 1)
                            block_of(kq[:, 0, :], 7, u).then_inc(s_kp, 1)
                            after(pe, s_vx, c, 1)
                            block_of(xp[:, 0, :], 2, u)
                            block_of(xp[:, 1, :], 3, u).then_inc(s_xp, 1)
                            after(pe, s_q, c, 1)
                            block_of(kq[:, 1, :], 6, u).then_inc(s_qp, 1)
                            pe.wait_ge(s_g, c + 1)
                            block_of(gz[:, 0, :], 0, u)
                            block_of(gz[:, 1, :], 1, u).then_inc(s_zp, 1)
                        else:
                            pe.wait_ge(s_prod, c + 1)
                            after(pe, s_lcopy, c, 1)
                            if isinstance(c, int):
                                pe.wait_ge(norm.low, min(c + 3, NC))
                            else:
                                pe.wait_ge(norm.low, c + 3)
                            for j in range(TPC):
                                for k in range(KD):
                                    ins = nc.tensor.matmul(turned[:, 0, j * NH + k * HB:j * NH + (k + 1) * HB],
                                                           prod[:, u, k, j * P:(j + 1) * P], core.head_of[:], start=True, stop=True)
                            ins.then_inc(s_lse, 1)
                    pipeline(pe, NC, 2, [0, 1, 2], step)

                @block.scalar
                def _(a):
                    def step(c, u, lag):
                        if lag == 0:
                            after(a, s_zp, c, 2)
                            norm.take(a, c, u)
                        else:
                            a.wait_ge(s_gp, c + 1)
                            after(a, s_rk, c, 1)
                            after(a, s_rx, c, 1)
                            for k in range(KD):
                                ins = nc.scalar.activation(g[:, k], gz[:, k, :], ACT.Sigmoid, bias=gbias[:, k:k + 1])
                            ins.then_inc(s_g, 1)
                            a.wait_ge(s_qp, c + 1)
                            nc.scalar.activation(q[:, cols(c)], kq[:, 1, :], ACT.Copy).then_inc(s_q, 1)
                            a.wait_ge(s_zp, c + 1)
                            nc.scalar.activation(z[:, :, cols(c)], gz[:], ACT.Sigmoid).then_inc(s_z, 1)
                    pipeline(a, NC, 2, [0, 1], step)

                @block.gpsimd
                def _(pool):
                    def step(c, u, lag):
                        pool.wait_ge(s_rk, c + 1)
                        pool.wait_ge(s_q, c + 1)
                        after(pool, s_lse, c, 2)
                        nc.gpsimd.tensor_tensor(prod[:, u], rk[:], q[:, cols(c)].unsqueeze(1).to_broadcast([P, KD, CH]),
                                                ALU.mult).then_inc(s_prod, 1)
                    pipeline(pool, NC, 2, [0], step)

                @block.vector
                def _(v):
                    nc.vector.tensor_scalar(onep[:], core.rstd_ln[:], 1.0, None, ALU.add).then_inc(s_rows, 1)
                    nc.vector.scalar_tensor_tensor(out=mr[:], in0=core.mean[:], scalar=-1.0, in1=core.rstd_ln[:],
                                                   op0=ALU.mult, op1=ALU.mult).then_inc(s_rows, 1)
                    v.wait_ge(s_rows, 2)

                    def step(c, u, lag):
                        if lag == 0:
                            norm.normalise(v, c, u)
                            v.wait_ge(norm.normed, c + 1)
                            for j in range(TPC):
                                t = c * TPC + j
                                nc.vector.tensor_scalar(x[:, t, :], x[:, t, :], onep[:, bass.ds(t, 1)], mr[:, bass.ds(t, 1)],
                                                        ALU.mult, ALU.add).then_inc(s_xup, 1)
                            norm.take_low(v, c, u)
                        elif lag == 1:
                            v.wait_ge(s_g, c + 1)
                            v.wait_ge(s_kp, c + 1)
                            after(v, s_rk, c, 1)
                            after(v, s_rx, c, 1)
                            nc.vector.scalar_tensor_tensor(out=vk[:], in0=g[:], scalar=1.0,
                                                           in1=kq[:, 0, :].unsqueeze(1).to_broadcast([P, KD, CH]),
                                                           op0=ALU.subtract, op1=ALU.mult).then_inc(s_vk, 1)
                            v.wait_ge(s_xp, c + 1)
                            nc.vector.scalar_tensor_tensor(out=vx[:], in0=g[:], scalar=1.0, in1=xp[:],
                                                           op0=ALU.subtract, op1=ALU.mult).then_inc(s_vx, 1)
                            v.wait_ge(s_vk, c + 1)
                            v.wait_ge(s_vx, c + 1)
                            nc.vector.memset(g[:].rearrange("p k (n s) -> p k n s", s=SCAN)[:, :, :, 0:1], 0.0).then_inc(s_cut, 1)
                            v.wait_ge(s_cut, c + 1)
                            after(v, s_prod, c, 1)
                            after(v, s_ck, c, 1)
                            nc.vector.tensor_tensor_scan(rk[:].rearrange("p k n -> p (k n)"), g[:].rearrange("p k n -> p (k n)"),
                                                         vk[:].rearrange("p k n -> p (k n)"), 0.0, ALU.mult, ALU.subtract).then_inc(s_rk, 1)
                            for k in range(KD):
                                ins = nc.vector.tensor_tensor_scan(run_x[:, k, cols(c)], g[:, k], vx[:, k], 0.0, ALU.mult, ALU.subtract)
                            ins.then_inc(s_rx, 1)
                            v.wait_ge(s_rk, c + 1)
                            nc.vector.tensor_copy(ck[:, :, bass.ds(c * (CH // SCAN), CH // SCAN)],
                                                  rk[:].rearrange("p k (n s) -> p k n s", s=SCAN)[:, :, :, 0]).then_inc(s_ck, 1)
                        else:
                            v.wait_ge(s_lse, c + 1)
                            nc.vector.tensor_copy(lse[:, bass.ds(c * TPC, TPC), :],
                                                  turned[:, 0, 0:TPC * NH].rearrange("p (j h) -> p j h", h=NH)).then_inc(s_lcopy, 1)
                    pipeline(v, NC, 2, [0, 1, 2], step)

        kb = core.sb("gc_kb", [P, B, KD, HB * NCK], ctx=ctx)
        xb = core.sb("gc_xb", [P, B, KD, P], ctx=ctx)
        maskb = core.sb("gc_maskb", [P, S // P, NCK], ctx=ctx)
        with ExitStack() as inner:
            xpre = core.sb("gc_xpre", [P, B, KD, P], ctx=inner)
            bp = core.ps("gc_bp", [P, B * KD, P], inner)
            s_kb, s_xpre, s_bp, s_xb, s_mask = (core.sem(f"gc_{n}") for n in ("kb", "xpre", "bp", "xb", "mask"))
            with nc.Block() as block:
                @block.vector
                def _(v):
                    heads = core.head_of[:].unsqueeze(2).to_broadcast([P, HB, NCK])
                    for b in range(B):
                        for k in range(KD):
                            first_rows = run_x[:, k, b * S:(b + 1) * S].rearrange("p (n s) -> p n s", s=SCAN)[:, :, 0]
                            nc.vector.tensor_tensor(xpre[:, b, k].rearrange("p (h n) -> p h n", h=HB),
                                                    first_rows.unsqueeze(1).to_broadcast([P, HB, NCK]), heads, ALU.mult).then_inc(s_xpre, 1)
                    for b in range(B):
                        for k in range(KD):
                            nc.vector.tensor_tensor(kb[:, b, k].rearrange("p (h n) -> p h n", h=HB),
                                                    ck[:, k, b * NCK:(b + 1) * NCK].unsqueeze(1).to_broadcast([P, HB, NCK]),
                                                    heads, ALU.mult).then_inc(s_kb, 1)
                    v.wait_ge(s_kb, B * KD)

                @block.tensor
                def _(pe):
                    for m in range(B * KD):
                        pe.wait_ge(s_xpre, m + 1)
                        ins = nc.tensor.transpose(bp[:, m, :], xpre[:, m // KD, m % KD, :], core.ident[:])
                    ins.then_inc(s_bp, 1)

                @block.scalar
                def _(a):
                    a.wait_ge(s_bp, 1)
                    nc.scalar.activation(xb[:].rearrange("p b k n -> p (b k) n"), bp[:], ACT.Copy).then_inc(s_xb, 1)
                    a.wait_ge(s_xb, 1)

                @block.gpsimd
                def _(pool):
                    nc.gpsimd.memset(maskb[:], 0.0).then_inc(s_mask, 1)
                    pool.wait_ge(s_mask, 1)
                    for half in range(P // SCAN):
                        rows = slice(half * SCAN, (half + 1) * SCAN)
                        nc.gpsimd.affine_select(out=maskb[rows], in_=maskb[rows], compare_op=ALU.is_gt, fill=-1e30, base=half,
                                                pattern=[[P // SCAN, S // P], [-1, NCK]], channel_multiplier=0).then_inc(s_mask, 1)
                    pool.wait_ge(s_mask, 3)

        qs = core.sb("gc_qs", [P, 2, CH], ctx=ctx)
        wt = core.sb("gc_wt", [P, 2, TPC, NW + NH], ctx=ctx)
        wn = core.sb("gc_wn", [P, 2, TPC, NW + NH], ctx=ctx)
        top, total, inv = (core.sb(f"gc_{n}", [P, 2, TPC, NH], ctx=ctx) for n in ("top", "total", "inv"))
        wts = core.sb("gc_wts", [P, KD, CH], ctx=ctx)
        wis = core.sb("gc_wis", [NH, CH], ctx=ctx)
        xcur = core.sb("gc_xcur", [P, KD, P], ctx=ctx)
        y1, y2 = (core.sb(f"gc_{n}", [P, KD, CH], ctx=ctx) for n in ("y1", "y2"))
        yh, yl = (core.sb(f"gc_{n}", [P, 2, KD, CH], F32R, ctx) for n in ("yh", "yl"))
        s_counted = core.sem("gb_counted")
        sr = core.ps("gc_sr", [P, 2, CH], ctx)
        wo_ = core.ps("gc_wo_", [P, 2, CH], ctx)
        wip = core.ps("gc_wip", [NH, CH], ctx)
        op = core.ps("gc_op", [P, KD, CH], ctx)
        (s_qs, s_s, s_mk, s_m1, s_top, s_sub, s_exp, s_t1, s_sum, s_inv, s_wn, s_wnl, s_wt, s_wtc, s_xc, s_r, s_o, s_y1, s_y2,
         s_y, s_yh, s_yl, s_out, s_x) = (core.sem(f"gb_{n}") for n in (
             "qs", "s", "mask", "m1", "top", "sub", "exp", "t1", "sum", "inv", "wn", "wnl", "wt", "wtc", "xcur", "r", "o",
             "y1", "y2", "y", "yh", "yl", "out", "x"))

        def heads(v, n=NCK):
            return v.rearrange("p j (h n) -> p j h n", n=n)

        with nc.Block() as block:
            @block.gpsimd
            def _(pool):
                def step(c, u, lag):
                    if lag[1] == "query":
                        after(pool, s_s, c, 2)
                        nc.gpsimd.tensor_copy(qs[:, u], q[:, bass.ds(c * CH, CH)]).then_inc(s_qs, 1)
                    else:
                        pool.wait_ge(s_inv, c + 1)
                        after(pool, s_wt, c, 2)
                        nc.gpsimd.tensor_tensor(heads(wn[:, u, :, 0:NW]), heads(wt[:, u, :, 0:NW]),
                                                inv[:, u].unsqueeze(3).to_broadcast([P, TPC, NH, NCK]), ALU.mult).then_inc(s_wn, 1)
                pipeline(pool, NC, 2, [(0, "query"), (1, "divide")], step)

            @block.tensor
            def _(pe):
                def step(c, u, lag, b):
                    if lag[1] == "scores":
                        pe.wait_ge(s_qs, c + 1)
                        after(pe, s_mk, c, 1)
                        after(pe, s_x, c, 3)
                        for j in range(TPC):
                            ins = nc.tensor.matmul(sr[:, j // 2, (j % 2) * NW:(j % 2 + 1) * NW], qs[:, u, j * P:(j + 1) * P],
                                                   kb[:].rearrange("p b k n -> p (b k n)")[:, bass.ds(b * NW, NW)], start=True, stop=True)
                        ins.then_inc(s_s, 1)
                    elif lag[1] == "turn":
                        pe.wait_ge(s_wn, c + 1)
                        pe.wait_ge(s_wnl, c + 1)
                        after(pe, s_wtc, c, 1)
                        after(pe, s_y1, c, 1)
                        for j in range(TPC):
                            for k in range(KD):
                                nc.tensor.transpose(wo_[:, k, j * P:(j + 1) * P], wn[:, u, j, k * P:(k + 1) * P], core.ident[:])
                            ins = nc.tensor.transpose(wip[:, j * P:(j + 1) * P], wn[:, u, j, NW:NW + NH], core.ident[:])
                        ins.then_inc(s_wt, 1)
                    elif lag[1] == "products":
                        pe.wait_ge(s_wtc, c + 1)
                        for k in range(KD):
                            ins = nc.tensor.matmul(wo_[:, k, :], head_row[:, k, :], wis[:], start=True, stop=True)
                        ins.then_inc(s_r, 1)
                        after(pe, s_y2, c, 1)
                        pe.wait_ge(s_xc, b + 1)
                        for k in range(KD):
                            ins = nc.tensor.matmul(op[:, k, :], xcur[:, k, :], wts[:, k, :], start=True, stop=True)
                        ins.then_inc(s_o, 1)
                    else:
                        pe.wait_ge(s_yl, c + 1)
                        pe.wait_ge(s_mk, min(c + 3, NC) if isinstance(c, int) else c + 3)
                        for j in range(TPC):
                            for k in range(KD):
                                ins = mm3(nc, sr[:, j // 2, (j % 2) * D:(j % 2 + 1) * D], [v[:, u, k, j * P:(j + 1) * P] for v in (yh, yl)],
                                          (woh[:, k, :], wol[:, k, :]), start=(k == 0), stop=(k == KD - 1))
                        ins.then_inc(s_out, 1)
                pipeline(pe, NC, 2, [(0, "scores"), (1, "turn"), (1, "products"), (2, "out")], step, per=2)

            @block.scalar
            def _(a):
                def step(c, u, lag, b):
                    if lag[1] == "exp":
                        a.wait_ge(s_sub, 2 * c + 2)
                        nc.scalar.activation(wt[:, u], wt[:, u], ACT.Exp, scale=SCALE).then_inc(s_exp, 1)
                    elif lag[1] == "weights":
                        if u == 0:
                            after(a, s_o, c, 1)
                            nc.scalar.activation(xcur[:].rearrange("p k n -> p (k n)"),
                                                 xb[:].rearrange("p b k n -> p (b k n)")[:, bass.ds(b * (KD * P), KD * P)],
                                                 ACT.Copy).then_inc(s_xc, 1)
                        a.wait_ge(s_wt, c + 1)
                        after(a, s_o, c, 1)
                        nc.scalar.activation(wis[:], wip[:], ACT.Copy)
                        nc.scalar.activation(wts[:], wo_[:], ACT.Copy).then_inc(s_wtc, 1)
                    else:
                        a.wait_ge(s_y, c + 1)
                        after(a, s_out, c, 2)
                        nc.scalar.activation(yh[:, u], y2[:], ACT.Copy).then_inc(s_yh, 1)
                pipeline(a, NC, 2, [(1, "weights"), (0, "exp"), (1, "high")], step, per=2)

            @block.vector
            def _(v):
                def step(c, u, lag):
                    cols = bass.ds(c * CH, CH)
                    if lag[1] == "scores":
                        l = lse[:, bass.ds(c * TPC, TPC), :]
                        v.wait_ge(s_s, c + 1)
                        after(v, s_wn, c, 2)
                        after(v, s_wnl, c, 2)
                        for half in range(2):
                            tiles = slice(half * 2, half * 2 + 2)
                            m = maskb[:, u * TPC + half * 2:u * TPC + half * 2 + 2, :].unsqueeze(2).to_broadcast([P, 2, NH, NCK])
                            ins = nc.vector.tensor_tensor(heads(wt[:, u, tiles, 0:NW]),
                                                          heads(sr[:, half, :].rearrange("p (j n) -> p j n", j=2)), m, ALU.add)
                        ins.then_inc(s_mk, 1)
                        v.wait_ge(s_mk, c + 1)
                        nc.vector.tensor_reduce(top[:, u], heads(wt[:, u, :, 0:NW]), AX_X, ALU.max).then_inc(s_m1, 1)
                        v.wait_ge(s_m1, c + 1)
                        nc.vector.tensor_tensor(top[:, u], top[:, u], l, ALU.max).then_inc(s_top, 1)
                        v.wait_ge(s_top, c + 1)
                        nc.vector.tensor_tensor(heads(wt[:, u, :, 0:NW]), heads(wt[:, u, :, 0:NW]),
                                                top[:, u].unsqueeze(3).to_broadcast([P, TPC, NH, NCK]), ALU.subtract).then_inc(s_sub, 1)
                        nc.vector.tensor_tensor(wt[:, u, :, NW:], l, top[:, u], ALU.subtract).then_inc(s_sub, 1)
                    elif lag[1] == "sum":
                        v.wait_ge(s_exp, c + 1)
                        nc.vector.tensor_reduce(total[:, u], heads(wt[:, u, :, 0:NW]), AX_X, ALU.add).then_inc(s_t1, 1)
                        v.wait_ge(s_t1, c + 1)
                        nc.vector.tensor_tensor(total[:, u], total[:, u], wt[:, u, :, NW:], ALU.add).then_inc(s_sum, 1)
                        v.wait_ge(s_sum, c + 1)
                        nc.vector.reciprocal(inv[:, u], total[:, u]).then_inc(s_inv, 1)
                        v.wait_ge(s_inv, c + 1)
                        after(v, s_wt, c, 2)
                        nc.vector.tensor_tensor(wn[:, u, :, NW:], wt[:, u, :, NW:], inv[:, u], ALU.mult).then_inc(s_wnl, 1)
                    elif lag[1] == "mix":
                        v.wait_ge(s_r, c + 1)
                        nc.vector.tensor_tensor(y1[:], wo_[:], run_x[:, :, cols], ALU.mult).then_inc(s_y1, 1)
                        v.wait_ge(s_o, c + 1)
                        v.wait_ge(s_y1, c + 1)
                        nc.vector.tensor_tensor(y1[:], op[:], y1[:], ALU.add).then_inc(s_y2, 1)
                        v.wait_ge(s_y2, c + 1)
                        after(v, s_yl, c, 1)
                        nc.vector.tensor_tensor(y2[:], y1[:], z[:, :, cols], ALU.mult).then_inc(s_y, 1)
                    elif lag[1] == "low":
                        v.wait_ge(s_yh, c + 1)
                        nc.vector.tensor_tensor(yl[:, u], y2[:], yh[:, u].bitcast(F32), ALU.subtract).then_inc(s_yl, 1)
                    else:
                        v.wait_ge(s_out, c + 1)
                        xv = x[:, bass.ds(c * TPC, TPC), :]
                        nc.vector.tensor_tensor(xv, sr[:].rearrange("p g (j n) -> p (g j) n", n=D), xv, ALU.add).then_inc(s_x, 1)
                        v.wait_ge(s_x, c + 1)
                        for j in range(TPC):
                            t = c * TPC + j
                            nc.vector.bn_stats(core.stats[:, t, :], x[:, t, :]).then_inc(s_counted, 1)
                pipeline(v, NC, 2, [(0, "scores"), (0, "sum"), (1, "mix"), (2, "add"), (1, "low")], step)
                v.wait_ge(s_counted, NT)


def linear_attention(core, w):
    nc, x = core.nc, core.x
    NH, DH = 16, 16
    TPS = S // P
    FILLS = 4
    with ExitStack() as ctx:
        wqk = [core.sb(f"la_wqk{n}", [P, KD, 2 * D], F32R, ctx) for n in "hl"]
        wkv = [core.sb(f"la_wkv{n}", [P, KD, 2 * D], F32R, ctx) for n in "hl"]
        wn = [core.sb(f"la_wn{n}", [P, KD, NH], F32R, ctx) for n in "hl"]
        wo = core.sb("la_wo", [P, KD, D], ctx=ctx)
        bq = core.sb("la_bq", [P, KD], ctx=ctx)
        bk = core.sb("la_bk", [P, KD], ctx=ctx)
        bkv = core.sb("la_bkv", [P, 2 * D], ctx=ctx)
        bn = core.sb("la_bn", [NH, 1], ctx=ctx)
        bo = core.sb("la_bo", [P, D], ctx=ctx)
        tri = core.sb("la_tri", [P, P], ctx=ctx)
        same = core.sb("la_same", [P, P], ctx=ctx)
        with ExitStack() as inner:
            rqk, rkv = (core.sb(f"la_raw{n}", [P, KD, 2 * D], ctx=inner) for n in ("qk", "kv"))
            rn_ = core.sb("la_rawn", [P, KD, NH], ctx=inner)
            row_stats(core, "la", weights=[(rqk[:], w["Wqk"], wqk[0][:], wqk[1][:]), (rkv[:], w["Wkv"], wkv[0][:], wkv[1][:]),
                                           (rn_[:], w["Wn"], wn[0][:], wn[1][:])],
                      loads=[(wo[:], w["Wo"]), (bq[:], w["bq"]), (bk[:], w["bk"]), (bkv[:], w["bkv"].partition_broadcast(P)),
                             (bn[:], w["bn"]), (bo[:], w["bo"].partition_broadcast(P))],
                      ones=[tri[:]])
        HB = P // DH
        qT = core.sb("la_qT", [P, 2, KD, CH], ctx=ctx)
        qm = core.sb("la_qm", [P, 2, KD, HB, CH], ctx=ctx)
        kT = core.sb("la_kT", [P, 2, KD, CH], ctx=ctx)
        kv = core.sb("la_kv", [P, 2, TPC, 2 * D], ctx=ctx)
        rnT = core.sb("la_rnT", [NH, CH], ctx=ctx)
        rn = core.sb("la_rn", [P, 2, TPC, NH], ctx=ctx)
        am = core.sb("la_am", [P, 2, FILLS, CH], ctx=ctx)
        sraw = core.sb("la_sraw", [P, KD, P], ctx=ctx)
        sblk = core.sb("la_sblk", [P, KD, P], ctx=ctx)
        cn = core.sb("la_cn", [P, 2, D], ctx=ctx)
        yT = core.sb("la_yT", [P, 2, KD, P], ctx=ctx)
        proj = core.ps("la_proj", [P, 2, CH], ctx)
        sc = core.ps("la_sc", [P, 2, CH], ctx)
        cp = core.ps("la_cp", [P, 2, CH], ctx)
        st = core.ps("la_st", [P, CH], ctx)
        yo = core.ps("la_yo", [P, CH], ctx)
        norm = Norm(core, "la", ctx, proj)
        s_counted = core.sem("la_counted")
        (s_made, s_qk, s_qke, s_qp, s_kv, s_kvb, s_n, s_rnT, s_rt, s_rn, s_nbn, s_sc, s_am, s_c, s_st, s_sr, s_sb, s_cn, s_yT, s_yTc, s_o, s_x, s_xb) = (
            core.sem(f"la_{n}") for n in ("made", "qk", "qkcopy", "qpar", "kv", "kvbias", "n", "rnT", "rnturn", "rn", "negbn", "sc", "am", "c", "st", "sraw",
                                          "sblk", "cn", "yT", "yTcopy", "o", "x", "xbias"))

        with nc.Block() as block:
            @block.tensor
            def _(pe):
                def prepare(part, c, s):
                    xs = (norm.xh, norm.xl)

                    def qk(m):
                        if m >= 2:
                            pe.wait_ge(s_qke, 4 * c + m - 1)
                        col = (m % 2) * D + (m // 2) * P
                        for k in range(KD):
                            ins = mm3(nc, proj[:, m % 2, :], [v[:, k, col:col + P] for v in wqk],
                                      [v[:, s, k] for v in xs], start=(k == 0), stop=(k == KD - 1))
                        ins.then_inc(s_qk, 1)

                    def kv_rows(j):
                        bank = (0, 1, 0, 0)[j]
                        if j < 2:
                            pe.wait_ge(s_qke, 4 * c + j + 3)
                        else:
                            pe.wait_ge(s_kvb, 4 * c + (j - 1 if j == 2 else 3))
                        for k in range(KD):
                            ins = mm3(nc, proj[:, bank, :], [v[:, s, k, j * P:(j + 1) * P] for v in xs],
                                      [v[:, k] for v in wkv], start=(k == 0), stop=(k == KD - 1))
                        ins.then_inc(s_kv, 1)

                    if part == 0:
                        after(pe, s_rn, c, 1)
                        after(pe, s_kvb, c, 1, TPC)
                        norm.transpose(pe, c, s)
                    elif part in (1, 2):
                        if part == 1:
                            pe.wait_ge(norm.low, c + 1)
                        qk(2 * part - 2)
                        qk(2 * part - 1)
                    elif part < 6:
                        kv_rows(part - 3)
                    elif part == 6:
                        pe.wait_ge(s_kvb, 4 * c + 2)
                        for k in range(KD):
                            ins = mm3(nc, proj[0:NH, 1, :], [v[:, k] for v in wn], [v[:, s, k] for v in xs],
                                      start=(k == 0), stop=(k == KD - 1))
                        ins.then_inc(s_n, 1)
                    else:
                        pe.wait_ge(s_rnT, c + 1)
                        kv_rows(3)
                        for j in range(TPC):
                            ins = nc.tensor.transpose(proj[:, 1, j * NH:(j + 1) * NH], rnT[:, j * P:(j + 1) * P],
                                                      core.ident[0:NH, 0:NH])
                        ins.then_inc(s_rt, 1)

                def context(t, u, j, cs, fills):
                    for f in fills:
                        pe.wait_ge(s_am, 4 * t + f + 1)
                        for q in range(4):
                            h = 8 * (q // 2) + 2 * f + q % 2
                            ins = nc.tensor.matmul(cp[:, u % 2, h * DH:(h + 1) * DH], am[:, u % 2, f, q * P:(q + 1) * P],
                                                   kv[:, cs, j, D + h * DH:D + (h + 1) * DH], start=(u == 0 and h == 0),
                                                   stop=(h == NH - 1), skip_group_check=True)
                    return ins

                def step(t, u, lag, c):
                    j, cs = u % TPC, u // TPC
                    tile = slice(j * P, (j + 1) * P)
                    if lag[1] in ("scores01", "scores23"):
                        if j == 0 and lag[1] == "scores01":
                            pe.wait_ge(s_qp, KD * (c + 1))
                        fs = (0, 1) if lag[1] == "scores01" else (2, 3)
                        for f in fs:
                            if isinstance(t, int) and 4 * t + f < 2:
                                pass
                            else:
                                pe.wait_ge(s_am, 4 * t + f - 1)
                        for k in range(KD):
                            for f in fs:
                                ins = nc.tensor.matmul(sc[:, f % 2, k * 256:(k + 1) * 256], kT[:, cs, k, tile],
                                                       qm[:, cs, k, 2 * f:2 * f + 2, tile], start=True, stop=True)
                                if k == KD - 1:
                                    ins.then_inc(s_sc, 1)
                    elif lag[1] == "turn":
                        pe.wait_ge(s_cn, t + 1)
                        after(pe, s_x, t, 1)
                        for k in range(KD):
                            ins = nc.tensor.transpose(yo[:, k * P:(k + 1) * P], cn[:, u % 2, k * P:(k + 1) * P], core.ident[:])
                        ins.then_inc(s_yT, 1)
                    elif lag[1] in ("prepare0", "prepare1"):
                        if not (isinstance(c, int) and c == NC - 1):
                            prepare(2 * j + int(lag[1][-1]), c + 1, 1 - cs)
                    elif lag[1] == "context01":
                        if j == 0:
                            pe.wait_ge(s_kvb, 4 * c + 4)
                        after(pe, s_cn, t, 2)
                        if u:
                            pe.wait_ge(s_sb, t)
                            for k in range(KD):
                                nc.tensor.matmul(cp[:, u % 2, k * P:(k + 1) * P], qT[:, cs, k, tile], sblk[:, k, :],
                                                 start=(k == 0), stop=False, skip_group_check=True)
                        context(t, u, j, cs, (0, 1))
                    elif lag[1] == "context23":
                        context(t, u, j, cs, (2, 3)).then_inc(s_c, 1)
                        after(pe, s_sr, t, 1)
                        for k in range(KD):
                            ins = nc.tensor.matmul(st[:, k * P:(k + 1) * P], kv[:, cs, j, k * P:(k + 1) * P],
                                                   kv[:, cs, j, D + k * P:D + (k + 1) * P], start=True, stop=True)
                        ins.then_inc(s_st, 1)
                    else:
                        pe.wait_ge(s_yTc, t + 1)
                        for k in range(KD):
                            ins = nc.tensor.matmul(yo[:, 0:D], yT[:, u % 2, k, :], wo[:, k, :], start=(k == 0), stop=(k == KD - 1))
                        ins.then_inc(s_o, 1)

                for part in range(8):
                    prepare(part, 0, 0)
                pipeline(pe, NT, TPS, [(1, "context01"), (0, "scores01"), (0, "prepare0"), (1, "context23"), (2, "turn"),
                                       (0, "scores23"), (0, "prepare1"), (2, "out")], step, per=TPC, ahead=True)

            @block.scalar
            def _(a):
                def prepare(part, c, s):
                    if part == 0:
                        after(a, s_n, c, 2)
                        norm.take(a, c, s)
                    elif part in (1, 2):
                        if part == 1:
                            after(a, s_st, c, 2, TPC)
                        k = part - 1
                        for m in (0, 1):
                            a.wait_ge(s_qk, 4 * c + 2 * k + m + 1)
                            to, bias = ((qT[:, s, k], bq), (kT[:, s, k], bk))[m]
                            nc.scalar.activation(to, proj[:, m, :], ACT.Identity, bias=bias[:, k:k + 1]).then_inc(s_qke, 1)
                        a.wait_ge(s_qke, 4 * c + 2 * k + 1)
                        for h in range(HB):
                            ins = nc.scalar.activation(qm[:, s, k, h], qT[:, s, k], ACT.Copy, scale=core.head_of[:, h:h + 1])
                        ins.then_inc(s_qp, 1)
                    elif part == 6:
                        a.wait_ge(s_n, c + 1)
                        after(a, s_rt, c, 1)
                        nc.scalar.activation(rnT[:], proj[0:NH, 1, :], ACT.Exp, scale=-1.0, bias=bn[:]).then_inc(s_rnT, 1)
                    elif part == 7:
                        a.wait_ge(s_rt, c + 1)
                        after(a, s_cn, c, 2, TPC)
                        nc.scalar.activation(rn[:, s].rearrange("p j h -> p (j h)"), proj[:, 1, 0:TPC * NH], ACT.Copy).then_inc(s_rn, 1)

                def step(t, u, lag, c):
                    j, cs = u % TPC, u // TPC
                    if lag[1] != "out":
                        if not (isinstance(c, int) and c == NC - 1):
                            prepare(2 * j + lag[1], c + 1, 1 - cs)
                    else:
                        a.wait_ge(s_yT, t + 1)
                        after(a, s_o, t, 2)
                        nc.scalar.activation(yT[:, u % 2].rearrange("p k n -> p (k n)"), yo[:, 0:D], ACT.Copy).then_inc(s_yTc, 1)
                nc.scalar.activation(bn[:], bn[:], ACT.Copy, scale=-1.0).then_inc(s_nbn, 1)
                a.wait_ge(s_nbn, 1)
                a.wait_ge(s_made, 2)
                for part in range(8):
                    prepare(part, 0, 0)
                pipeline(a, NT, TPS, [(0, 0), (2, "out"), (0, 1)], step, per=TPC, ahead=True)

            @block.gpsimd
            def _(pool):
                nc.gpsimd.affine_select(out=tri[:], in_=tri[:], compare_op=ALU.is_ge, fill=0.0, base=0,
                                        pattern=[[1, P]], channel_multiplier=-1).then_inc(s_made, 1)
                nc.gpsimd.tensor_copy(same[:].rearrange("p (h d) -> p h d", d=DH),
                                      core.head_of[:].unsqueeze(2).to_broadcast([P, P // DH, DH])).then_inc(s_made, 1)
                pool.wait_ge(s_made, 2)

                def pstep(t, u, lag, c):
                    if lag == 0:
                        if u % TPC == 0:
                            pool.wait_ge(norm.normed, c + 1)
                        nc.gpsimd.tensor_tensor(x[:, t, :], x[:, t, :], bo[:], ALU.add).then_inc(s_xb, 1)
                    else:
                        pool.wait_ge(s_sr, t + 1)
                        pool.wait_ge(s_c, t + 1)
                        nc.gpsimd.tensor_tensor(sblk[:], sraw[:], same[:].unsqueeze(1).to_broadcast([P, KD, P]),
                                                ALU.mult).then_inc(s_sb, 1)
                pipeline(pool, NT, TPS, [0, 1], pstep, per=TPC)

            @block.vector
            def _(v):
                def prepare(part, c, s):
                    if part == 0:
                        norm.take_low(v, c, s)
                    elif part in (3, 4, 5, 7):
                        j = min(part - 3, 3)
                        v.wait_ge(s_kv, 4 * c + j + 1)
                        after(v, s_st, c, 2, TPC)
                        nc.vector.tensor_tensor(kv[:, s, j], proj[:, (0, 1, 0, 0)[j], :], bkv[:], ALU.add).then_inc(s_kvb, 1)

                def mask(t, u, f):
                    v.wait_ge(s_sc, 4 * t + f + 1)
                    if f == 0:
                        after(v, s_c, t, 2)
                    nc.vector.tensor_tensor(am[:, u % 2, f].rearrange("p (h n) -> p h n", n=P),
                                            sc[:, f % 2, :].rearrange("p (h n) -> p h n", n=P),
                                            tri[:].unsqueeze(1).to_broadcast([P, 4, P]), ALU.mult).then_inc(s_am, 1)

                def step(t, u, lag, c):
                    j, cs = u % TPC, u // TPC
                    last = isinstance(c, int) and c == NC - 1
                    if lag[1] == "mask01":
                        mask(t, u, 0)
                        mask(t, u, 1)
                    elif lag[1] == "mask23":
                        mask(t, u, 2)
                        mask(t, u, 3)
                        if j == 3 and not (isinstance(c, int) and c >= NC - 2):
                            norm.normalise(v, c + 2, cs)
                    elif lag[1] == "state":
                        v.wait_ge(s_st, t + 1)
                        after(v, s_sb, t, 1)
                        sp_ = st[:, 0:D].rearrange("p (k n) -> p k n", k=KD)
                        if u == 0:
                            nc.vector.tensor_copy(sraw[:], sp_).then_inc(s_sr, 1)
                        else:
                            nc.vector.tensor_tensor(sraw[:], sp_, sraw[:], ALU.add).then_inc(s_sr, 1)
                        v.wait_ge(s_c, t + 1)
                        if j == 0:
                            v.wait_ge(s_rn, c + 1)
                        after(v, s_yT, t, 2)
                        nc.vector.tensor_tensor(cn[:, u % 2].rearrange("p (h d) -> p h d", d=DH),
                                                cp[:, u % 2, 0:D].rearrange("p (h d) -> p h d", d=DH),
                                                rn[:, cs, j].unsqueeze(2).to_broadcast([P, NH, DH]), ALU.mult).then_inc(s_cn, 1)
                    elif lag[1] in ("prepare0", "prepare1"):
                        if not last:
                            prepare(2 * j + int(lag[1][-1]), c + 1, 1 - cs)
                    else:
                        v.wait_ge(s_o, t + 1)
                        v.wait_ge(s_xb, t + 1)
                        nc.vector.tensor_tensor(x[:, t, :], yo[:, 0:D], x[:, t, :], ALU.add).then_inc(s_x, 1)
                        v.wait_ge(s_x, t + 1)
                        nc.vector.bn_stats(core.stats[:, t, :], x[:, t, :]).then_inc(s_counted, 1)
                norm.normalise(v, 0, 0)
                norm.normalise(v, 1, 1)
                v.wait_ge(s_made, 2)
                for part in range(8):
                    prepare(part, 0, 0)
                pipeline(v, NT, TPS, [(0, "mask01"), (0, "prepare0"), (1, "state"), (0, "prepare1"), (0, "mask23"), (2, "add")], step,
                         per=TPC, ahead=True)
                v.wait_ge(s_counted, NT)


def lora_attention(core, w):
    nc, x = core.nc, core.x
    NH, DH, L, RANK = 16, 16, w["ctxT"].shape[-1] // B, 16
    HH = NH // 2
    HB = 4
    HL = HH * L
    J = -(-HL // P)
    VW = DH + 1
    VJ = 52
    SCALE = DH ** -0.5
    TPS = S // P
    with ExitStack() as ctx:
        wq = [core.sb(f"lo_wq{n}", [P, KD, D], F32R, ctx) for n in "hl"]
        wp = core.sb("lo_wp", [P, KD, D], ctx=ctx)
        kb = [core.sb(f"lo_kb{n}", [P, B, 2, HL], F32R, ctx) for n in "hl"]
        vp = core.sb("lo_vp", [P, B, 2 * J, VJ], ctx=ctx)
        bq = core.sb("lo_bq", [P, KD], ctx=ctx)
        bp = core.sb("lo_bp", [P, D], ctx=ctx)
        causal = core.sb("lo_causal", [P, HB, L], ctx=ctx)
        parts = []
        for h in range(NH):
            k0 = 0
            while k0 < L:
                r = h % HH * L + k0
                m = min(L - k0, P - r % P)
                parts.append((h, k0, m, h // HH * J + r // P, r % P))
                k0 += m
        heads_of = [sorted({q[0] for q in parts if q[3] == j}) for j in range(2 * J)]
        v1 = core.sb("lo_v1", [L, B, NH, VW], ctx=ctx)
        with ExitStack() as inner:
            ctxT = core.sb("lo_ctxT", [P, KD, B * L], ctx=inner)
            raw = core.sb("lo_raw", [P, KD, 4 * D], ctx=inner)
            aT = core.sb("lo_a", [RANK, 3, D], ctx=inner)
            bT = core.sb("lo_b", [RANK, 4 * D], ctx=inner)
            weff = core.sb("lo_weff", [P, KD, 4 * D], ctx=inner)
            bfk = core.sb("lo_bfk", [P, KD], ctx=inner)
            bfv = core.sb("lo_bfv", [L, D], ctx=inner)
            kT = core.sb("lo_kT", [P, KD, B * L], ctx=inner)
            kblk = core.sb("lo_kblk", [P, 2, HL], ctx=inner)
            row_stats(core, "lo", loads=[(ctxT[:], w["ctxT"]), (raw[:], w["W"]), (aT[:], w["A"]), (bT[:], w["B"]), (bfk[:], w["bfk"]),
                                         (bfv[:], w["bfv"].partition_broadcast(L)), (bq[:], w["bq"]),
                                         (bp[:], w["bp"].partition_broadcast(P))],
                      zeros=[vp[:], causal[:]], ones=[v1[:]])
            lp = core.ps("lo_lp", [P, 2, 512], inner)
            kp = core.ps("lo_kp", [P, KD, 512], inner)
            vps = core.ps("lo_vps", [P, 2, 512], inner)
            s_lp, s_w, s_wh, s_wl, s_kp, s_kT, s_kb, s_kh, s_kl, s_vp, s_v, s_pack, s_causal = (
                core.sem(f"lo_{n}") for n in ("lp", "w", "wh", "wl", "kp", "kT", "kb", "kh", "kl", "vp", "v", "pack", "causal"))
            with nc.Block() as block:
                @block.tensor
                def _(pe):
                    for m in range(4 * KD):
                        part, k = m // KD, m % KD
                        after(pe, s_w, m, 2)
                        nc.tensor.matmul(lp[:, m % 2, 0:D], aT[:, (0, 1, 1, 2)[part], k * P:(k + 1) * P],
                                         bT[:, part * D:(part + 1) * D], start=True, stop=True).then_inc(s_lp, 1)
                    for g in range(KD):
                        pe.wait_ge(s_w, 2 * KD)
                        for k in range(KD):
                            ins = nc.tensor.matmul(kp[:, g, 0:B * L], weff[:, k, D + g * P:D + (g + 1) * P], ctxT[:, k, :],
                                                   start=(k == 0), stop=(k == KD - 1))
                        ins.then_inc(s_kp, 1)
                    pe.wait_ge(s_w, 3 * KD)
                    for b in range(B):
                        after(pe, s_v, b, 2)
                        for k in range(KD):
                            ins = nc.tensor.matmul(vps[0:L, b % 2, 0:D], ctxT[:, k, b * L:(b + 1) * L], weff[:, k, 2 * D:3 * D],
                                                   start=(k == 0), stop=(k == KD - 1))
                        ins.then_inc(s_vp, 1)

                @block.scalar
                def _(a):
                    for g in range(KD):
                        a.wait_ge(s_kp, g + 1)
                        nc.scalar.activation(kT[:, g], kp[:, g, 0:B * L], ACT.Identity, bias=bfk[:, g:g + 1]).then_inc(s_kT, 1)
                    a.wait_ge(s_w, 4 * KD)
                    nc.scalar.activation(wq[0][:], weff[:, :, 0:D], ACT.Copy).then_inc(s_wh, 1)
                    nc.scalar.activation(wp[:], weff[:, :, 3 * D:], ACT.Copy).then_inc(s_wh, 1)
                    for m in range(2 * B):
                        a.wait_ge(s_kb, m + 1)
                        nc.scalar.activation(kb[0][:, m // 2, m % 2], kblk[:, m % 2], ACT.Copy).then_inc(s_kh, 1)
                    a.wait_ge(s_wh, 2)

                @block.vector
                def _(v):
                    for m in range(4 * KD):
                        part, k = m // KD, m % KD
                        v.wait_ge(s_lp, m + 1)
                        cols = slice(part * D, (part + 1) * D)
                        nc.vector.scalar_tensor_tensor(out=weff[:, k, cols], in0=lp[:, m % 2, 0:D], scalar=1.0 / 16.0,
                                                       in1=raw[:, k, cols], op0=ALU.mult, op1=ALU.add).then_inc(s_w, 1)
                    for m in range(2 * B + 1):
                        if m < 2 * B:
                            b, g = m // 2, m % 2
                            v.wait_ge(s_kT, g + 1)
                            after(v, s_kl, m, 2)
                            nc.vector.tensor_tensor(kblk[:, g].rearrange("p (h l) -> p h l", l=L),
                                                    kT[:, g, b * L:(b + 1) * L].unsqueeze(1).to_broadcast([P, HH, L]),
                                                    core.head_of[:].unsqueeze(2).to_broadcast([P, HH, L]), ALU.mult).then_inc(s_kb, 1)
                        if m:
                            b, g = (m - 1) // 2, (m - 1) % 2
                            v.wait_ge(s_kh, m)
                            nc.vector.tensor_tensor(kb[1][:, b, g], kblk[:, g], kb[0][:, b, g].bitcast(F32),
                                                    ALU.subtract).then_inc(s_kl, 1)
                    v.wait_ge(s_wh, 1)
                    nc.vector.tensor_tensor(wq[1][:], weff[:, :, 0:D], wq[0][:].bitcast(F32), ALU.subtract).then_inc(s_wl, 1)
                    for b in range(B):
                        v.wait_ge(s_vp, b + 1)
                        nc.vector.tensor_tensor(v1[:, b, :, 0:DH], vps[0:L, b % 2, 0:D].rearrange("p (h d) -> p h d", d=DH),
                                                bfv[:].rearrange("p (h d) -> p h d", d=DH), ALU.add).then_inc(s_v, 1)
                    v.wait_ge(s_wl, 1)
                    v.wait_ge(s_kl, 2 * B)
                    v.wait_ge(s_v, B)

                @block.gpsimd
                def _(pool):
                    nc.gpsimd.affine_select(out=causal[:], in_=causal[:], compare_op=ALU.is_ge, fill=-1e30, base=0,
                                            pattern=[[0, HB], [-1, L]], channel_multiplier=1).then_inc(s_causal, 1)
                    pool.wait_ge(s_causal, 1)


        NS = 4
        e = core.sb("lo_e", [P, NS, J * P], ctx=ctx)
        pt = core.sb("lo_pt", [P, 2, J, P], ctx=ctx)
        top = core.sb("lo_top", [P, NS, HH], ctx=ctx)
        inv = core.sb("lo_inv", [P, 2, NH], ctx=ctx)
        qf = core.sb("lo_qf", [P, KD, CH], ctx=ctx)
        q = [core.sb(f"lo_q{n}", [P, 2, KD, CH], F32R, ctx) for n in "hl"]
        yn = core.sb("lo_yn", [P, 2, D], ctx=ctx)
        yT = core.sb("lo_yT", [P, 2, KD, P], ctx=ctx)
        sc = core.ps("lo_sc", [P, 2, 2, 512], ctx)
        pp = core.ps("lo_pp", [P, 2, 512], ctx)
        yp = core.ps("lo_yp", [P, 512], ctx)
        yo = core.ps("lo_yo", [P, 512], ctx)
        norm = Norm(core, "lo", ctx, None)
        s_counted = core.sem("lp_counted")
        (s_pad, s_s, s_top, s_sub, s_exp, s_pt, s_ptc, s_y, s_inv, s_yn, s_yT, s_yTc, s_o, s_x, s_xb, s_q, s_qf, s_qh, s_ql) = (
            core.sem(f"lp_{n}") for n in ("pad", "s", "top", "sub", "exp", "pt", "ptcopy", "y", "inv", "yn", "yT", "yTcopy", "o", "x",
                                          "xbias", "q", "qcopy", "qhigh", "qlow"))
        SLOT = [(0, 1), (0, 1), (1, 0), (0, 1)]
        T_SLOT, Q_SLOT = 0, 1

        def is_last(c):
            return isinstance(c, int) and c == NC - 1

        with nc.Block() as block:
            @block.sync
            def _(sp):
                for h, k0, m, j, r in parts:
                    at = (h - heads_of[j][0]) * VW
                    sp.dma_start(vp[r:r + m, :, j, at:at + VW], v1[k0:k0 + m, :, h, :]).then_inc(s_pack, 16)
                sp.wait_ge(s_pack, 16 * len(parts))

            @block.tensor
            def _(pe):
                def queries(c, s):
                    pe.wait_ge(norm.low, c + 1)
                    for g in range(2):
                        for k in range(KD):
                            ins = mm3(nc, sc[:, Q_SLOT, g, :], [v[:, k, g * P:(g + 1) * P] for v in wq],
                                      [v[:, s, k] for v in (norm.xh, norm.xl)], start=(k == 0), stop=(k == KD - 1))
                    ins.then_inc(s_q, 1)

                def scores(t, u, g, c):
                    j, cs = u % TPC, u // TPC
                    if j == 0 and g == 0:
                        pe.wait_ge(s_ql, c + 1)
                    if (j, g) == (2, 1) and not is_last(c):
                        pe.wait_ge(norm.low, c + 2)
                    elif (j, g) == (3, 1) and not is_last(c):
                        pe.wait_ge(s_qf, c + 2)
                    elif (j, g) in ((2, 1), (3, 1)):
                        pe.wait_ge(s_sub, 2 * t - 1)
                    elif isinstance(t, int) and 2 * t + g < 2:
                        pass
                    elif (j, g) in ((2, 0), (3, 0)):
                        pe.wait_ge(s_sub, 2 * t)
                    else:
                        pe.wait_ge(s_sub, 2 * t + g - 1)
                    for half in range(2):
                        out = sc[:, SLOT[j][g], half, 0:HB * L]
                        rhs = [v[:].rearrange("p b g n -> p (b g n)")[:, bass.ds((t - u) * (2 * HL // 8) + g * HL + half * HB * L, HB * L)]
                               for v in kb]
                        ins = mm3(nc, out, [v[:, cs, g, j * P:(j + 1) * P] for v in q], rhs, start=True, stop=(u != 0))
                        if u == 0:
                            ins = nc.tensor.matmul(out, core.ident[:], causal[:].rearrange("p h l -> p (h l)"), start=False, stop=True)
                    ins.then_inc(s_s, 1)

                def turn(t, u, g):
                    m = 2 * t + g
                    pe.wait_ge(s_exp, m + 1)
                    if not (isinstance(t, int) and m == 0):
                        pe.wait_ge(s_ptc, m)
                    for j in range(J):
                        ins = nc.tensor.transpose(pp[:, j // 4, (j % 4) * P:(j % 4 + 1) * P],
                                                  e[:, (2 * u + g) % NS, j * P:(j + 1) * P], core.ident[:])
                    ins.then_inc(s_pt, 1)

                def values(t, u, g):
                    if isinstance(t, int) and t == 0 and g == 0:
                        pe.wait_ge(s_pack, 16 * len(parts))
                    pe.wait_ge(s_ptc, 2 * t + g + 1)
                    if g == 0:
                        after(pe, s_yn, t, 1)
                    for j in range(J):
                        hs = heads_of[g * J + j]
                        rhs = vp[:].rearrange("p b j n -> p (b j n)")[
                            :, bass.ds((t - u) * (2 * J * VJ // 8) + (g * J + j) * VJ, len(hs) * VW)]
                        ins = nc.tensor.matmul(yp[:, hs[0] * VW:(hs[-1] + 1) * VW], pt[:, g, j, :], rhs,
                                               start=(g == 0 and j == 0), stop=(g == 1 and j == J - 1), skip_group_check=True)
                    ins.then_inc(s_y, 1)

                def step(t, u, lag, c):
                    j, cs = u % TPC, u // TPC
                    if lag[1] == "out_turn":
                        pe.wait_ge(s_yn, t + 1)
                        after(pe, s_x, t, 1)
                        for k in range(KD):
                            ins = nc.tensor.transpose(yo[:, k * P:(k + 1) * P], yn[:, u % 2, k * P:(k + 1) * P], core.ident[:])
                        ins.then_inc(s_yT, 1)
                    elif lag[1] == "s0":
                        scores(t, u, 0, c)
                    elif lag[1] == "t0":
                        turn(t, u, 0)
                    elif lag[1] == "s1":
                        scores(t, u, 1, c)
                    elif lag[1] == "v0t1":
                        values(t, u, 0)
                        turn(t, u, 1)
                    elif lag[1] == "next":
                        if not is_last(c) and j == 1:
                            pe.wait_ge(s_sub, 2 * t + 1)
                            norm.turned = sc[:, T_SLOT]
                            norm.transpose(pe, c + 1, 1 - cs)
                        if not is_last(c) and j == 2:
                            pe.wait_ge(s_sub, 2 * t + 1)
                            queries(c + 1, 1 - cs)
                    elif lag[1] == "v1":
                        values(t, u, 1)
                    else:
                        pe.wait_ge(s_yTc, t + 1)
                        for k in range(KD):
                            ins = nc.tensor.matmul(yo[:, 0:D], yT[:, u % 2, k, :], wp[:, k, :], start=(k == 0), stop=(k == KD - 1))
                        ins.then_inc(s_o, 1)

                norm.turned = sc[:, T_SLOT]
                norm.transpose(pe, 0, 0)
                queries(0, 0)
                pe.wait_ge(s_qf, 1)
                pe.wait_ge(s_pad, 1)
                pipeline(pe, NT, TPS, [(1, "t0"), (0, "s0"), (2, "out_turn"), (1, "v0t1"), (0, "s1"), (0, "next"), (1, "v1"), (2, "out")],
                         step, per=TPC, ahead=True)

            @block.scalar
            def _(a):
                def chunk_queries(c, s):
                    a.wait_ge(s_q, c + 1)
                    after(a, s_ql, c, 1)
                    for g in range(2):
                        ins = nc.scalar.activation(qf[:, g], sc[:, Q_SLOT, g, :], ACT.Identity, bias=bq[:, g:g + 1])
                    ins.then_inc(s_qf, 1)
                    a.wait_ge(s_qf, c + 1)
                    after(a, s_s, c, 2, 2 * TPC)
                    nc.scalar.activation(q[0][:, s], qf[:], ACT.Copy).then_inc(s_qh, 1)

                def step(t, u, lag, c):
                    j, cs = u % TPC, u // TPC
                    if lag[1] in ("e0", "e1"):
                        m = 2 * t + int(lag[1][1])
                        slot = (2 * u + int(lag[1][1])) % NS
                        a.wait_ge(s_sub, m + 1)
                        nc.scalar.activation(e[:, slot, 0:HL], e[:, slot, 0:HL], ACT.Exp, scale=SCALE).then_inc(s_exp, 1)
                    elif lag[1] in ("p0", "p1"):
                        g = int(lag[1][1])
                        a.wait_ge(s_pt, 2 * t + g + 1)
                        after(a, s_y, t, 1, 2)
                        nc.scalar.activation(pt[:, g], pp[:].rearrange("p g n -> p (g n)")[:, 0:J * P], ACT.Copy).then_inc(s_ptc, 1)
                    elif lag[1] == "next":
                        if not is_last(c) and j == 1:
                            norm.turned = sc[:, T_SLOT]
                            after(a, s_q, c + 1, 2)
                            norm.take(a, c + 1, 1 - cs)
                        if not is_last(c) and j == 2:
                            chunk_queries(c + 1, 1 - cs)
                    else:
                        a.wait_ge(s_yT, t + 1)
                        after(a, s_o, t, 2)
                        nc.scalar.activation(yT[:, u % 2].rearrange("p k n -> p (k n)"), yo[:, 0:D], ACT.Copy).then_inc(s_yTc, 1)
                norm.turned = sc[:, T_SLOT]
                norm.take(a, 0, 0)
                chunk_queries(0, 0)
                pipeline(a, NT, TPS, [(1, "p0"), (1, "e1"), (2, "y"), (0, "e0"), (1, "p1"), (0, "next")], step, per=TPC, ahead=True)

            @block.gpsimd
            def _(pool):
                nc.gpsimd.memset(e[:, :, HL:], 0.0).then_inc(s_pad, 1)

                def step(t, u, lag, c):
                    if u % TPC == 0:
                        pool.wait_ge(norm.normed, c + 1)
                    nc.gpsimd.tensor_tensor(x[:, t, :], x[:, t, :], bp[:], ALU.add).then_inc(s_xb, 1)
                pipeline(pool, NT, TPS, [0], step, per=TPC)

            @block.vector
            def _(v):
                def queries_low(c, s):
                    v.wait_ge(s_qh, c + 1)
                    nc.vector.tensor_tensor(q[1][:, s], qf[:], q[0][:, s].bitcast(F32), ALU.subtract).then_inc(s_ql, 1)

                def softmax(t, u, g):
                    m, slot = 2 * t + g, (2 * u + g) % NS
                    view = sc[:, SLOT[u % TPC][g], :, 0:HB * L].rearrange("p b (h l) -> p b h l", l=L)
                    tops = top[:, slot].rearrange("p (b h) -> p b h", h=HB)
                    v.wait_ge(s_s, m + 1)
                    nc.vector.tensor_reduce(tops, view, AX_X, ALU.max).then_inc(s_top, 1)
                    v.wait_ge(s_top, m + 1)
                    after(v, s_pt, t, 2, 2)
                    nc.vector.tensor_tensor(e[:, slot, 0:HL].rearrange("p (b h l) -> p b h l", h=HB, l=L), view,
                                            tops.unsqueeze(3).to_broadcast([P, 2, HB, L]), ALU.subtract).then_inc(s_sub, 1)

                def step(t, u, lag, c):
                    j, cs = u % TPC, u // TPC
                    if lag[1] == "softmax":
                        for g in range(2):
                            softmax(t, u, g)
                        if j == 0 and not is_last(c):
                            norm.normalise(v, c + 1, 1 - cs)
                    elif lag[1] == "next":
                        if not is_last(c) and j == 1:
                            norm.turned = sc[:, T_SLOT]
                            norm.take_low(v, c + 1, 1 - cs)
                        if not is_last(c) and j == 2:
                            queries_low(c + 1, 1 - cs)
                    elif lag[1] == "divide":
                        v.wait_ge(s_y, 2 * t + 2)
                        yv = yp[:, 0:NH * VW].rearrange("p (h d) -> p h d", d=VW)
                        nc.vector.reciprocal(inv[:, u % 2], yv[:, :, DH]).then_inc(s_inv, 1)
                        v.wait_ge(s_inv, t + 1)
                        after(v, s_yT, t, 2)
                        nc.vector.tensor_tensor(yn[:, u % 2].rearrange("p (h d) -> p h d", d=DH), yv[:, :, 0:DH],
                                                inv[:, u % 2].unsqueeze(2).to_broadcast([P, NH, DH]), ALU.mult).then_inc(s_yn, 1)
                    else:
                        v.wait_ge(s_o, t + 1)
                        v.wait_ge(s_xb, t + 1)
                        nc.vector.tensor_tensor(x[:, t, :], yo[:, 0:D], x[:, t, :], ALU.add).then_inc(s_x, 1)
                        v.wait_ge(s_x, t + 1)
                        nc.vector.bn_stats(core.stats[:, t, :], x[:, t, :]).then_inc(s_counted, 1)
                norm.normalise(v, 0, 0)
                norm.turned = sc[:, T_SLOT]
                norm.take_low(v, 0, 0)
                queries_low(0, 0)
                pipeline(v, NT, TPS, [(0, "softmax"), (1, "divide"), (0, "next"), (2, "add")], step, per=TPC, ahead=True)
                v.wait_ge(s_counted, NT)


def decoder(nc, out, w):
    with ExitStack() as ctx:
        core = Core(nc, ctx)
        load_and_constants(core, w["x"])
        gated_chunks(core, w["gated"])
        core.end_branch()
        core.counted = True
        soft_attention(core, w["soft"])
        core.end_branch()
        core.counted = True
        experts(core, w["moe"]["weights"], w["moe"]["gate_w"], w["moe"]["expert_bias"])
        core.end_branch()
        core.counted = False
        linear_attention(core, w["linear"])
        core.end_branch()
        core.counted = True
        lora_attention(core, w["lora"])
        core.end_branch()
        core.counted = True
        picked_adapter(core, w["adapter"], out)



def kernel(**inputs):
    import numpy as np
    import concourse.bacc as _bacc
    from concourse.bass_utils import run_bass_kernel_spmd as _run

    a = {name: np.asarray(v) for name, v in inputs.items()}

    def feature_rows(m):
        return m.reshape(KD, P, -1).transpose(1, 0, 2)

    def column(b):
        return b.reshape(-1, P).T

    head_row = (np.arange(D).reshape(1, KD, P) // 16 == np.arange(16).reshape(16, 1, 1)).astype(np.float32)
    first = np.arange(8, 0, -1).astype(np.float32)

    context = a["ctx_1024"].reshape(-1, D).T.reshape(KD, P, -1).transpose(1, 0, 2)
    W_in = a["L0_attn_W_in"]
    wide, q, k = W_in[:, 0:3 * D], W_in[:, 3 * D:3 * D + 32], W_in[:, 3 * D + 32:]
    Wkv, Wqk = a["L0_xattn_Wkv"], a["L1_attn_Wqk"]

    def with_shared(routed, shared):
        return np.concatenate([routed, shared[None]]).transpose(0, 2, 1)

    expert_weights = np.stack([with_shared(a["L0_ffn_w_gate"], a["L0_ffn_shared_gate_w"]),
                               with_shared(a["L0_ffn_w_up"], a["L0_ffn_shared_up_w"]),
                               with_shared(a["L0_ffn_w_down"], a["L0_ffn_shared_down_w"])], 1)

    def per_head(m):
        return m.reshape(KD, P, 8, P).transpose(1, 0, 2, 3)

    pair_rows = np.zeros((P, 8, D), np.float32)
    for e in range(8):
        pair_rows[64 * (e % 2):64 * (e % 2) + 64, e] = a["L1_ffn_Wd2"][e]

    operands = {
        "gated": dict(
            W_in=feature_rows(np.concatenate([wide] + [q] * 4 + [k] * 4, axis=1)),
            W_out=feature_rows(a["L0_attn_W_out"]), rms_weight=column(a["L0_attn_rms_weight"]),
            gate_bias=column(a["L0_attn_gate_bias"]), head_row=head_row),
        "soft": dict(
            ctxT=context, Wk=per_head(Wkv[:, :, 0:P]), Wv=per_head(Wkv[:, :, P:]),
            WqT=a["L0_xattn_Wq"].transpose(2, 1, 0), Wproj=a["L0_xattn_Wproj"].transpose(1, 0, 2),
            b_proj=a["L0_xattn_b_proj"]),
        "moe": dict(
            weights=expert_weights.reshape(-1, 3, KD, P, D).transpose(0, 3, 1, 2, 4),
            gate_w=a["L0_ffn_gate_w"].T, expert_bias=a["L0_ffn_expert_bias"]),
        "linear": dict(
            Wqk=feature_rows(Wqk), Wkv=feature_rows(np.concatenate([Wqk[:, D:], a["L1_attn_Wv"]], axis=1)),
            Wn=feature_rows(a["L1_attn_Wn"]), Wo=feature_rows(a["L1_attn_Wo"]),
            bq=column(a["L1_attn_bqk"][0:D]), bk=column(a["L1_attn_bqk"][D:]),
            bkv=np.concatenate([a["L1_attn_bqk"][D:], a["L1_attn_bv"]]), bn=a["L1_attn_bn"][:, None], bo=a["L1_attn_bo"],
            ),
        "lora": dict(
            W=feature_rows(np.concatenate([a["L1_xattn_Wq"], a["L1_xattn_Wf"], a["L1_xattn_Wp"]]).T),
            A=np.stack([a["L1_xattn_Aq"], a["L1_xattn_Af"], a["L1_xattn_Ap"]], axis=1),
            B=np.concatenate([a["L1_xattn_Bq"], a["L1_xattn_Bf"], a["L1_xattn_Bp"]]).T,
            bfk=column(a["L1_xattn_bf"][0:D]), bfv=a["L1_xattn_bf"][D:], bq=column(a["L1_xattn_bq"]),
            bp=a["L1_xattn_bp"]),
        "adapter": dict(
            Wd1=feature_rows(a["L1_ffn_Wd1"].transpose(1, 0, 2)), Wd2=pair_rows,
            bd1=column(a["L1_ffn_bd1"]), bd2=feature_rows(a["L1_ffn_bd2"].T), W_base=feature_rows(a["L1_ffn_W_base"]),
            Wa_down=a["L1_ffn_Wa_down"].transpose(1, 0, 2).reshape(KD, P, 8, 64).transpose(1, 0, 2, 3),
            Wa_up=a["L1_ffn_Wa_up"].transpose(1, 0, 2), ba_up=a["L1_ffn_ba_up"][None],
            ba_down=a["L1_ffn_ba_down"].T, first=first, b_base=a["L1_ffn_b_base"]),
    }
    operands["adapter"]["Wd1"] = operands["adapter"]["Wd1"].reshape(P, KD, -1)

    nc = _bacc.Bacc("TRN2", target_bir_lowering=False, num_devices=1)
    arrays, aps = {}, {}

    def operand(name, value):
        arrays[name] = np.ascontiguousarray(value)
        return nc.dram_tensor(name, arrays[name].shape, F32, kind="ExternalInput").ap()

    for tag, group in operands.items():
        aps[tag] = {name: operand(f"{tag}_{name}_dram", value) for name, value in group.items()}
    aps["lora"]["ctxT"] = aps["soft"]["ctxT"]
    aps["x"] = operand("x_dram", a["x"])
    out = nc.dram_tensor("out_dram", a["x"].shape, F32, kind="ExternalOutput").ap()
    decoder(nc, out, aps)
    r = _run(nc, [arrays], core_ids=[0])
    return r.results[0]["out_dram"]
```
